# Optimizing a Trainium2 kernel written in Bass

```python
import numpy as np
import jax
import jax.numpy as jnp

def _softmax(x, axis=-1):
    return jax.nn.softmax(x, axis=axis)

def _gelu(x):
    return jax.nn.gelu(x, approximate=True)

def _silu(x):
    return jax.nn.silu(x)

def _sigmoid(x):
    return jax.nn.sigmoid(x)

def _layernorm(x, axis=-1, eps=1e-05):
    m = jnp.mean(x, axis=axis, keepdims=True)
    v = jnp.var(x, axis=axis, keepdims=True)
    return (x - m) / jnp.sqrt(v + eps)

def _scatter_add(tgt, idx, src, axis=0):
    return tgt.at[idx].add(src)

def _segment_sum(src, seg, n):
    return jax.ops.segment_sum(src, seg, n)
kernel_name = 'mk_gps_d2_gnn_r8_0c73e1'

def setup_inputs(seed: int=0):
    np.random.seed(seed)
    _w = jnp.asarray

    def _rec_inputs():
        import jax
        import jax.numpy as jnp
        _gk = jax.random.key(seed)
        x = -0.0003713 + 1 * jax.random.normal(jax.random.fold_in(_gk, 1), (6250, 256), jnp.float32)
        src = jax.random.randint(jax.random.fold_in(_gk, 2), (200000,), 0, 6250, jnp.int32)
        dst = jnp.minimum((6250 * jax.random.uniform(jax.random.fold_in(_gk, 3), (200000,)) ** 2.0).astype(jnp.int32), 49999)
        _o = jnp.argsort(dst, stable=True)
        src = src[_o]
        dst = dst[_o]
        return (x, src, dst)
    x, src, dst = _rec_inputs()

    def _L0_gnn_setup():
        import jax, jax.numpy as jnp
        import numpy as np
        N = 6250
        E = 200000
        DIN = 256
        DOUT = 64
        HEADS = 4
        SLOPE = 0.2
        key = jax.random.key(seed)
        k = jax.random.split(key, 7)
        h = jax.random.normal(k[0], (N, DIN), dtype=jnp.float32)
        W = jax.random.normal(k[1], (DIN, DOUT), dtype=jnp.float32) * 0.05
        b = jnp.zeros((DOUT,), dtype=jnp.float32)
        a_src = jax.random.normal(k[2], (HEADS, DOUT), dtype=jnp.float32) * 0.05
        a_dst = jax.random.normal(k[3], (HEADS, DOUT), dtype=jnp.float32) * 0.05
        row = jnp.sort(jax.random.randint(k[4], (E,), 0, N, dtype=jnp.int32))
        col = jax.random.randint(k[5], (E,), 0, N, dtype=jnp.int32)
        return {'h': h, 'W': W, 'b': b, 'a_src': a_src, 'a_dst': a_dst, 'row': row, 'col': col}
    _L0_gnn_all = _L0_gnn_setup()
    _L0_gnn_in = {k: v for k, v in _L0_gnn_all.items() if k in ('W', 'b', 'a_src', 'a_dst')}
    del _L0_gnn_all

    def _L0_mix_setup():
        import jax, jax.numpy as jnp
        import numpy as np
        C_CURV = 1.0
        MIN_NORM = 1e-15
        BALL_EPS = 1e-05
        ATT_EPS = 1e-15
        DIM = 32

        def _norm(x):
            return jnp.clip(jnp.linalg.norm(x, axis=-1, keepdims=True), MIN_NORM)

        def proj(x, c):
            maxnorm = (1.0 - BALL_EPS) / jnp.sqrt(c)
            n = _norm(x)
            return jnp.where(n > maxnorm, x / n * maxnorm, x)

        def expmap0(u, c):
            sc = jnp.sqrt(c)
            n = _norm(u)
            return jnp.tanh(sc * n) * u / (sc * n)

        def logmap0(p, c):
            sc = jnp.sqrt(c)
            n = _norm(p)
            return jnp.arctanh(jnp.clip(sc * n, -1.0 + 1e-07, 1.0 - 1e-07)) * p / (sc * n)

        def mobius_add(x, y, c):
            x2 = jnp.sum(x * x, -1, keepdims=True)
            y2 = jnp.sum(y * y, -1, keepdims=True)
            xy = jnp.sum(x * y, -1, keepdims=True)
            num = (1 + 2 * c * xy + c * y2) * x + (1 - c * x2) * y
            den = 1 + 2 * c * xy + c * c * x2 * y2
            return num / jnp.clip(den, MIN_NORM)

        def conv1d(x, w, pad, groups=1):
            return jax.lax.conv_general_dilated(x, w, (1,), [(pad, pad)], dimension_numbers=('NCH', 'OIH', 'NCH'), feature_group_count=groups)

        def batchnorm(x, gamma, beta):
            mean = jnp.mean(x, axis=(0, 2), keepdims=True)
            var = jnp.var(x, axis=(0, 2), keepdims=True)
            xn = (x - mean) * jax.lax.rsqrt(var + 1e-05)
            return gamma[None, :, None] * xn + beta[None, :, None]

        def _reference_tuple_inner(x, w_qkv, bn_gamma, bn_beta, w_dw, w_pw, w_res, b_res):
            c = C_CURV
            h = logmap0(proj(x, c), c)
            h = jnp.transpose(h, (1, 2, 0))
            h = conv1d(h, w_qkv, pad=2)
            h = batchnorm(h, bn_gamma, bn_beta)
            h = jax.nn.relu(jnp.transpose(h, (2, 0, 1)))
            qkv = proj(expmap0(h, c), c)
            t = jnp.transpose(logmap0(proj(qkv, c), c), (1, 2, 0))
            s = conv1d(t, w_dw, pad=2, groups=t.shape[1])
            s = conv1d(s, w_pw, pad=0, groups=t.shape[1] // DIM)
            cat = jnp.concatenate([t, s], axis=1)
            ai = proj(expmap0(jnp.transpose(cat, (2, 0, 1)), c), c)
            t2 = logmap0(proj(ai, c), c)
            L, N, C2 = t2.shape
            g = C2 // (3 * DIM)
            qkv3 = jnp.transpose(t2, (1, 2, 0)).reshape(N, g, 3 * DIM, L)
            q, k, v = jnp.split(qkv3, 3, axis=2)
            q = jax.nn.relu(q)
            k = jax.nn.relu(k)
            vk = jnp.einsum('ngdl,ngel->ngde', v, k)
            out = jnp.einsum('ngde,ngdl->ngdl', vk, q)
            out = out / (jnp.sum(v, -1, keepdims=True) + ATT_EPS)
            out = jnp.transpose(out.reshape(N, g * DIM, L), (2, 0, 1))
            fx_h = proj(expmap0(out, c), c)
            ft = jnp.transpose(logmap0(proj(fx_h, c), c), (1, 2, 0))
            ft = conv1d(ft, w_res, pad=0) + b_res[None, :, None]
            fx = proj(expmap0(jnp.transpose(ft, (2, 0, 1)), c), c)
            residual = mobius_add(fx, x, c)
            return (fx, residual)
        key = jax.random.key(seed)
        ks = jax.random.split(key, 6)
        L, N, C, TD = (256, 16, 256, 256)
        x = jax.random.normal(ks[0], (L, N, C), jnp.float32) * 0.05
        w_qkv = jax.random.normal(ks[1], (3 * TD, C, 5), jnp.float32) / np.sqrt(C * 5)
        bn_gamma = jnp.ones((3 * TD,), jnp.float32)
        bn_beta = jnp.zeros((3 * TD,), jnp.float32)
        w_dw = jax.random.normal(ks[2], (3 * TD, 1, 5), jnp.float32) / np.sqrt(5.0)
        w_pw = jax.random.normal(ks[3], (3 * TD, DIM, 1), jnp.float32) / np.sqrt(DIM)
        w_res = jax.random.normal(ks[4], (C, 2 * TD, 1), jnp.float32) / np.sqrt(2 * TD)
        b_res = jnp.zeros((C,), jnp.float32)
        return {'x': x, 'w_qkv': w_qkv, 'bn_gamma': bn_gamma, 'bn_beta': bn_beta, 'w_dw': w_dw, 'w_pw': w_pw, 'w_res': w_res, 'b_res': b_res}
    _L0_mix_all = _L0_mix_setup()
    _L0_mix_in = {k: v for k, v in _L0_mix_all.items() if k in ('w_qkv', 'bn_gamma', 'bn_beta', 'w_dw', 'w_pw', 'w_res', 'b_res')}
    del _L0_mix_all

    def _L0_ffn_setup():
        import jax, jax.numpy as jnp
        import numpy as np
        D_MODEL = 256
        EXPERT_DIM = 512
        NUM_EXPERTS = 8
        TOP_K = 2
        SEQ_LEN = 256
        BATCH = 2
        key = jax.random.key(seed)
        ks = jax.random.split(key, 8)
        s = 0.02
        x = jax.random.normal(ks[0], (SEQ_LEN, BATCH, D_MODEL), dtype=jnp.float32)
        Wg = jax.random.normal(ks[1], (D_MODEL, NUM_EXPERTS), dtype=jnp.float32) * s
        bg = jax.random.normal(ks[2], (NUM_EXPERTS,), dtype=jnp.float32) * s
        bias = jnp.zeros((NUM_EXPERTS,), dtype=jnp.float32)
        W1 = jax.random.normal(ks[3], (NUM_EXPERTS, D_MODEL, EXPERT_DIM), dtype=jnp.float32) * s
        b1 = jax.random.normal(ks[4], (NUM_EXPERTS, EXPERT_DIM), dtype=jnp.float32) * s
        W2 = jax.random.normal(ks[5], (NUM_EXPERTS, EXPERT_DIM, D_MODEL), dtype=jnp.float32) * s
        b2 = jax.random.normal(ks[6], (NUM_EXPERTS, D_MODEL), dtype=jnp.float32) * s
        return {'x': x, 'Wg': Wg, 'bg': bg, 'bias': bias, 'W1': W1, 'b1': b1, 'W2': W2, 'b2': b2}
    _L0_ffn_all = _L0_ffn_setup()
    _L0_ffn_in = {k: v for k, v in _L0_ffn_all.items() if k in ('Wg', 'bg', 'bias', 'W1', 'b1', 'W2', 'b2')}
    del _L0_ffn_all

    def _L1_gnn_setup():
        import jax, jax.numpy as jnp
        import numpy as np
        N = 6250
        E = 50000
        IN_CH = 256
        HEADS = 4
        OUT_CH = 64
        HID = HEADS * OUT_CH
        ALPHA = 0.2
        LN_EPS = 1e-05
        key = jax.random.key(seed)
        ks = jax.random.split(key, 8)
        h = jax.random.normal(ks[0], (N, IN_CH), dtype=jnp.float32)
        edge_row = jax.random.randint(ks[1], (E,), 0, N, dtype=jnp.int32)
        edge_col = jax.random.randint(ks[2], (E,), 0, N, dtype=jnp.int32)

        def xavier(k, shape, fan_in, fan_out):
            lim = np.sqrt(6.0 / (fan_in + fan_out)).astype(np.float32)
            return jax.random.uniform(k, shape, jnp.float32, -lim, lim)
        W = xavier(ks[3], (IN_CH, HID), IN_CH, HID)
        attn_fc = xavier(ks[4], (HEADS, 2 * OUT_CH), 2 * OUT_CH, 1)
        ln_gamma = jnp.ones((HID,), jnp.float32)
        ln_beta = jnp.zeros((HID,), jnp.float32)
        ffn_w = xavier(ks[5], (HID, HID), HID, HID)
        ffn_b = jnp.zeros((HID,), jnp.float32)
        return {'h': h, 'edge_row': edge_row, 'edge_col': edge_col, 'W': W, 'attn_fc': attn_fc, 'ln_gamma': ln_gamma, 'ln_beta': ln_beta, 'ffn_w': ffn_w, 'ffn_b': ffn_b}
    _L1_gnn_all = _L1_gnn_setup()
    _L1_gnn_in = {k: v for k, v in _L1_gnn_all.items() if k in ('W', 'attn_fc', 'ln_gamma', 'ln_beta', 'ffn_w', 'ffn_b')}
    del _L1_gnn_all

    def _L1_mix_setup():
        import jax, jax.numpy as jnp
        import numpy as np
        B, N, C, H = (8, 2048, 256, 8)
        D = C // H
        GH = C // 4
        key = jax.random.key(seed)
        ks = jax.random.split(key, 6)
        s = 0.02
        return {'x': jax.random.normal(ks[0], (B, N, C), dtype=jnp.float32), 'Wqkv': jax.random.normal(ks[1], (C, 3 * C), dtype=jnp.float32) * s, 'Wproj': jax.random.normal(ks[2], (C, C), dtype=jnp.float32) * s, 'bproj': jnp.zeros((C,), dtype=jnp.float32), 'ln_g': jnp.ones((C,), dtype=jnp.float32), 'ln_b': jnp.zeros((C,), dtype=jnp.float32), 'Wg1': jax.random.normal(ks[3], (C, GH), dtype=jnp.float32) * s, 'bg1': jnp.zeros((GH,), dtype=jnp.float32), 'Wg2': jax.random.normal(ks[4], (GH, C), dtype=jnp.float32) * s, 'bg2': jnp.zeros((C,), dtype=jnp.float32)}
    _L1_mix_all = _L1_mix_setup()
    _L1_mix_in = {k: v for k, v in _L1_mix_all.items() if k in ('Wqkv', 'Wproj', 'bproj', 'ln_g', 'ln_b', 'Wg1', 'bg1', 'Wg2', 'bg2')}
    del _L1_mix_all

    def _L1_ffn_setup():
        import jax, jax.numpy as jnp
        import numpy as np
        BN_EPS = 0.001

        def _bn(h, g, b, m, v):
            return g * (h - m) * jax.lax.rsqrt(v + BN_EPS) + b
        key = jax.random.key(seed)
        ks = jax.random.split(key, 8)
        B, F, Df = (256, 64, 256)
        E, H, D = (8, 256, 256)
        s1 = 1.0 / np.sqrt(Df)
        s2 = 1.0 / np.sqrt(H)
        return {'x': jax.random.normal(ks[0], (B, F, Df), jnp.float32), 'Wr': jax.random.normal(ks[1], (Df, E), jnp.float32) * s1, 'br': jnp.zeros((E,), jnp.float32), 'W1': jax.random.normal(ks[2], (E, Df, H), jnp.float32) * s1, 'b1': jnp.zeros((E, H), jnp.float32), 'g1': jnp.ones((E, H), jnp.float32), 'be1': jnp.zeros((E, H), jnp.float32), 'm1': jnp.zeros((E, H), jnp.float32), 'v1': jnp.ones((E, H), jnp.float32), 'W2': jax.random.normal(ks[3], (E, H, H), jnp.float32) * s2, 'b2': jnp.zeros((E, H), jnp.float32), 'g2': jnp.ones((E, H), jnp.float32), 'be2': jnp.zeros((E, H), jnp.float32), 'm2': jnp.zeros((E, H), jnp.float32), 'v2': jnp.ones((E, H), jnp.float32), 'Wo': jax.random.normal(ks[4], (E, H, D), jnp.float32) * s2, 'bo': jnp.zeros((E, D), jnp.float32)}
    _L1_ffn_all = _L1_ffn_setup()
    _L1_ffn_in = {k: v for k, v in _L1_ffn_all.items() if k in ('Wr', 'br', 'W1', 'b1', 'g1', 'be1', 'm1', 'v1', 'W2', 'b2', 'g2', 'be2', 'm2', 'v2', 'Wo', 'bo')}
    del _L1_ffn_all
    return {'x': x, 'src': src, 'dst': dst, 'L0_gnn_W': _L0_gnn_in['W'], 'L0_gnn_b': _L0_gnn_in['b'], 'L0_gnn_a_src': _L0_gnn_in['a_src'], 'L0_gnn_a_dst': _L0_gnn_in['a_dst'], 'L0_mix_w_qkv': _L0_mix_in['w_qkv'], 'L0_mix_bn_gamma': _L0_mix_in['bn_gamma'], 'L0_mix_bn_beta': _L0_mix_in['bn_beta'], 'L0_mix_w_dw': _L0_mix_in['w_dw'], 'L0_mix_w_pw': _L0_mix_in['w_pw'], 'L0_mix_w_res': _L0_mix_in['w_res'], 'L0_mix_b_res': _L0_mix_in['b_res'], 'L0_ffn_Wg': _L0_ffn_in['Wg'], 'L0_ffn_bg': _L0_ffn_in['bg'], 'L0_ffn_bias': _L0_ffn_in['bias'], 'L0_ffn_W1': _L0_ffn_in['W1'], 'L0_ffn_b1': _L0_ffn_in['b1'], 'L0_ffn_W2': _L0_ffn_in['W2'], 'L0_ffn_b2': _L0_ffn_in['b2'], 'L1_gnn_W': _L1_gnn_in['W'], 'L1_gnn_attn_fc': _L1_gnn_in['attn_fc'], 'L1_gnn_ln_gamma': _L1_gnn_in['ln_gamma'], 'L1_gnn_ln_beta': _L1_gnn_in['ln_beta'], 'L1_gnn_ffn_w': _L1_gnn_in['ffn_w'], 'L1_gnn_ffn_b': _L1_gnn_in['ffn_b'], 'L1_mix_Wqkv': _L1_mix_in['Wqkv'], 'L1_mix_Wproj': _L1_mix_in['Wproj'], 'L1_mix_bproj': _L1_mix_in['bproj'], 'L1_mix_ln_g': _L1_mix_in['ln_g'], 'L1_mix_ln_b': _L1_mix_in['ln_b'], 'L1_mix_Wg1': _L1_mix_in['Wg1'], 'L1_mix_bg1': _L1_mix_in['bg1'], 'L1_mix_Wg2': _L1_mix_in['Wg2'], 'L1_mix_bg2': _L1_mix_in['bg2'], 'L1_ffn_Wr': _L1_ffn_in['Wr'], 'L1_ffn_br': _L1_ffn_in['br'], 'L1_ffn_W1': _L1_ffn_in['W1'], 'L1_ffn_b1': _L1_ffn_in['b1'], 'L1_ffn_g1': _L1_ffn_in['g1'], 'L1_ffn_be1': _L1_ffn_in['be1'], 'L1_ffn_m1': _L1_ffn_in['m1'], 'L1_ffn_v1': _L1_ffn_in['v1'], 'L1_ffn_W2': _L1_ffn_in['W2'], 'L1_ffn_b2': _L1_ffn_in['b2'], 'L1_ffn_g2': _L1_ffn_in['g2'], 'L1_ffn_be2': _L1_ffn_in['be2'], 'L1_ffn_m2': _L1_ffn_in['m2'], 'L1_ffn_v2': _L1_ffn_in['v2'], 'L1_ffn_Wo': _L1_ffn_in['Wo'], 'L1_ffn_bo': _L1_ffn_in['bo']}

def reference(x, src, dst, L0_gnn_W, L0_gnn_b, L0_gnn_a_src, L0_gnn_a_dst, L0_mix_w_qkv, L0_mix_bn_gamma, L0_mix_bn_beta, L0_mix_w_dw, L0_mix_w_pw, L0_mix_w_res, L0_mix_b_res, L0_ffn_Wg, L0_ffn_bg, L0_ffn_bias, L0_ffn_W1, L0_ffn_b1, L0_ffn_W2, L0_ffn_b2, L1_gnn_W, L1_gnn_attn_fc, L1_gnn_ln_gamma, L1_gnn_ln_beta, L1_gnn_ffn_w, L1_gnn_ffn_b, L1_mix_Wqkv, L1_mix_Wproj, L1_mix_bproj, L1_mix_ln_g, L1_mix_ln_b, L1_mix_Wg1, L1_mix_bg1, L1_mix_Wg2, L1_mix_bg2, L1_ffn_Wr, L1_ffn_br, L1_ffn_W1, L1_ffn_b1, L1_ffn_g1, L1_ffn_be1, L1_ffn_m1, L1_ffn_v1, L1_ffn_W2, L1_ffn_b2, L1_ffn_g2, L1_ffn_be2, L1_ffn_m2, L1_ffn_v2, L1_ffn_Wo, L1_ffn_bo):
    import jax
    import jax.numpy as jnp

    def _L0_gnn_ref(h, W, b, a_src, a_dst, row, col):
        import jax, jax.numpy as jnp
        import numpy as np
        N = 6250
        E = 200000
        DIN = 256
        DOUT = 64
        HEADS = 4
        SLOPE = 0.2
        hW = h @ W + b
        s = hW @ a_src.T
        d = hW @ a_dst.T
        outs = []
        for head in range(HEADS):
            e = jax.nn.leaky_relu(s[row, head] + d[col, head], negative_slope=SLOPE)
            m = jax.lax.stop_gradient(jax.ops.segment_max(e, row, num_segments=N))
            ex = jnp.exp(e - m[row])
            den = jax.ops.segment_sum(ex, row, num_segments=N)
            alpha = ex / den[row]
            outs.append(jax.ops.segment_sum(alpha[:, None] * hW[col], row, num_segments=N))
        return jnp.concatenate(outs, axis=1)

    def _L0_mix_ref(x, w_qkv, bn_gamma, bn_beta, w_dw, w_pw, w_res, b_res):
        import jax, jax.numpy as jnp
        import numpy as np
        C_CURV = 1.0
        MIN_NORM = 1e-15
        BALL_EPS = 1e-05
        ATT_EPS = 1e-15
        DIM = 32

        def _norm(x):
            return jnp.clip(jnp.linalg.norm(x, axis=-1, keepdims=True), MIN_NORM)

        def proj(x, c):
            maxnorm = (1.0 - BALL_EPS) / jnp.sqrt(c)
            n = _norm(x)
            return jnp.where(n > maxnorm, x / n * maxnorm, x)

        def expmap0(u, c):
            sc = jnp.sqrt(c)
            n = _norm(u)
            return jnp.tanh(sc * n) * u / (sc * n)

        def logmap0(p, c):
            sc = jnp.sqrt(c)
            n = _norm(p)
            return jnp.arctanh(jnp.clip(sc * n, -1.0 + 1e-07, 1.0 - 1e-07)) * p / (sc * n)

        def mobius_add(x, y, c):
            x2 = jnp.sum(x * x, -1, keepdims=True)
            y2 = jnp.sum(y * y, -1, keepdims=True)
            xy = jnp.sum(x * y, -1, keepdims=True)
            num = (1 + 2 * c * xy + c * y2) * x + (1 - c * x2) * y
            den = 1 + 2 * c * xy + c * c * x2 * y2
            return num / jnp.clip(den, MIN_NORM)

        def conv1d(x, w, pad, groups=1):
            return jax.lax.conv_general_dilated(x, w, (1,), [(pad, pad)], dimension_numbers=('NCH', 'OIH', 'NCH'), feature_group_count=groups)

        def batchnorm(x, gamma, beta):
            mean = jnp.mean(x, axis=(0, 2), keepdims=True)
            var = jnp.var(x, axis=(0, 2), keepdims=True)
            xn = (x - mean) * jax.lax.rsqrt(var + 1e-05)
            return gamma[None, :, None] * xn + beta[None, :, None]

        def _reference_tuple_inner(x, w_qkv, bn_gamma, bn_beta, w_dw, w_pw, w_res, b_res):
            c = C_CURV
            h = logmap0(proj(x, c), c)
            h = jnp.transpose(h, (1, 2, 0))
            h = conv1d(h, w_qkv, pad=2)
            h = batchnorm(h, bn_gamma, bn_beta)
            h = jax.nn.relu(jnp.transpose(h, (2, 0, 1)))
            qkv = proj(expmap0(h, c), c)
            t = jnp.transpose(logmap0(proj(qkv, c), c), (1, 2, 0))
            s = conv1d(t, w_dw, pad=2, groups=t.shape[1])
            s = conv1d(s, w_pw, pad=0, groups=t.shape[1] // DIM)
            cat = jnp.concatenate([t, s], axis=1)
            ai = proj(expmap0(jnp.transpose(cat, (2, 0, 1)), c), c)
            t2 = logmap0(proj(ai, c), c)
            L, N, C2 = t2.shape
            g = C2 // (3 * DIM)
            qkv3 = jnp.transpose(t2, (1, 2, 0)).reshape(N, g, 3 * DIM, L)
            q, k, v = jnp.split(qkv3, 3, axis=2)
            q = jax.nn.relu(q)
            k = jax.nn.relu(k)
            vk = jnp.einsum('ngdl,ngel->ngde', v, k)
            out = jnp.einsum('ngde,ngdl->ngdl', vk, q)
            out = out / (jnp.sum(v, -1, keepdims=True) + ATT_EPS)
            out = jnp.transpose(out.reshape(N, g * DIM, L), (2, 0, 1))
            fx_h = proj(expmap0(out, c), c)
            ft = jnp.transpose(logmap0(proj(fx_h, c), c), (1, 2, 0))
            ft = conv1d(ft, w_res, pad=0) + b_res[None, :, None]
            fx = proj(expmap0(jnp.transpose(ft, (2, 0, 1)), c), c)
            residual = mobius_add(fx, x, c)
            return (fx, residual)
        return _reference_tuple_inner(x, w_qkv, bn_gamma, bn_beta, w_dw, w_pw, w_res, b_res)[0]

    def _L0_ffn_ref(x, Wg, bg, bias, W1, b1, W2, b2):
        import jax, jax.numpy as jnp
        import numpy as np
        D_MODEL = 256
        EXPERT_DIM = 512
        NUM_EXPERTS = 8
        TOP_K = 2
        SEQ_LEN = 256
        BATCH = 2
        x_flat = x.reshape(-1, D_MODEL)
        gate_logits = x_flat @ Wg + bg + bias
        topk_vals, topk_idx = jax.lax.top_k(gate_logits, TOP_K)
        topk_w = jax.nn.softmax(topk_vals, axis=-1)
        combine = (jax.nn.one_hot(topk_idx, NUM_EXPERTS, dtype=x.dtype) * topk_w[..., None]).sum(axis=1)
        h = jax.nn.relu(jnp.einsum('td,edh->teh', x_flat, W1) + b1)
        y = jnp.einsum('teh,ehd->ted', h, W2) + b2
        out = jnp.einsum('ted,te->td', y, combine)
        return out.reshape(x.shape)

    def _L1_gnn_ref(h, edge_row, edge_col, W, attn_fc, ln_gamma, ln_beta, ffn_w, ffn_b):
        import jax, jax.numpy as jnp
        import numpy as np
        N = 6250
        E = 50000
        IN_CH = 256
        HEADS = 4
        OUT_CH = 64
        HID = HEADS * OUT_CH
        ALPHA = 0.2
        LN_EPS = 1e-05
        Wh = (h @ W).reshape(N, HEADS, OUT_CH)
        Wh_i = Wh[edge_row]
        Wh_j = Wh[edge_col]
        a_src = attn_fc[:, :OUT_CH]
        a_dst = attn_fc[:, OUT_CH:]
        e = jnp.einsum('ehd,hd->eh', Wh_i, a_src) + jnp.einsum('ehd,hd->eh', Wh_j, a_dst)
        e = jax.nn.leaky_relu(e, negative_slope=ALPHA)
        e = jnp.exp(e - jnp.max(e, axis=0, keepdims=True))
        e_sum = jax.ops.segment_sum(e, edge_row, num_segments=N)
        alpha = e / (e_sum[edge_row] + 1e-15)
        h_new = jax.ops.segment_sum(Wh_j * alpha[..., None], edge_row, num_segments=N)
        h_new = h_new.reshape(N, HID) + Wh.reshape(N, HID)
        mu = jnp.mean(h_new, axis=-1, keepdims=True)
        var = jnp.var(h_new, axis=-1, keepdims=True)
        h_new = (h_new - mu) * jax.lax.rsqrt(var + LN_EPS) * ln_gamma + ln_beta
        return jax.nn.relu(h_new @ ffn_w + ffn_b)

    def _L1_mix_ref(x, Wqkv, Wproj, bproj, ln_g, ln_b, Wg1, bg1, Wg2, bg2):
        import jax, jax.numpy as jnp
        import numpy as np
        B, N, C, H = (8, 2048, 256, 8)
        D = C // H
        GH = C // 4
        b, n, c = x.shape
        h, d = (H, D)
        qkv = (x @ Wqkv).reshape(b, n, 3, h, d)
        q, k, v = (qkv[:, :, 0], qkv[:, :, 1], qkv[:, :, 2])
        k = jax.nn.softmax(k, axis=1)
        context = jnp.einsum('bnhd,bnhv->bhdv', k, v)
        out = jnp.einsum('bnhd,bhdv->bnhv', q, context).reshape(b, n, c)
        mu = jnp.mean(x, axis=-1, keepdims=True)
        var = jnp.var(x, axis=-1, keepdims=True)
        xn = (x - mu) * jax.lax.rsqrt(var + 1e-05) * ln_g + ln_b
        hgate = jax.nn.gelu(xn @ Wg1 + bg1, approximate=False)
        gate = jax.nn.sigmoid(hgate @ Wg2 + bg2)
        return out * gate @ Wproj + bproj

    def _L1_ffn_ref(x, Wr, br, W1, b1, g1, be1, m1, v1, W2, b2, g2, be2, m2, v2, Wo, bo):
        import jax, jax.numpy as jnp
        import numpy as np
        BN_EPS = 0.001

        def _bn(h, g, b, m, v):
            return g * (h - m) * jax.lax.rsqrt(v + BN_EPS) + b
        feat = jnp.mean(x, axis=0)
        w = jax.nn.softmax(feat @ Wr + br, axis=-1)
        h = jnp.einsum('bfd,edh->bfeh', x, W1) + b1
        h = jax.nn.relu(_bn(h, g1, be1, m1, v1))
        h = jnp.einsum('bfeh,ehk->bfek', h, W2) + b2
        h = jax.nn.relu(_bn(h, g2, be2, m2, v2))
        y = jnp.einsum('bfeh,ehd->bfed', h, Wo) + bo
        return jnp.einsum('bfed,fe->bfd', y, w)
    xn = _layernorm(x, axis=-1)
    x = x + _L0_gnn_ref(xn, L0_gnn_W, L0_gnn_b, L0_gnn_a_src, L0_gnn_a_dst, src, dst) + _L0_mix_ref(xn[None], L0_mix_w_qkv, L0_mix_bn_gamma, L0_mix_bn_beta, L0_mix_w_dw, L0_mix_w_pw, L0_mix_w_res, L0_mix_b_res)[0]
    x = x + _L0_ffn_ref(_layernorm(x, axis=-1)[None], L0_ffn_Wg, L0_ffn_bg, L0_ffn_bias, L0_ffn_W1, L0_ffn_b1, L0_ffn_W2, L0_ffn_b2)[0]
    xn = _layernorm(x, axis=-1)
    x = x + _L1_gnn_ref(xn, src, dst, L1_gnn_W, L1_gnn_attn_fc, L1_gnn_ln_gamma, L1_gnn_ln_beta, L1_gnn_ffn_w, L1_gnn_ffn_b) + _L1_mix_ref(xn[None], L1_mix_Wqkv, L1_mix_Wproj, L1_mix_bproj, L1_mix_ln_g, L1_mix_ln_b, L1_mix_Wg1, L1_mix_bg1, L1_mix_Wg2, L1_mix_bg2)[0]
    x = x + _L1_ffn_ref(_layernorm(x, axis=-1)[None], L1_ffn_Wr, L1_ffn_br, L1_ffn_W1, L1_ffn_b1, L1_ffn_g1, L1_ffn_be1, L1_ffn_m1, L1_ffn_v1, L1_ffn_W2, L1_ffn_b2, L1_ffn_g2, L1_ffn_be2, L1_ffn_m2, L1_ffn_v2, L1_ffn_Wo, L1_ffn_bo)[0]
    return x

_drawn_inputs = setup_inputs


def setup_inputs(seed=0):
    import zlib

    import numpy as np

    out = dict(_drawn_inputs(seed))
    spreads = {'L0_gnn_b': (0.0, 0.1),
     'L0_mix_bn_gamma': (1.0, 0.6),
     'L0_mix_bn_beta': (0.0, 0.425),
     'L0_mix_b_res': (0.0, 0.1),
     'L0_ffn_bias': (0.0, 0.1),
     'L1_gnn_ln_gamma': (1.0, 0.6),
     'L1_gnn_ln_beta': (0.0, 0.728),
     'L1_gnn_ffn_b': (0.0, 0.76),
     'L1_mix_bproj': (0.0, 0.508),
     'L1_mix_ln_g': (1.0, 0.6),
     'L1_mix_ln_b': (0.0, 0.8),
     'L1_mix_bg1': (0.0, 0.8),
     'L1_mix_bg2': (0.0, 0.8),
     'L1_ffn_br': (0.0, 2.0),
     'L1_ffn_b1': (0.0, 1.583),
     'L1_ffn_g1': (1.0, 0.6),
     'L1_ffn_be1': (0.0, 1.869),
     'L1_ffn_m1': (0.0, 1.661),
     'L1_ffn_v1': (1.0, 0.6),
     'L1_ffn_b2': (0.0, 1.214),
     'L1_ffn_g2': (1.0, 0.6),
     'L1_ffn_be2': (0.0, 1.471),
     'L1_ffn_m2': (0.0, 1.22),
     'L1_ffn_v2': (1.0, 0.6),
     'L1_ffn_bo': (0.0, 0.8)}
    factors = {'L0_gnn_a_src': 3.648,
     'L0_mix_w_dw': 5.55,
     'L0_mix_w_pw': 5.5,
     'L0_ffn_bg': 4.339,
     'L0_ffn_b1': 8.0,
     'L0_ffn_b2': 3.387,
     'L1_mix_Wqkv': 6.446,
     'L1_mix_Wproj': 6.101,
     'L1_mix_Wg1': 8.0,
     'L1_mix_Wg2': 8.0,
     'L1_gnn_attn_fc': 2.708}
    for name, (base, spread) in spreads.items():
        noise = np.random.default_rng([zlib.crc32(name.encode()), seed]).standard_normal(out[name].shape)
        drawn = base * np.exp(spread * noise) if base else spread * noise
        out[name] = jnp.asarray(drawn.astype(out[name].dtype))
    for name, factor in factors.items():
        out[name] = (out[name] * factor).astype(out[name].dtype)
    return out
```

```python
import math

import numpy as np
import concourse.bass as bass
from concourse import mybir
from contextlib import ExitStack, contextmanager

F32 = mybir.dt.float32
BF16 = mybir.dt.bfloat16
I32 = mybir.dt.int32
U32 = mybir.dt.uint32
ALU = mybir.AluOpType
ACT = mybir.ActivationFunctionType
AX = mybir.AxisListType
ds = bass.ds

P = 128
N = 6250
NT = -(-N // P)
LAST = N - (NT - 1) * P
E = 200000
EC = E // P
ER = E - EC * P
EJ = EC + 1
KT = 8
STEP_RING = 4
UNIT = 2 * P
TILES = -(-((E + NT * (UNIT - 1)) // UNIT) * 2 // (STEP_RING * KT)) * STEP_RING * KT
PAIRS = TILES // 2
D = 256
AW = 260
BIG = 1.0e30
HEADROOM = 60.0


class Space:
    pass


class Chain:

    def __init__(self, eng, sem, per=0, turn=None):
        self.eng, self.sem, self.n, self.per, self.turn = eng, sem, 0, per, turn

    def __call__(self, ins):
        self.n += 1
        ins.then_inc(self.sem, 1)
        self.wait()

    def wait(self):
        if self.turn is None:
            self.eng.wait_ge(self.sem, self.n)
        else:
            self.eng.wait_ge(self.sem, self.turn * self.per + self.n)

    def end(self):
        assert self.turn is None or self.n == self.per, (self.n, self.per)

@contextmanager
def semaphore(nc, name):
    handle = nc.alloc_semaphore(name)
    yield handle
    nc.clear_and_free_semaphores([handle])

@contextmanager
def stage(nc):
    with ExitStack() as own:
        own.callback(nc.all_engine_barrier)
        yield own


def stage_constants(nc, g, ctx):
    def sb(name, shape, dt=F32):
        return ctx.enter_context(nc.sbuf_tensor(name, shape, dt))
    g.iota_row = sb("iota_row", [P, P])
    g.lane = sb("lane", [P, 1])
    g.ident = sb("ident", [P, P])
    g.before = sb("before", [P, P])
    g.ones = sb("ones", [P, P])
    with stage(nc) as own:
        made = own.enter_context(semaphore(nc, "iotas_made"))
        chain = own.enter_context(semaphore(nc, "const_chain"))
        with nc.Block() as block:
            @block.gpsimd
            def _(pool):
                nc.gpsimd.iota(g.iota_row[:, :], pattern=[[1, P]], base=0, channel_multiplier=0,
                               allow_small_or_imprecise_dtypes=True).then_inc(made, 1)
                nc.gpsimd.iota(g.lane[:, :], pattern=[[0, 1]], base=0, channel_multiplier=1,
                               allow_small_or_imprecise_dtypes=True).then_inc(made, 1)
                nc.gpsimd.memset(g.ones[:, :], 1.0).then_inc(made, 1)

            @block.vector
            def _(dve):
                dve.wait_ge(made, 3)
                nc.vector.tensor_scalar(g.ident[:, :], g.iota_row[:, :], g.lane[:, :], None, ALU.is_equal)
                nc.vector.tensor_scalar(g.before[:, :], g.iota_row[:, :], g.lane[:, :], None, ALU.is_gt)

HALF = 11
SCATTER_TURNS = EC // (2 * HALF)
assert SCATTER_TURNS * 2 * HALF == EC


def scatter_edges(nc, g, pool, lo, hi):
    def one_turn(turn, first):
        for half in range(2):
            if not first:
                pool.wait_ge(g.scattered[half], turn * (16 * HALF))
            k = half * HALF
            nc.gpsimd.tensor_copy(g.st_addr[:, k:k + HALF], g.addr[:, ds(turn * (2 * HALF) + k, HALF)]).then_inc(g.pairs_staged, 1)
            nc.gpsimd.tensor_copy(g.st_pair[:, k:k + HALF, :].rearrange("p k w -> p (k w)"),
                                  g.pair[:, :, :].rearrange("p k w -> p (k w)")[:, ds(turn * (4 * HALF) + 2 * k, 2 * HALF)])\
                .then_inc(g.pairs_staged, 1)
            pool.wait_ge(g.pairs_staged, turn * 4 + 2 * half + 2)
            pool.nop(nofuse=True)
            for k in range(half * HALF, half * HALF + HALF):
                pool.indirect_dma_start(g.edge_list, bass.IndirectOffsetOnAxis(ap=g.st_addr[:, k:k + 1], axis=0),
                                        g.st_pair[:, k, :], None).then_inc(g.scattered[half], 16)
    if lo == 0:
        one_turn(0, True)
        lo = 1
    with pool.Fori(lo, hi) as turn:
        one_turn(turn, False)


def stage_places(nc, g, src, dst, ctx, lists, edge_list):
    def sbp(name, shape, dt=F32):
        return ctx.enter_context(nc.sbuf_tensor(name, shape, dt))
    g.col_idx = sbp("col_idx", [P, TILES], I32)
    g.row_loc = sbp("row_loc", [P, TILES])
    g.empty_bias = sbp("empty_bias", [P, TILES])
    g.pair_block = sbp("pair_block", [1, PAIRS], I32)
    g.edge_list = edge_list
    g.addr = lists.enter_context(nc.sbuf_tensor("addr", [P, EJ], I32))
    g.pair = lists.enter_context(nc.sbuf_tensor("pair", [P, EJ, 2], I32))
    g.st_addr = lists.enter_context(nc.sbuf_tensor("st_addr", [P, 2 * HALF], U32))
    g.st_pair = lists.enter_context(nc.sbuf_tensor("st_pair", [P, 2 * HALF, 2], I32))
    g.pairs_staged = lists.enter_context(semaphore(nc, "pairs_staged"))
    g.scattered = [lists.enter_context(semaphore(nc, "scattered_even")), lists.enter_context(semaphore(nc, "scattered_odd"))]
    addr, pair = g.addr, g.pair
    with stage(nc) as own:
        def sb(name, shape, dt=F32):
            return own.enter_context(nc.sbuf_tensor(name, shape, dt))

        def sem(name):
            return own.enter_context(semaphore(nc, name))
        srcs = sb("srcs", [P, EJ], I32)
        dsts = sb("dsts", [P, EJ], I32)
        blk_i = sb("blk_i", [P, EJ], I32)
        blk = sb("blk", [P, EJ])
        blk_h = sb("blk_h", [P, EJ + 1], BF16)
        hit_h = sb("hit_h", [P, EJ + 1], BF16)
        hit = sb("hit", [P, EJ])
        cum = sb("cum", [P, EJ])
        own_cum = sb("own_cum", [P, 2, EJ])
        pos = sb("pos", [P, EJ])
        zero = sb("zero", [P, EJ])
        blocks = sb("blocks", [P, NT])
        cnt = sb("cnt", [P, NT])
        tot_i = sb("tot_i", [P, NT], I32)
        npair = sb("npair", [P, NT])
        pair_end = sb("pair_end", [P, NT])
        base = sb("base", [P, NT])
        end_col = sb("end_col", [NT, P])
        pair_no = sb("pair_no", [NT, PAIRS])
        past = sb("past", [NT, PAIRS])
        empty = sb("empty", [P, TILES, 2], I32)
        ps_a = own.enter_context(nc.psum_tensor("ps_sort_a", [P, 512], F32))
        ps_t = own.enter_context(nc.psum_tensor("ps_sort_t", [P, 512], F32))
        ps_b = own.enter_context(nc.psum_tensor("ps_sort_b", [P, 4, 512], F32))
        cleared, loaded, iotas, counted, chain = sem("last_cleared"), sem("edges_loaded"), sem("sort_iotas"), sem("blocks_counted"), sem("sort_chain")
        sums, ends, ends_t, past_ready, blocks_of = sem("count_sums"), sem("ends_made"), sem("ends_turned"), sem("past_ready"), sem("pair_blocks")
        blank, blanked, chain_v = sem("blank_made"), sem("list_blanked"), sem("place_chain")
        ranked, placed, pos_zero = sem("block_ranked"), sem("block_placed"), sem("pos_zero")
        order = own.enter_context(nc.Block())

        @order.sync
        def _(sp):
            sp.wait_ge(cleared, 2)
            sp.dma_start(srcs[:, 0:EC], src[0:EC * P].rearrange("(p j) -> p j", p=P)).then_inc(loaded, 16)
            sp.dma_start(dsts[:, 0:EC], dst[0:EC * P].rearrange("(p j) -> p j", p=P)).then_inc(loaded, 16)
            sp.dma_start(srcs[0:ER, EC:EJ], src[EC * P:E].rearrange("(p j) -> p j", j=1)).then_inc(loaded, 16)
            sp.dma_start(dsts[0:ER, EC:EJ], dst[EC * P:E].rearrange("(p j) -> p j", j=1)).then_inc(loaded, 16)
            sp.wait_ge(blank, 2)
            sp.dma_start(edge_list.rearrange("(p t) w -> p (t w)", p=P),
                         empty[:, :, :].rearrange("p t w -> p (t w)")).then_inc(blanked, 16)
            sp.wait_ge(blanked, 16)

        @order.gpsimd
        def _(pool):
            nc.gpsimd.iota(blocks[:, :], pattern=[[1, NT]], base=0, channel_multiplier=0,
                           allow_small_or_imprecise_dtypes=True).then_inc(iotas, 1)
            nc.gpsimd.iota(pair_no[:, :], pattern=[[1, PAIRS]], base=0, channel_multiplier=0,
                           allow_small_or_imprecise_dtypes=True).then_inc(iotas, 1)
            nc.gpsimd.memset(empty[:, :, 0], 0).then_inc(blank, 1)
            nc.gpsimd.memset(empty[:, :, 1], -1).then_inc(blank, 1)
            nc.gpsimd.memset(pos[:, :], 0.0).then_inc(pos_zero, 1)
            pool.wait_ge(pos_zero, 1)

            def place(turn, r, first):
                v = turn * 2 + r
                pool.wait_ge(ranked, v + 1)
                if not (first and r == 0):
                    pool.wait_ge(placed, v)
                nc.gpsimd.tensor_tensor(pos[:, :], pos[:, :], own_cum[:, r, :], ALU.add).then_inc(placed, 1)
            place(0, 0, True)
            place(0, 1, True)
            with pool.Fori(1, NT // 2) as turn:
                place(turn, 0, False)
                place(turn, 1, False)
            if NT % 2:
                place(NT // 2, 0, False)
        @order.vector
        def _(dve):
            nc.vector.memset(srcs[:, EC:EJ], 0).then_inc(cleared, 1)
            nc.vector.memset(dsts[:, EC:EJ], 0).then_inc(cleared, 1)
            nc.vector.memset(zero[:, :], 0.0)
            link = Chain(dve, chain)
            dve.wait_ge(loaded, 64)
            dve.wait_ge(iotas, 2)
            nc.vector.tensor_copy(pair[:, :, 0], dsts[:, :])
            nc.vector.tensor_single_scalar(pair[:, :, 1], srcs[:, :], P - 1, ALU.bitwise_and)
            link(nc.vector.tensor_single_scalar(blk_i[:, :], srcs[:, :], 7, ALU.logical_shift_right))
            link(nc.vector.tensor_copy(blk[:, :], blk_i[:, :]))
            link(nc.vector.memset(blk[ER:P, EC:EJ], -1.0))
            link(nc.vector.memset(blk_h[:, EJ:EJ + 1], -1.0))
            link(nc.vector.tensor_copy(blk_h[:, 0:EJ], blk[:, :]))
            with dve.Fori(0, NT) as v:
                nc.vector.tensor_scalar(hit_h[:, :], blk_h[:, :], blocks[:, ds(v, 1)], 0.0, ALU.is_equal, ALU.add,
                                        accum_out=cnt[:, ds(v, 1)]).then_inc(counted, 1)
                dve.wait_ge(counted, v + 1)
            dve.wait_ge(sums, 1)
            link(nc.vector.tensor_scalar(tot_i[:, :], ps_a[:, 0:NT], float(UNIT - 1), None, ALU.add))
            link(nc.vector.tensor_single_scalar(tot_i[:, :], tot_i[:, :], 8, ALU.logical_shift_right))
            link(nc.vector.tensor_copy(npair[:, :], tot_i[:, :]))
            link(nc.vector.tensor_tensor_scan(pair_end[:, :], npair[:, :], zero[:, 0:NT], 0.0, ALU.add, ALU.add))
            nc.vector.tensor_copy(end_col[0:1, 0:1], pair_end[0:1, 0:1]).then_inc(ends, 1)
            link(nc.vector.tensor_tensor(base[:, :], pair_end[:, :], npair[:, :], ALU.subtract))
            link(nc.vector.tensor_scalar(base[:, :], base[:, :], float(UNIT), -1.0, ALU.mult, ALU.add))
            link(nc.vector.tensor_tensor(base[:, :], base[:, :], ps_a[:, NT:2 * NT], ALU.add))
            dve.wait_ge(ends_t, 1)
            link(nc.vector.tensor_copy(end_col[:, :], ps_t[0:NT, 0:P]))
            nc.vector.tensor_scalar(past[:, :], pair_no[:, :], end_col[:, 0:1], None, ALU.is_ge).then_inc(past_ready, 1)
            dve.wait_ge(blocks_of, 1)
            link(nc.vector.tensor_scalar(g.pair_block[:, :].rearrange("a (c n) -> a c n", c=4),
                                         ps_b[0:1, :, 0:PAIRS // 4], float(NT - 1), None, ALU.min))
            SORT_STEPS = 2

            def ranks(turn, r, first):
                v = turn * 2 + r
                step = Chain(dve, chain_v, SORT_STEPS, v)
                step(nc.vector.tensor_scalar(hit_h[:, :], blk_h[:, :], blocks[:, ds(v, 1)], None, ALU.is_equal))
                step(nc.vector.tensor_tensor_scan(cum[:, :], hit_h[:, 0:EJ], zero[:, :], base[:, ds(v, 1)], ALU.add, ALU.add))
                step.end()
                if not first:
                    dve.wait_ge(placed, v - 1)
                nc.vector.scalar_tensor_tensor(own_cum[:, r, :], blk[:, :], blocks[:, ds(v, 1)], cum[:, :],
                                               ALU.is_equal, ALU.mult).then_inc(ranked, 1)
                dve.wait_ge(ranked, v + 1)
            ranks(0, 0, True)
            ranks(0, 1, True)
            with dve.Fori(1, NT // 2) as turn:
                ranks(turn, 0, False)
                ranks(turn, 1, False)
            if NT % 2:
                ranks(NT // 2, 0, False)
            dve.wait_ge(placed, NT)
            link(nc.vector.tensor_copy(addr[:, :], pos[:, :]))
            link(nc.vector.tensor_single_scalar(blk_i[:, :], addr[:, :], P - 1, ALU.bitwise_and))
            link(nc.vector.tensor_copy(blk[:, :], blk_i[:, :]))
            link(nc.vector.tensor_single_scalar(blk_i[:, :], addr[:, :], 7, ALU.logical_shift_right))
            link(nc.vector.tensor_copy(hit[:, :], blk_i[:, :]))
            link(nc.vector.scalar_tensor_tensor(addr[:, :], blk[:, :], float(TILES), hit[:, :], ALU.mult, ALU.add))

        @order.tensor
        def _(pe):
            pe.wait_ge(counted, NT)
            nc.tensor.matmul(ps_a[:, 0:NT], g.ones[:, :], cnt[:, :], start=True, stop=True)
            nc.tensor.matmul(ps_a[:, NT:2 * NT], g.before[:, :], cnt[:, :], start=True, stop=True).then_inc(sums, 1)
            pe.wait_ge(ends, 1)
            nc.tensor.transpose(ps_t[0:NT, 0:P], pair_end[:, :], g.ident[:, :]).then_inc(ends_t, 1)
            pe.wait_ge(past_ready, 1)
            for c in range(4):
                last = nc.tensor.matmul(ps_b[:, c, 0:PAIRS // 4], g.ones[0:NT, :],
                                        past[:, c * (PAIRS // 4):(c + 1) * (PAIRS // 4)], start=True, stop=True)
            last.then_inc(blocks_of, 1)


def stage_list(nc, g, lo):
    with stage(nc) as own:
        back = own.enter_context(nc.sbuf_tensor("list_back", [P, TILES, 2], I32))
        listed, chain = own.enter_context(semaphore(nc, "list_read")), own.enter_context(semaphore(nc, "list_chain"))
        with nc.Block() as block:
            @block.gpsimd
            def _(pool):
                if lo < SCATTER_TURNS:
                    scatter_edges(nc, g, pool, lo, SCATTER_TURNS)
                pool.wait_ge(g.scattered[0], SCATTER_TURNS * (16 * HALF))
                nc.gpsimd.tensor_copy(g.st_addr[:, 0:1], g.addr[:, EC:EJ]).then_inc(g.pairs_staged, 1)
                nc.gpsimd.tensor_copy(g.st_pair[:, 0, :], g.pair[:, EC, :]).then_inc(g.pairs_staged, 1)
                pool.wait_ge(g.pairs_staged, 4 * SCATTER_TURNS + 2)
                pool.nop(nofuse=True)
                pool.indirect_dma_start(g.edge_list, bass.IndirectOffsetOnAxis(ap=g.st_addr[0:ER, 0:1], axis=0),
                                        g.st_pair[0:ER, 0, :], None).then_inc(g.scattered[0], 16)

            @block.sync
            def _(sp):
                sp.wait_ge(g.scattered[0], 16 * HALF * SCATTER_TURNS + 16)
                sp.wait_ge(g.scattered[1], 16 * HALF * SCATTER_TURNS)
                sp.dma_start(back[:, :, :].rearrange("p t w -> p (t w)"),
                             g.edge_list.rearrange("(p t) w -> p (t w)", p=P)).then_inc(listed, 16)

            @block.vector
            def _(dve):
                dve.wait_ge(listed, 16)
                nc.vector.tensor_copy(g.col_idx[:, :], back[:, :, 0])
                link = Chain(dve, chain)
                link(nc.vector.tensor_copy(g.row_loc[:, :], back[:, :, 1]))
                nc.vector.tensor_scalar(g.empty_bias[:, :], g.row_loc[:, :], 0.0, -BIG, ALU.is_lt, ALU.mult)


def stage_aggregate(nc, g, tag, table, width, shared, rows, acc, top):
    STEPS = TILES // KT
    TURNS = STEPS // STEP_RING
    VW = width - 4
    KP = KT // 2
    with stage(nc) as own:
        def sb(name, shape, dt=F32):
            return own.enter_context(nc.sbuf_tensor(name + tag, shape, dt))

        def sem(name):
            return own.enter_context(semaphore(nc, name + tag))
        got = sb("got", [P, STEP_RING, KT, width])
        st_idx = sb("st_idx", [P, STEP_RING, KT], I32)
        hot = sb("hot", [P, STEP_RING, KT, P])
        hot_t = sb("hot_t", [P, 2, KT, P])
        weighted = sb("weighted", [P, 2, KT, AW])
        z = sb("z", [P, KT, 4])
        z2 = sb("z2", [P, KT, 4])
        ps_t = own.enter_context(nc.psum_tensor("ps_hot" + tag, [P, KT * P], F32))
        ps_s = own.enter_context(nc.psum_tensor("ps_score" + tag, [P, 2, 512], F32))
        ps_g = own.enter_context(nc.psum_tensor("ps_sum" + tag, [P, KP, 512], F32))
        idx_staged, hot_ready, hot_turned, hot_copied = sem("idx_staged"), sem("hot_ready"), sem("hot_turned"), sem("hot_copied")
        scored, z_ready, w_ready, scaled = sem("scored"), sem("z_ready"), sem("w_ready"), sem("scaled")
        summed, added, chain, cleared = sem("summed"), sem("added"), sem("z_chain"), sem("acc_cleared")
        gathered = [sem(f"gathered{r}") for r in range(STEP_RING)]
        block = own.enter_context(nc.Block())

        def scores(r):
            return ps_s[:, r % 2, 0:KT * 8].rearrange("p (k c) -> p k c", c=8)

        def blocks_of(pair, count, engine):
            _, values = nc.values_load_multi_w_load_instructions(g.pair_block[0:1, ds(pair, count)], engines=(engine,),
                                                                 min_val=0, max_val=NT - 1)
            return values

        def later(turn, r, by):
            return turn + (r + by) // STEP_RING, (r + by) % STEP_RING

        def exists(last, r, by):
            return not last or r + by < STEP_RING

        def all_turns(eng, one_turn):
            one_turn(0, True, False)
            with eng.Fori(1, TURNS - 1) as turn:
                one_turn(turn, False, False)
            one_turn(TURNS - 1, False, True)

        @block.gpsimd
        def _(pool):
            def gather(turn, r, first):
                j = turn * STEP_RING + r
                pool.wait_ge(idx_staged, j + 1)
                if not first:
                    pool.wait_ge(scaled, j - (STEP_RING - 1))
                pool.nop(nofuse=True)
                for k in range(KT):
                    pool.indirect_dma_start(got[:, r, k, :], None, table,
                                            bass.IndirectOffsetOnAxis(ap=st_idx[:, r, k:k + 1], axis=0))\
                        .then_inc(gathered[r], 16)
            for r in range(STEP_RING):
                gather(0, r, True)
            with pool.Fori(1, TURNS) as turn:
                for r in range(STEP_RING):
                    gather(turn, r, False)

        @block.scalar
        def _(act):
            def weigh(turn, r, first):
                i = turn * STEP_RING + r
                act.wait_ge(z_ready, i + 1)
                if not (first and r < 2):
                    act.wait_ge(summed, (i - 1) * KP)
                nc.scalar.activation(weighted[:, r % 2, :, 256:AW], z[:, :, :], ACT.Exp).then_inc(w_ready, 1)

            def keep_turned(turn, r, first):
                i = turn * STEP_RING + r
                act.wait_ge(hot_turned, i + 1)
                if not (first and r < 2):
                    act.wait_ge(scored, i - 1)
                for c in range(2):
                    last = nc.scalar.copy(hot_t[:, r % 2, :, :].rearrange("p k n -> p (k n)")[:, c * 512:(c + 1) * 512],
                                          ps_t[:, c * 512:(c + 1) * 512])
                last.then_inc(hot_copied, 1)

            def one_turn(turn, first, last):
                for r in range(STEP_RING):
                    if exists(last, r, 2):
                        t, q = later(turn, r, 2)
                        keep_turned(t, q, first and r + 2 < STEP_RING)
                    if exists(last, r, 1):
                        t, q = later(turn, r, 1)
                        weigh(t, q, first and r + 1 < STEP_RING)
            keep_turned(0, 0, True)
            keep_turned(0, 1, True)
            weigh(0, 0, True)
            all_turns(act, one_turn)

        @block.tensor
        def _(pe):
            def turn_and_score(turn, r, first):
                i = turn * STEP_RING + r
                pe.wait_ge(hot_ready, i + 1)
                if not (first and r == 0):
                    pe.wait_ge(hot_copied, i)
                for k in range(KT):
                    last = nc.tensor.transpose(ps_t[:, k * P:(k + 1) * P], hot[:, r, k, :], g.ident[:, :])
                last.then_inc(hot_turned, 1)
                blocks = blocks_of(i * KP, KP, mybir.EngineType.PE)
                if not (first and r < 2):
                    pe.wait_ge(z_ready, i - 1)
                pe.wait_ge(hot_copied, i + 1)
                for k in range(KT):
                    b = blocks[k // 2]
                    last = nc.tensor.matmul(ps_s[:, r % 2, k * 8:(k + 1) * 8], hot_t[:, r % 2, k, :], rows[:, ds(b * 8, 8)],
                                            start=True, stop=True)
                last.then_inc(scored, 1)

            def sum_up(turn, r, first, half):
                i = turn * STEP_RING + r
                pe.wait_ge(scaled, i + 1)
                for p in half:
                    if not (first and r == 0):
                        pe.wait_ge(added, i * KP + (p - KP + 1))
                    for k in (2 * p, 2 * p + 1):
                        last = nc.tensor.matmul(ps_g[:, p, 0:AW], hot[:, r, k, :], weighted[:, r % 2, k, :],
                                                start=(k == 2 * p), stop=(k == 2 * p + 1))
                    last.then_inc(summed, 1)

            def one_turn(turn, first, last):
                for r in range(STEP_RING):
                    sum_up(turn, r, first, range(KP // 2))
                    if exists(last, r, 2):
                        t, q = later(turn, r, 2)
                        turn_and_score(t, q, first and r + 2 < STEP_RING)
                    sum_up(turn, r, first, range(KP // 2, KP))
            turn_and_score(0, 0, True)
            turn_and_score(0, 1, True)
            all_turns(pe, one_turn)

        @block.vector
        def _(dve):
            def stage_idx(turn, r):
                nc.vector.tensor_copy(st_idx[:, r, :], g.col_idx[:, ds((turn * STEP_RING + r) * KT, KT)]).then_inc(idx_staged, 1)

            def one_hot(turn, r):
                j = (turn * STEP_RING + r) * KT
                nc.vector.tensor_tensor(hot[:, r, :, :], g.iota_row[:, :].unsqueeze(1).to_broadcast([P, KT, P]),
                                        g.row_loc[:, ds(j, KT)].unsqueeze(2).to_broadcast([P, KT, P]),
                                        ALU.is_equal).then_inc(hot_ready, 1)

            def exponents(turn, r):
                i = turn * STEP_RING + r
                link = Chain(dve, chain, 4, i)
                dve.wait_ge(gathered[r], turn * (16 * KT) + 16 * KT)
                link(nc.vector.tensor_tensor(z2[:, :, :], got[:, r, :, VW:width],
                                             g.empty_bias[:, ds(i * KT, KT)].unsqueeze(2).to_broadcast([P, KT, 4]), ALU.add))
                dve.wait_ge(scored, i + 1)
                link(nc.vector.tensor_tensor(z2[:, :, :], z2[:, :, :], scores(r)[:, :, 0:4], ALU.add))
                link(nc.vector.tensor_tensor(top[:, :, :], top[:, :, :], z2[:, :, :], ALU.max))
                link(nc.vector.scalar_tensor_tensor(z2[:, :, :], z2[:, :, :], 0.2, z2[:, :, :], ALU.mult, ALU.max))
                nc.vector.tensor_tensor(z[:, :, :], z2[:, :, :], scores(r)[:, :, 4:8], ALU.subtract).then_inc(z_ready, 1)
                link.end()

            def scale(turn, r):
                i = turn * STEP_RING + r
                dve.wait_ge(w_ready, i + 1)
                w = weighted[:, r % 2, :, 256:AW].unsqueeze(3).to_broadcast([P, KT, 4, 64])
                out = weighted[:, r % 2, :, 0:256].rearrange("p k (h d) -> p k h d", h=4)
                if shared:
                    v = got[:, r, :, 0:64].unsqueeze(2).to_broadcast([P, KT, 4, 64])
                else:
                    v = got[:, r, :, 0:256].rearrange("p k (h d) -> p k h d", h=4)
                nc.vector.tensor_tensor(out, v, w, ALU.mult).then_inc(scaled, 1)

            def add(turn, r, first, half, blocks):
                i = turn * STEP_RING + r
                for p, b in zip(half, blocks):
                    dve.wait_ge(summed, i * KP + p + 1)
                    if not (first and r == 0 and p == 0):
                        dve.wait_ge(added, i * KP + p)
                    nc.vector.tensor_tensor(acc[:, ds(b * AW, AW)], acc[:, ds(b * AW, AW)], ps_g[:, p, 0:AW],
                                            ALU.add).then_inc(added, 1)
            LOW, HIGH = range(KP // 2), range(KP // 2, KP)
            DVE = mybir.EngineType.DVE

            def one_turn(turn, first, last):
                for r in range(STEP_RING):
                    i = turn * STEP_RING + r
                    t, q = (turn, r - 1) if r else (turn - 1, STEP_RING - 1)
                    if first and r == 0:
                        blocks = (None,) * len(HIGH) + tuple(blocks_of(i * KP, len(LOW), DVE))
                    else:
                        blocks = blocks_of(i * KP - len(HIGH), KP, DVE)
                    if not last:
                        stage_idx(turn + 1, r)
                    scale(turn, r)
                    if not (first and r == 0):
                        add(t, q, first, HIGH, blocks[:len(HIGH)])
                    if exists(last, r, 3):
                        one_hot(*later(turn, r, 3))
                    if exists(last, r, 1):
                        exponents(*later(turn, r, 1))
                    add(turn, r, first, LOW, blocks[len(HIGH):])
                if last:
                    add(turn, STEP_RING - 1, False, HIGH, blocks_of(turn * STEP_RING * KP + (STEP_RING - 1) * KP + len(LOW), len(HIGH), DVE))
            nc.vector.memset(top[:, :, :], -BIG).then_inc(cleared, 1)
            nc.vector.memset(acc[:, :], 0.0).then_inc(cleared, 1)
            for r in range(STEP_RING):
                stage_idx(0, r)
            for r in range(3):
                one_hot(0, r)
            dve.wait_ge(cleared, 2)
            exponents(0, 0)
            all_turns(dve, one_turn)

NTP = NT + NT % 2
NPAD = NTP * P
HALF2 = NTP // 2
SCATTERS = {"table": (0, 6), "moments": (6, 12), "mix": (12, 53), "ball": (53, 57)}
LIM = 0.9999899864196777
ATANH_LIM = 0.5 * math.log((1.0 + LIM) / (1.0 - LIM))


def stage_load(nc, g, x, ctx):
    g.x = ctx.enter_context(nc.sbuf_tensor("x_res", [P, NTP, D], F32))
    g.mean = ctx.enter_context(nc.sbuf_tensor("ln_mean", [P, NTP], F32))
    g.rstd = ctx.enter_context(nc.sbuf_tensor("ln_rstd", [P, NTP], F32))
    g.var = ctx.enter_context(nc.sbuf_tensor("ln_var", [P, NTP], F32))
    with stage(nc) as own:
        blank, loaded = own.enter_context(semaphore(nc, "x_blank")), own.enter_context(semaphore(nc, "x_loaded"))
        with nc.Block() as block:
            @block.vector
            def _(dve):
                nc.vector.memset(g.x[:, NT - 1:NTP, :], 0.0).then_inc(blank, 1)

            @block.sync
            def _(sp):
                sp.dma_start(g.x[:, 0:NT - 1, :], x[0:(NT - 1) * P, :].rearrange("(t p) d -> p t d", p=P)).then_inc(loaded, 16)
                sp.wait_ge(blank, 1)
                sp.dma_start(g.x[0:LAST, NT - 1, :], x[(NT - 1) * P:N, :]).then_inc(loaded, 16)
                sp.wait_ge(loaded, 32)


def stage_ln_stats(nc, g, tag, eps=1e-5, source=None):
    if source is None:
        def source(i):
            return g.x[:, ds(i, 1), :].rearrange("p t d -> p (t d)")
    with stage(nc) as own:
        def sem(name):
            return own.enter_context(semaphore(nc, name + tag))
        stats = own.enter_context(nc.sbuf_tensor("stats" + tag, [P, NTP * 6], F32))
        sd = own.enter_context(nc.sbuf_tensor("sd" + tag, [P, NTP], F32))
        got, spread, chain, rooted = sem("stat_got"), sem("spread"), sem("stat_chain"), sem("rooted")
        with nc.Block() as block:
            @block.vector
            def _(dve):
                with dve.Fori(0, NTP) as i:
                    nc.vector.bn_stats(stats[:, ds(i * 6, 6)], source(i)).then_inc(got, 1)
                dve.wait_ge(got, NTP)
                half = stats[:, :].rearrange("p (t c) -> p t c", c=6)
                link = Chain(dve, chain)
                link(nc.vector.tensor_tensor(g.mean[:, :], half[:, :, 1], half[:, :, 4], ALU.add))
                link(nc.vector.tensor_scalar(g.mean[:, :], g.mean[:, :], 0.5, None, ALU.mult))
                link(nc.vector.tensor_tensor(sd[:, :], half[:, :, 1], g.mean[:, :], ALU.subtract))
                link(nc.vector.tensor_tensor(sd[:, :], sd[:, :], sd[:, :], ALU.mult))
                link(nc.vector.tensor_tensor(g.var[:, :], half[:, :, 2], half[:, :, 5], ALU.add))
                link(nc.vector.scalar_tensor_tensor(g.var[:, :], g.var[:, :], 1.0 / D, sd[:, :], ALU.mult, ALU.add))
                nc.vector.tensor_scalar(sd[:, :], g.var[:, :], eps, None, ALU.add).then_inc(spread, 1)
                dve.wait_ge(rooted, 1)
                nc.vector.reciprocal(g.rstd[:, :], sd[:, :])

            @block.scalar
            def _(act):
                act.wait_ge(spread, 1)
                nc.scalar.activation(sd[:, :], sd[:, :], ACT.Sqrt).then_inc(rooted, 1)


def stage_l0_gnn_table(nc, g, w, w_t, b, a_src, a_dst, table):
    with stage(nc) as own:
        def sb(name, shape, dt=F32):
            return own.enter_context(nc.sbuf_tensor(name, shape, dt))

        def sem(name):
            return own.enter_context(semaphore(nc, name))

        def pb(name, shape):
            return own.enter_context(nc.psum_tensor(name, shape, F32))
        wl = sb("wl", [P, 2, 72])
        wt = sb("wt", [64, 256])
        eye_a = sb("eye_a", [64, 72])
        b_col = sb("b_col", [64, 1])
        b_wide = sb("b_wide", [64, P])
        bias = sb("bias_bc", [P, 72])
        n = sb("n0", [P, NTP])
        f = sb("f0", [P, NTP])
        inv_f = sb("inv_f0", [P, NTP])
        q = sb("q0", [P, NTP])
        lo = sb("lo0", [P, NTP])
        hi = sb("hi0", [P, NTP])
        small = sb("small0", [P, NTP], I32)
        scl = sb("scl0", [P, NTP])
        xs = sb("xs", [P, 2, D])
        st = sb("st0", [P, 2, 2, P])
        row = sb("row0", [P, 2, 72])
        colmax = sb("colmax", [P, 4])
        allmax = sb("allmax", [P, 4])
        ps_x = pb("ps_x0", [P, 2, 512])
        ps_r = pb("ps_r0", [P, 2, 512])
        ps_w = pb("ps_w0", [P, 2, 512])
        loaded, chain, prepared, biased = sem("w0_loaded"), sem("f0_chain"), sem("w0_prepared"), sem("b0_ready")
        rooted, logged, tail, wide = sem("n0_rooted"), sem("n0_logged"), sem("log_in"), sem("b_wide_ready")
        xs_ready, turned, staged, kept = sem("xs_ready"), sem("xs_turned"), sem("xs_staged"), sem("xt_kept")
        rowed, row_ready, written, factors = sem("row_mm"), sem("row_ready"), [sem("row_out0"), sem("row_out1")], sem("factors")
        reduced, maxed, maxes = sem("max_reduced"), sem("max_ready"), sem("run_max")
        wl_ready = sem("wl_ready")
        with nc.Block() as block:
            @block.sync
            def _(sp):
                with nc.allow_non_contiguous_dma(reason="small columns"):
                    sp.dma_start(wl[:, :, 0:64], w.rearrange("(c p) n -> p c n", p=P)).then_inc(loaded, 16)
                    sp.dma_start(wt[:, :], w_t).then_inc(loaded, 16)
                    sp.dma_start(eye_a[:, 64:68], a_dst).then_inc(loaded, 16)
                    sp.dma_start(eye_a[:, 68:72], a_src).then_inc(loaded, 16)
                    sp.dma_start(b_col[:, :], b.rearrange("(p o) -> p o", o=1)).then_inc(loaded, 16)

                def put(turn, r):
                    sp.wait_ge(row_ready, turn * 2 + (r + 1))
                    sp.dma_start(table[ds((turn * 2 + r) * P, P), :], row[:, r, 0:68]).then_inc(written[r], 16)
                with sp.Fori(0, HALF2) as turn:
                    put(turn, 0)
                    put(turn, 1)
                for r in range(2):
                    sp.wait_ge(written[r], 16 * HALF2)

            @block.scalar
            def _(act):
                act.wait_ge(chain, 2)
                nc.scalar.activation(n[:, :], q[:, :], ACT.Sqrt).then_inc(rooted, 1)
                act.wait_ge(tail, 1)
                nc.scalar.activation(lo[:, :], lo[:, :], ACT.Ln).then_inc(logged, 1)

                def stage(turn, r, first):
                    i = turn * 2 + r
                    act.wait_ge(turned, i + 1)
                    if not first:
                        act.wait_ge(rowed, i - 1)
                        act.wait_ge(kept, i - 1)
                    nc.scalar.copy(st[:, r, :, :].rearrange("p c n -> p (c n)"), ps_x[:, r, 0:256]).then_inc(staged, 1)
                stage(0, 0, True)
                stage(0, 1, True)
                with act.Fori(1, HALF2) as turn:
                    stage(turn, 0, False)
                    stage(turn, 1, False)

            @block.gpsimd
            def _(pool):
                scatter_edges(nc, g, pool, *SCATTERS["table"])
                pool.wait_ge(maxes, NTP)
                nc.gpsimd.partition_all_reduce(allmax[:, :], colmax[:, :], P, bass.bass_isa.ReduceOp.max).then_inc(reduced, 1)

            @block.tensor
            def _(pe):
                pe.wait_ge(loaded, 80)
                for c in range(2):
                    nc.tensor.matmul(ps_w[:, c, 0:8], wt[:, c * P:(c + 1) * P], eye_a[:, 64:72],
                                     start=True, stop=True).then_inc(prepared, 1)
                pe.wait_ge(wide, 2)
                nc.tensor.matmul(ps_x[:, 0, 0:72], b_wide[:, :], eye_a[:, :], start=True, stop=True).then_inc(biased, 1)
                pe.wait_ge(factors, 1)

                def turn_tile(turn, r, first):
                    i = turn * 2 + r
                    pe.wait_ge(xs_ready, i + 1)
                    if not first:
                        pe.wait_ge(staged, i - 1)
                    for c in range(2):
                        last = nc.tensor.transpose(ps_x[:, r, c * P:(c + 1) * P], xs[:, r, c * P:(c + 1) * P], g.ident[:, :])
                    last.then_inc(turned, 1)

                def row_tile(turn, r, first):
                    i = turn * 2 + r
                    pe.wait_ge(staged, i + 1)
                    if not first:
                        pe.wait_ge(row_ready, i - 1)
                    for c in range(2):
                        last = nc.tensor.matmul(ps_r[:, r, 0:72], st[:, r, c, :], wl[:, c, :], start=(c == 0), stop=(c == 1))
                    last.then_inc(rowed, 1)
                for first in (True, False):
                    def both(turn):
                        turn_tile(turn, 0, first)
                        turn_tile(turn, 1, first)
                        row_tile(turn, 0, first)
                        row_tile(turn, 1, first)
                    if first:
                        pe.wait_ge(wl_ready, 2)
                        both(0)
                    else:
                        with pe.Fori(1, HALF2) as turn:
                            both(turn)

            @block.vector
            def _(dve):
                link = Chain(dve, chain)
                link(nc.vector.tensor_tensor(q[:, :], g.rstd[:, :], g.rstd[:, :], ALU.mult))
                link(nc.vector.scalar_tensor_tensor(q[:, :], g.var[:, :], float(D), q[:, :], ALU.mult, ALU.mult))
                dve.wait_ge(rooted, 1)
                link(nc.vector.tensor_scalar(n[:, :], n[:, :], 1e-15, None, ALU.max))
                link(nc.vector.tensor_scalar(q[:, :], n[:, :], LIM, None, ALU.min))
                link(nc.vector.tensor_scalar(hi[:, :], q[:, :], -1.0, 1.0, ALU.mult, ALU.add))
                link(nc.vector.reciprocal(hi[:, :], hi[:, :]))
                link(nc.vector.scalar_tensor_tensor(lo[:, :], q[:, :], 1.0, hi[:, :], ALU.add, ALU.mult))
                nc.vector.tensor_scalar(small[:, :], q[:, :], 0.25, None, ALU.is_lt).then_inc(tail, 1)
                link(nc.vector.tensor_tensor(scl[:, :], q[:, :], q[:, :], ALU.mult))
                link(nc.vector.tensor_scalar(hi[:, :], scl[:, :], 1.0 / 15, 1.0 / 13, ALU.mult, ALU.add))
                for k in (11, 9, 7, 5, 3, 1):
                    link(nc.vector.tensor_tensor(hi[:, :], hi[:, :], scl[:, :], ALU.mult))
                    link(nc.vector.tensor_scalar(hi[:, :], hi[:, :], 1.0 / k, None, ALU.add))
                link(nc.vector.tensor_tensor(hi[:, :], hi[:, :], q[:, :], ALU.mult))
                dve.wait_ge(logged, 1)
                link(nc.vector.tensor_scalar(lo[:, :], lo[:, :], 0.5, None, ALU.mult))
                link(nc.vector.copy_predicated(lo[:, :], small[:, :], hi[:, :]))
                link(nc.vector.reciprocal(n[:, :], n[:, :]))
                link(nc.vector.tensor_tensor(f[:, :], lo[:, :], n[:, :], ALU.mult))
                link(nc.vector.reciprocal(inv_f[:, :], f[:, :]))
                link(nc.vector.tensor_tensor(scl[:, :], f[:, :], g.rstd[:, :], ALU.mult))
                dve.wait_ge(loaded, 80)
                nc.vector.tensor_copy(eye_a[:, 0:64], g.ident[0:64, 0:64]).then_inc(wide, 1)
                nc.vector.tensor_copy(b_wide[:, :], b_col[:, :].to_broadcast([64, P])).then_inc(wide, 1)
                for c in range(2):
                    dve.wait_ge(prepared, c + 1)
                    nc.vector.tensor_copy(wl[:, c, 64:72], ps_w[:, c, 0:8]).then_inc(wl_ready, 1)
                dve.wait_ge(biased, 1)
                nc.vector.tensor_copy(bias[:, :], ps_x[:, 0, 0:72]).then_inc(factors, 1)
                link(nc.vector.memset(colmax[:, :], -BIG))
                dve.wait_ge(factors, 1)

                def norm(turn, r, first):
                    i = turn * 2 + r
                    if not first:
                        dve.wait_ge(turned, i - 1)
                    nc.vector.tensor_scalar(xs[:, r, :], g.x[:, ds(i, 1), :].rearrange("p t d -> p (t d)"),
                                            g.mean[:, ds(i, 1)], scl[:, ds(i, 1)], ALU.subtract, ALU.mult).then_inc(xs_ready, 1)

                def finish(turn, r, first):
                    i = turn * 2 + r
                    dve.wait_ge(staged, i + 1)
                    nc.vector.tensor_copy(g.xt[:, :, ds(i * P, P)], st[:, r, :, :]).then_inc(kept, 1)
                    dve.wait_ge(rowed, i + 1)
                    if not first:
                        dve.wait_ge(written[r], turn * 16)
                    nc.vector.scalar_tensor_tensor(row[:, r, :], ps_r[:, r, 0:72], inv_f[:, ds(i, 1)], bias[:, :],
                                                   ALU.mult, ALU.add).then_inc(row_ready, 1)
                    dve.wait_ge(row_ready, i + 1)
                    nc.vector.tensor_copy(g.rows[:, ds(i * 8, 4)], row[:, r, 68:72])
                    if not (first and r == 0):
                        dve.wait_ge(maxes, i)
                    nc.vector.tensor_tensor(colmax[:, :], colmax[:, :], row[:, r, 64:68], ALU.max).then_inc(maxes, 1)
                norm(0, 0, True)
                norm(0, 1, True)
                finish(0, 0, True)
                finish(0, 1, True)
                with dve.Fori(1, HALF2) as turn:
                    norm(turn, 0, False)
                    norm(turn, 1, False)
                    finish(turn, 0, False)
                    finish(turn, 1, False)
                dve.wait_ge(maxes, NTP)
                dve.wait_ge(reduced, 1)
                rows = g.rows[:, :].rearrange("p (t c) -> p t c", c=8)
                link(nc.vector.tensor_tensor(rows[:, :, 4:8], rows[:, :, 0:4],
                                             allmax[:, :].unsqueeze(1).to_broadcast([P, NTP, 4]), ALU.add))
                link(nc.vector.scalar_tensor_tensor(rows[:, :, 4:8], rows[:, :, 4:8], 0.2, rows[:, :, 4:8], ALU.mult, ALU.max))
                link(nc.vector.tensor_scalar(rows[:, :, 4:8], rows[:, :, 4:8], -HEADROOM, None, ALU.add))


def stage_l0_mix(nc, g, w_qkv, bn_g, bn_b, w_dw, w_pw, w_res, b_res):
    M = 6
    with ExitStack() as mid:
        def sbm(name, shape, dt=F32):
            return mid.enter_context(nc.sbuf_tensor(name, shape, dt))
        wq = sbm("wq", [P, 2, M * P])
        gam = sbm("bn_gamma", [P, M])
        bet = sbm("bn_beta", [P, M])
        dw = sbm("dw", [P, M])
        pw = sbm("pw", [P, M, 32])
        bd = sbm("bd", [P, M, P])
        wr = sbm("wr", [P, 4, D])
        br = sbm("br", [P, D])

        def ft(i):
            return g.xt[:, :, ds(i * P, P)]

        def two(ap):
            return ap.rearrange("p (c n) -> p c n", c=2)
        s3 = sbm("s3", [P, NTP])
        s4 = sbm("s4", [P, NTP])
        FT_ = 512
        FULL = N // FT_
        REST = N - FULL * FT_
        with stage(nc) as own:
            def sb(name, shape, dt=F32):
                return own.enter_context(nc.sbuf_tensor(name, shape, dt))

            def sem(name):
                return own.enter_context(semaphore(nc, name))
            st6 = sb("st6", [P, M, (FULL + 1) * 6])
            mv = sb("mv6", [P, M, 2])
            tmp = sb("tmp6", [P, M])
            pst = own.enter_context(nc.psum_tensor("ps_bn", [P, M, 512], F32))
            ps_b = own.enter_context(nc.psum_tensor("ps_bd", [P, 512], F32))
            loaded, made, seen, chain, root = sem("wq_loaded"), sem("bn_h"), sem("bn_seen"), sem("bn_chain"), sem("bn_root")
            pw_t, bd0 = sem("pw_spread"), sem("bd_zero")
            own.enter_context(nc.allow_non_contiguous_dma(reason="per channel columns"))
            with nc.Block() as block:
                @block.sync
                def _(sp):
                    sp.dma_start(wq[:, :, :], w_qkv.rearrange("(c p) n -> p c n", p=P)).then_inc(loaded, 16)
                    for t, a in ((gam, bn_g), (bet, bn_b), (dw, w_dw)):
                        sp.dma_start(t[:, :], a.rearrange("(m p) -> p m", p=P)).then_inc(loaded, 16)
                    sp.dma_start(wr[:, :, :], w_res.rearrange("(c p) n -> p c n", p=P)).then_inc(loaded, 16)
                    sp.dma_start(br[:, :], b_res.rearrange("(o n) -> o n", o=1).to_broadcast([P, D])).then_inc(loaded, 16)
                    sp.wait_ge(bd0, 1)
                    for m in range(M):
                        for q in range(4):
                            c = m * P + 32 * q
                            sp.dma_start(bd[32 * q:32 * q + 32, m, 32 * q:32 * q + 32], w_pw[:, c:c + 32]).then_inc(loaded, 16)

                @block.gpsimd
                def _(pool):
                    nc.gpsimd.memset(bd[:, :, :], 0.0).then_inc(bd0, 1)
                    scatter_edges(nc, g, pool, *SCATTERS["moments"])

                @block.tensor
                def _(pe):
                    pe.wait_ge(loaded, 16 * (6 + 4 * M))

                    def tile(at, width, first, turn):
                        for m in range(M):
                            if not first:
                                pe.wait_ge(seen, turn * M + (m + 1 - M))
                            for c in range(2):
                                last = nc.tensor.matmul(pst[:, m, 0:width], wq[:, c, m * P:(m + 1) * P],
                                                        g.xt[:, c, ds(at, width)], start=(c == 0), stop=(c == 1))
                            last.then_inc(made, 1)
                    tile(0, FT_, True, 0)
                    with pe.Fori(1, FULL) as turn:
                        tile(turn * FT_, FT_, False, turn)
                    tile(FULL * FT_, REST, False, FULL)

                @block.scalar
                def _(act):
                    act.wait_ge(root, 1)
                    nc.scalar.activation(tmp[:, :], tmp[:, :], ACT.Sqrt).then_inc(root, 1)

                @block.vector
                def _(dve):
                    link = Chain(dve, chain)

                    def stat(turn, width):
                        for m in range(M):
                            dve.wait_ge(made, turn * M + (m + 1))
                            nc.vector.bn_stats(st6[:, m, ds(turn * 6, 6)], pst[:, m, 0:width]).then_inc(seen, 1)
                    with dve.Fori(0, FULL) as turn:
                        stat(turn, FT_)
                    stat(FULL, REST)
                    dve.wait_ge(seen, (FULL + 1) * M)
                    for m in range(M):
                        link(nc.vector.bn_aggr(mv[:, m, :], st6[:, m, :]))
                    nc.vector.tensor_scalar(tmp[:, :], mv[:, :, 1], 1e-5, None, ALU.add).then_inc(root, 1)
                    dve.wait_ge(root, 2)
                    dve.wait_ge(loaded, 16 * (6 + 4 * M))
                    link(nc.vector.reciprocal(tmp[:, :], tmp[:, :]))
                    link(nc.vector.tensor_tensor(gam[:, :], gam[:, :], tmp[:, :], ALU.mult))
                    link(nc.vector.tensor_tensor(tmp[:, :], mv[:, :, 0], gam[:, :], ALU.mult))
                    link(nc.vector.tensor_tensor(bet[:, :], bet[:, :], tmp[:, :], ALU.subtract))
                    link(nc.vector.tensor_tensor(bd[:, :, :], bd[:, :, :], dw[:, :].unsqueeze(2).to_broadcast([P, M, P]), ALU.mult))
        with stage(nc) as own:
            def sb(name, shape, dt=F32):
                return own.enter_context(nc.sbuf_tensor(name, shape, dt))

            def sem(name):
                return own.enter_context(semaphore(nc, name))
            ut = sb("ut", [P, M, 2 * P])
            junk = sb("junk_sq", [P, 1536])
            qk = sb("qk", [P, 2, 16, 2, 32])
            qs = sb("qs", [P, 16, 32])
            ks = sb("ks", [P, 16])
            v = sb("v_s", [P, 2, 512])
            den = sb("den_v", [P, 512])
            o = sb("o_s", [P, 2, 512])
            ot = sb("ot", [P, 2, 512])
            s2 = sb("s2", [P, 2])
            f2 = sb("f2", [P, 2])
            fr = sb("fr", [P, 2])
            ps_h = own.enter_context(nc.psum_tensor("ps_h", [P, M * 2 * P], F32))
            ps_c = own.enter_context(nc.psum_tensor("ps_cat", [P, 2 * M * P], F32))
            ps_o = own.enter_context(nc.psum_tensor("ps_o", [P, 512], F32))
            ps_g = own.enter_context(nc.psum_tensor("ps_g", [P, 512], F32))
            h_made, u_ready, cat_made, sq_ready = sem("h_made"), sem("u_ready"), sem("cat_made"), sem("sq_ready")
            f2_ready, f_ready, v_ready = sem("f2_ready"), sem("f_ready"), sem("v_ready")
            o_ready, o_turned, ot_ready, g_made, g_kept, chain, s3_ready = (
                sem("o_ready"), sem("o_turned"), sem("ot_ready"), sem("g_made"), sem("g_kept"), sem("mix_chain"), sem("s3_ready"))
            grp = ps_c[:, :].rearrange("p (g s e) -> p g s e", s=3, e=32)
            with nc.Block() as block:
                @block.gpsimd
                def _(pool):
                    scatter_edges(nc, g, pool, *SCATTERS["mix"])

                @block.tensor
                def _(pe):
                    def heads(turn, first):
                        if not first:
                            pe.wait_ge(u_ready, turn * M)
                        for m in range(M):
                            for c in range(2):
                                last = nc.tensor.matmul(ps_h[:, m * 2 * P:(m + 1) * 2 * P], wq[:, c, m * P:(m + 1) * P],
                                                        g.xt[:, c, ds(turn * (2 * P), 2 * P)], start=(c == 0), stop=(c == 1))
                            last.then_inc(h_made, 1)

                    def cat(turn, r, first):
                        i = turn * 2 + r
                        if not (first and r == 0):
                            pe.wait_ge(v_ready, i)
                        for m in range(M):
                            nc.tensor.transpose(ps_c[:, m * P:(m + 1) * P], ut[:, m, r * P:(r + 1) * P], g.ident[:, :])
                        for m in range(M):
                            last = nc.tensor.matmul(ps_c[:, (M + m) * P:(M + m + 1) * P], ut[:, m, r * P:(r + 1) * P],
                                                    bd[:, m, :], start=True, stop=True)
                        last.then_inc(cat_made, 1)

                    def out(turn, r, first):
                        i = turn * 2 + r
                        pe.wait_ge(o_ready, i + 1)
                        if not (first and r == 0):
                            pe.wait_ge(ot_ready, i)
                        for c in range(4):
                            last = nc.tensor.transpose(ps_o[:, c * P:(c + 1) * P], o[:, r, c * P:(c + 1) * P], g.ident[:, :])
                        last.then_inc(o_turned, 1)
                        pe.wait_ge(ot_ready, i + 1)
                        if not (first and r == 0):
                            pe.wait_ge(g_kept, i)
                        for c in range(4):
                            last = nc.tensor.matmul(ps_g[:, 0:D], ot[:, r, c * P:(c + 1) * P], wr[:, c, :],
                                                    start=(c == 0), stop=(c == 3))
                        last.then_inc(g_made, 1)

                    def both(turn, first):
                        heads(turn, first)
                        pe.wait_ge(u_ready, turn * M + M)
                        cat(turn, 0, first)
                        cat(turn, 1, first)
                        out(turn, 0, first)
                        out(turn, 1, first)
                    both(0, True)
                    with pe.Fori(1, HALF2) as turn:
                        both(turn, False)

                @block.scalar
                def _(act):
                    def both(turn, first):
                        if not first:
                            act.wait_ge(cat_made, turn * 2)
                        for m in range(M):
                            act.wait_ge(h_made, turn * M + (m | 1) + 1)
                            nc.scalar.activation(ut[:, m, :], ps_h[:, m * 2 * P:(m + 1) * 2 * P], ACT.Relu,
                                                 bias=bet[:, m:m + 1], scale=gam[:, m:m + 1]).then_inc(u_ready, 1)
                        for r in range(2):
                            i = turn * 2 + r
                            act.wait_ge(cat_made, i + 1)
                            if not (first and r == 0):
                                act.wait_ge(s3_ready, i)
                            nc.scalar.activation(junk[:, :], ps_c[:, :], ACT.Square, accum_out=s2[:, r:r + 1]).then_inc(sq_ready, 1)
                            if not first:
                                act.wait_ge(o_ready, i - 1)
                            nc.scalar.activation(qk[:, r, :, :, :], grp[:, :, 0:2, :], ACT.Relu).then_inc(sq_ready, 1)
                            act.wait_ge(f2_ready, i + 1)
                            nc.scalar.activation(fr[:, r:r + 1], f2[:, r:r + 1], ACT.Sqrt).then_inc(f_ready, 1)
                            act.wait_ge(f_ready, i + 1)
                            nc.scalar.activation(v[:, r, :].rearrange("p (g e) -> p g e", e=32), grp[:, :, 2, :], ACT.Copy,
                                                 scale=fr[:, r:r + 1]).then_inc(v_ready, 1)
                            act.wait_ge(o_ready, i + 1)
                            nc.scalar.activation(junk[:, 0:512], o[:, r, :], ACT.Square, accum_out=s3[:, ds(i, 1)]).then_inc(s3_ready, 1)
                            act.wait_ge(o_turned, i + 1)
                            if not first:
                                act.wait_ge(g_made, i - 1)
                            nc.scalar.copy(ot[:, r, :], ps_o[:, :]).then_inc(ot_ready, 1)
                    both(0, True)
                    with act.Fori(1, HALF2) as turn:
                        both(turn, False)

                @block.vector
                def _(dve):
                    def both(turn, first):
                        for r in range(2):
                            i = turn * 2 + r
                            link = Chain(dve, chain, 8, i)
                            dve.wait_ge(sq_ready, i * 2 + 1)
                            link(nc.vector.tensor_scalar(f2[:, r:r + 1], s2[:, r:r + 1], 1e-30, None, ALU.max))
                            link(nc.vector.reciprocal(f2[:, r:r + 1], f2[:, r:r + 1]))
                            nc.vector.tensor_scalar(f2[:, r:r + 1], f2[:, r:r + 1], ATANH_LIM ** 2, 1.0,
                                                    ALU.mult, ALU.min).then_inc(f2_ready, 1)
                            dve.wait_ge(sq_ready, i * 2 + 2)
                            link(nc.vector.tensor_reduce(ks[:, :], qk[:, r, :, 1, :], AX.X, ALU.add))
                            dve.wait_ge(f2_ready, i + 1)
                            link(nc.vector.tensor_scalar(ks[:, :], ks[:, :], f2[:, r:r + 1], None, ALU.mult))
                            link(nc.vector.tensor_tensor(qs[:, :, :], qk[:, r, :, 0, :],
                                                         ks[:, :].unsqueeze(2).to_broadcast([P, 16, 32]), ALU.mult))
                            dve.wait_ge(v_ready, i + 1)
                            link(nc.vector.tensor_scalar(den[:, :], v[:, r, :], 1e-15, None, ALU.add))
                            link(nc.vector.reciprocal(den[:, :], den[:, :]))
                            if not first:
                                dve.wait_ge(o_turned, i - 1)
                            link(nc.vector.tensor_tensor(den[:, :], den[:, :], v[:, r, :], ALU.mult))
                            nc.vector.tensor_tensor(o[:, r, :].rearrange("p (g e) -> p g e", e=32),
                                                    den[:, :].rearrange("p (g e) -> p g e", e=32),
                                                    qs[:, :, :], ALU.mult).then_inc(o_ready, 1)
                            link.end()
                            dve.wait_ge(g_made, i + 1)
                            nc.vector.tensor_copy(ft(i), two(ps_g[:, 0:D])).then_inc(g_kept, 1)
                    both(0, True)
                    with dve.Fori(1, HALF2) as turn:
                        both(turn, False)
        with stage(nc) as own:
            def sem(name):
                return own.enter_context(semaphore(nc, name))
            junk = own.enter_context(nc.sbuf_tensor("junk4", [P, D], F32))
            f3, f3r, n4, th, chain = sem("f3"), sem("f3r"), sem("n4"), sem("th"), sem("fx_chain")
            ft_ready, sq = sem("ft_ready"), sem("ft_sq")
            with nc.Block() as block:
                @block.gpsimd
                def _(pool):
                    scatter_edges(nc, g, pool, *SCATTERS["ball"])

                @block.vector
                def _(dve):
                    link = Chain(dve, chain)
                    link(nc.vector.tensor_scalar(s3[:, :], s3[:, :], 1e-30, None, ALU.max))
                    link(nc.vector.reciprocal(s3[:, :], s3[:, :]))
                    nc.vector.tensor_scalar(s3[:, :], s3[:, :], ATANH_LIM ** 2, 1.0, ALU.mult, ALU.min).then_inc(f3, 1)
                    dve.wait_ge(f3r, 1)
                    with dve.Fori(0, NTP) as i:
                        row = ft(i)
                        nc.vector.scalar_tensor_tensor(row, row, s3[:, ds(i, 1)], two(br[:, :]), ALU.mult, ALU.add).then_inc(ft_ready, 1)
                    dve.wait_ge(sq, NTP)
                    nc.vector.tensor_scalar(s4[:, :], s4[:, :], 1e-30, None, ALU.max).then_inc(n4, 1)
                    dve.wait_ge(th, 2)
                    link(nc.vector.reciprocal(s4[:, :], s4[:, :]))
                    link(nc.vector.tensor_scalar(s3[:, :], s3[:, :], LIM, None, ALU.min))
                    link(nc.vector.tensor_tensor(s3[:, :], s3[:, :], s4[:, :], ALU.mult))
                    with dve.Fori(0, NTP) as i:
                        row = ft(i)
                        xr = g.x[:, ds(i, 1), :].rearrange("p t (c n) -> p (t c) n", c=2)
                        nc.vector.scalar_tensor_tensor(xr, row, s3[:, ds(i, 1)], xr, ALU.mult, ALU.add)

                @block.scalar
                def _(act):
                    act.wait_ge(f3, 1)
                    nc.scalar.activation(s3[:, :], s3[:, :], ACT.Sqrt).then_inc(f3r, 1)
                    with act.Fori(0, NTP) as i:
                        act.wait_ge(ft_ready, i + 1)
                        nc.scalar.activation(two(junk[:, :]), ft(i), ACT.Square,
                                             accum_out=s4[:, ds(i, 1)]).then_inc(sq, 1)
                        act.wait_ge(sq, i + 1)
                    act.wait_ge(n4, 1)
                    nc.scalar.activation(s4[:, :], s4[:, :], ACT.Sqrt).then_inc(th, 1)
                    act.wait_ge(th, 1)
                    nc.scalar.activation(s3[:, :], s4[:, :], ACT.Tanh).then_inc(th, 1)

SUP = 7
SW = SUP * P
HW = SW // 2
SUPS = NT // SUP
EXPERTS = 8
assert SUPS * SUP == NT and HW <= 512


def stage_add_messages(nc, g, acc, tag, eps_term=None):
    with stage(nc) as own:
        chain = own.enter_context(semaphore(nc, "msg_chain" + tag))
        rden = own.enter_context(nc.sbuf_tensor("rden" + tag, [P, NT, 4], F32))
        a3 = acc[:, :].rearrange("p (t w) -> p t w", w=AW)
        with nc.Block() as block:
            @block.vector
            def _(dve):
                link = Chain(dve, chain)
                link(nc.vector.tensor_scalar(rden[:, :, :], a3[:, 0:NT, 256:AW], 1e-35, None, ALU.max))
                link(nc.vector.reciprocal(rden[:, :, :], rden[:, :, :]))
                for s in range(SUPS):
                    t = slice(s * SUP, (s + 1) * SUP)
                    part = a3[:, t, 0:256].rearrange("p t (h d) -> p t h d", h=4)
                    link(nc.vector.tensor_tensor(part, part, rden[:, t, :].unsqueeze(3).to_broadcast([P, SUP, 4, 64]), ALU.mult))
                    nc.vector.tensor_tensor(g.x[:, t, :], g.x[:, t, :], a3[:, t, 0:256], ALU.add)


def stage_turn(nc, g, tag, fill, width, out=None, table=None, source=None, keep_xt=True, gate=None):
    AT = D
    if source is None:
        def source(i):
            return g.x[:, ds(i, 1), :].rearrange("p t d -> p (t d)")
    with stage(nc) as own:
        def sb(name, shape, dt=F32):
            return own.enter_context(nc.sbuf_tensor(name + tag, shape, dt))

        def sem(name):
            return own.enter_context(semaphore(nc, name + tag))

        def pb(name, shape):
            return own.enter_context(nc.psum_tensor(name + tag, shape, F32))
        wl = sb("wl", [P, 2, width])
        bias = sb("bias_bc", [P, width])
        fill(own, wl, bias)
        xs = sb("xs", [P, 2, D])
        st = sb("st", [P, 2, 2, P])
        row = sb("row", [P, 2, width])
        colmax = sb("colmax", [P, 4])
        allmax = sb("allmax", [P, 4])
        ps_x = pb("ps_x", [P, 2, 512])
        ps_r = pb("ps_r", [P, 2, 512])
        xs_ready, turned, staged, kept = sem("xs_ready"), sem("xs_turned"), sem("xs_staged"), sem("xt_kept")
        rowed, row_ready, written = sem("row_mm"), sem("row_ready"), [sem("row_out0"), sem("row_out1")]
        reduced, maxes, chain = sem("max_reduced"), sem("run_max"), sem("turn_chain")
        with nc.Block() as block:
            if table is not None:
                @block.sync
                def _(sp):
                    def put(turn, r):
                        sp.wait_ge(row_ready, turn * 2 + (r + 1))
                        sp.dma_start(table[ds((turn * 2 + r) * P, P), :], row[:, r, 0:AT + 4]).then_inc(written[r], 16)
                    with sp.Fori(0, HALF2) as turn:
                        put(turn, 0)
                        put(turn, 1)
                    for r in range(2):
                        sp.wait_ge(written[r], 16 * HALF2)

            @block.scalar
            def _(act):
                def stage(turn, r, first):
                    i = turn * 2 + r
                    act.wait_ge(turned, i + 1)
                    if not first:
                        act.wait_ge(rowed, i - 1)
                        if keep_xt:
                            act.wait_ge(kept, i - 1)
                    nc.scalar.copy(st[:, r, :, :].rearrange("p c n -> p (c n)"), ps_x[:, r, 0:256]).then_inc(staged, 1)
                stage(0, 0, True)
                stage(0, 1, True)
                with act.Fori(1, HALF2) as turn:
                    stage(turn, 0, False)
                    stage(turn, 1, False)

            @block.gpsimd
            def _(pool):
                def keep(turn, r):
                    i = turn * 2 + r
                    pool.wait_ge(staged, i + 1)
                    nc.gpsimd.tensor_copy(g.xt[:, :, ds(i * P, P)], st[:, r, :, :]).then_inc(kept, 1)
                if keep_xt:
                    with pool.Fori(0, HALF2) as turn:
                        keep(turn, 0)
                        keep(turn, 1)
                if table is not None:
                    pool.wait_ge(maxes, NTP)
                    nc.gpsimd.partition_all_reduce(allmax[:, :], colmax[:, :], P, bass.bass_isa.ReduceOp.max).then_inc(reduced, 1)

            @block.tensor
            def _(pe):
                def turn_tile(turn, r, first):
                    i = turn * 2 + r
                    pe.wait_ge(xs_ready, i + 1)
                    if not first:
                        pe.wait_ge(staged, i - 1)
                    for c in range(2):
                        last = nc.tensor.transpose(ps_x[:, r, c * P:(c + 1) * P], xs[:, r, c * P:(c + 1) * P], g.ident[:, :])
                    last.then_inc(turned, 1)

                def row_tile(turn, r, first):
                    i = turn * 2 + r
                    pe.wait_ge(staged, i + 1)
                    if not first:
                        pe.wait_ge(row_ready, i - 1)
                    for c in range(2):
                        last = nc.tensor.matmul(ps_r[:, r, 0:width], st[:, r, c, :], wl[:, c, :], start=(c == 0), stop=(c == 1))
                    last.then_inc(rowed, 1)

                def both(turn, first):
                    turn_tile(turn, 0, first)
                    turn_tile(turn, 1, first)
                    row_tile(turn, 0, first)
                    row_tile(turn, 1, first)
                both(0, True)
                with pe.Fori(1, HALF2) as turn:
                    both(turn, False)

            @block.vector
            def _(dve):
                def norm(turn, r, first):
                    i = turn * 2 + r
                    if not first:
                        dve.wait_ge(turned, i - 1)
                    nc.vector.tensor_scalar(xs[:, r, :], source(i),
                                            g.mean[:, ds(i, 1)], g.rstd[:, ds(i, 1)], ALU.subtract, ALU.mult).then_inc(xs_ready, 1)

                def finish(turn, r, first):
                    i = turn * 2 + r
                    dve.wait_ge(rowed, i + 1)
                    if table is None and out is None:
                        nc.vector.tensor_tensor(row[:, r, :], ps_r[:, r, 0:width], bias[:, :], ALU.add).then_inc(row_ready, 1)
                        dve.wait_ge(row_ready, i + 1)
                        xr = g.x[:, ds(i, 1), :].rearrange("p t d -> p (t d)")
                        nc.vector.scalar_tensor_tensor(xr, row[:, r, :], 0.0, xr, ALU.max, ALU.add)
                        return
                    if table is None:
                        nc.vector.tensor_tensor(out[:, ds(i * width, width)], ps_r[:, r, 0:width], bias[:, :],
                                                ALU.add).then_inc(row_ready, 1)
                        return
                    if not first:
                        dve.wait_ge(written[r], turn * 16)
                    if gate is not None:
                        nc.vector.scalar_tensor_tensor(gate[0][:, ds(i * 64, 64)], ps_r[:, r, AT + 8:width], gate[1][:, ds(i, 1)],
                                                       bias[:, AT + 8:width], ALU.mult, ALU.add)
                    nc.vector.tensor_copy(row[:, r, 0:AT + 8], ps_r[:, r, 0:AT + 8]).then_inc(row_ready, 1)
                    dve.wait_ge(row_ready, i + 1)
                    nc.vector.tensor_copy(g.rows[:, ds(i * 8, 4)], row[:, r, AT + 4:AT + 8])
                    if not (first and r == 0):
                        dve.wait_ge(maxes, i)
                    nc.vector.tensor_tensor(colmax[:, :], colmax[:, :], row[:, r, AT:AT + 4], ALU.max).then_inc(maxes, 1)
                link = Chain(dve, chain)
                link(nc.vector.memset(colmax[:, :], -BIG))
                norm(0, 0, True)
                norm(0, 1, True)
                finish(0, 0, True)
                finish(0, 1, True)
                with dve.Fori(1, HALF2) as turn:
                    norm(turn, 0, False)
                    norm(turn, 1, False)
                    finish(turn, 0, False)
                    finish(turn, 1, False)
                if table is not None:
                    dve.wait_ge(maxes, NTP)
                    dve.wait_ge(reduced, 1)
                    rows = g.rows[:, :].rearrange("p (t c) -> p t c", c=8)
                    link(nc.vector.tensor_tensor(rows[:, :, 4:8], rows[:, :, 0:4],
                                                 allmax[:, :].unsqueeze(1).to_broadcast([P, NTP, 4]), ALU.add))
                    link(nc.vector.scalar_tensor_tensor(rows[:, :, 4:8], rows[:, :, 4:8], 0.2, rows[:, :, 4:8], ALU.mult, ALU.max))
                    link(nc.vector.tensor_scalar(rows[:, :, 4:8], rows[:, :, 4:8], -HEADROOM, None, ALU.add))


def load_wide(nc, own, tag, pairs, biases=(), bias=None):
    loaded = own.enter_context(semaphore(nc, "wide_loaded" + tag))
    chain = own.enter_context(semaphore(nc, "wide_chain" + tag))
    parts = [own.enter_context(nc.sbuf_tensor(f"wide_part{k}" + tag, [P, b.shape[0]], F32)) for k, b in enumerate(biases)]
    with nc.allow_non_contiguous_dma(reason="columns of weights"), nc.Block() as block:
        @block.sync
        def _(sp):
            for to, of in pairs:
                sp.dma_start(to, of).then_inc(loaded, 16)
            for to, of in zip(parts, biases):
                sp.dma_start(to[:, :], of.rearrange("(o n) -> o n", o=1).to_broadcast([P, of.shape[0]])).then_inc(loaded, 16)
            sp.wait_ge(loaded, 16 * (len(pairs) + len(parts)))

        @block.vector
        def _(dve):
            if bias is not None:
                link = Chain(dve, chain)
                if not parts:
                    nc.vector.memset(bias[:, :], 0.0)
                    return
                dve.wait_ge(loaded, 16 * (len(pairs) + len(parts)))
                link(nc.vector.tensor_copy(bias[:, :], parts[0][:, :]))
                for part in parts[1:]:
                    link(nc.vector.tensor_tensor(bias[:, :], bias[:, :], part[:, :], ALU.add))


def stage_top2(nc, g, comb):
    with stage(nc) as own:
        def sb(name, shape, dt=F32):
            return own.enter_context(nc.sbuf_tensor(name, shape, dt))
        iota8 = sb("iota8", [P, 8])
        back8 = sb("back8", [P, 8])
        eq = sb("eq8", [P, NTP, 8])
        hot = [sb("first8", [P, NTP, 8]), sb("second8", [P, NTP, 8])]
        m = [sb("m_first", [P, NTP]), sb("m_second", [P, NTP])]
        at = sb("at8", [P, NTP])
        chain = own.enter_context(semaphore(nc, "top_chain"))
        dif, exped = own.enter_context(semaphore(nc, "top_dif")), own.enter_context(semaphore(nc, "top_exp"))
        lg = comb[:, :].rearrange("p (t e) -> p t e", e=8)

        def wide(a):
            return a[:, :].unsqueeze(2).to_broadcast([P, NTP, 8])
        with nc.Block() as block:
            @block.vector
            def _(dve):
                link = Chain(dve, chain)
                link(nc.vector.tensor_scalar(back8[:, :], g.iota_row[:, 0:8], -1.0, 8.0, ALU.mult, ALU.add))
                for k in range(2):
                    link(nc.vector.tensor_reduce(m[k][:, :], lg, AX.X, ALU.max))
                    link(nc.vector.tensor_tensor(eq[:, :, :], lg, wide(m[k]), ALU.is_equal))
                    back = back8[:, :].unsqueeze(1).to_broadcast([P, NTP, 8])
                    link(nc.vector.tensor_tensor(eq[:, :, :], eq[:, :, :], back, ALU.mult))
                    link(nc.vector.tensor_reduce(at[:, :], eq[:, :, :], AX.X, ALU.max))
                    link(nc.vector.tensor_tensor(hot[k][:, :, :], eq[:, :, :], wide(at), ALU.is_equal))
                    if k == 0:
                        link(nc.vector.scalar_tensor_tensor(lg, hot[0][:, :, :], -BIG, lg, ALU.mult, ALU.add))
                nc.vector.tensor_tensor(m[1][:, :], m[1][:, :], m[0][:, :], ALU.subtract).then_inc(dif, 1)
                dve.wait_ge(exped, 1)
                link(nc.vector.tensor_scalar(m[0][:, :], m[1][:, :], 1.0, None, ALU.add))
                link(nc.vector.reciprocal(m[0][:, :], m[0][:, :]))
                link(nc.vector.tensor_tensor(m[1][:, :], m[1][:, :], m[0][:, :], ALU.mult))
                link(nc.vector.tensor_tensor(hot[0][:, :, :], hot[0][:, :, :], wide(m[0]), ALU.mult))
                link(nc.vector.tensor_tensor(hot[1][:, :, :], hot[1][:, :, :], wide(m[1]), ALU.mult))
                link(nc.vector.tensor_tensor(lg, hot[0][:, :, :], hot[1][:, :, :], ALU.add))

            @block.scalar
            def _(act):
                act.wait_ge(dif, 1)
                nc.scalar.activation(m[1][:, :], m[1][:, :], ACT.Exp).then_inc(exped, 1)


def stage_softmax8(nc, g, comb):
    with stage(nc) as own:
        m = own.enter_context(nc.sbuf_tensor("m_soft", [P, NTP], F32))
        chain = own.enter_context(semaphore(nc, "soft_chain"))
        dif, exped = own.enter_context(semaphore(nc, "soft_dif")), own.enter_context(semaphore(nc, "soft_exp"))
        lg = comb[:, :].rearrange("p (t e) -> p t e", e=8)
        wide = m[:, :].unsqueeze(2).to_broadcast([P, NTP, 8])
        with nc.Block() as block:
            @block.vector
            def _(dve):
                link = Chain(dve, chain)
                link(nc.vector.tensor_reduce(m[:, :], lg, AX.X, ALU.max))
                nc.vector.tensor_tensor(lg, lg, wide, ALU.subtract).then_inc(dif, 1)
                dve.wait_ge(exped, 1)
                link(nc.vector.tensor_reduce(m[:, :], lg, AX.X, ALU.add))
                link(nc.vector.reciprocal(m[:, :], m[:, :]))
                link(nc.vector.tensor_tensor(lg, lg, wide, ALU.mult))

            @block.scalar
            def _(act):
                act.wait_ge(dif, 1)
                nc.scalar.activation(lg, lg, ACT.Exp).then_inc(exped, 1)


def stage_expert_bias(nc, g, tag, comb, b_out):
    GROUPS = -(-NTP // 16)
    with stage(nc) as own:
        def sb(name, shape, dt=F32):
            return own.enter_context(nc.sbuf_tensor(name + tag, shape, dt))

        def sem(name):
            return own.enter_context(semaphore(nc, name + tag))
        bo = sb("bo", [P, 4, D])
        ct = sb("ct", [P, GROUPS, P])
        ps_t = own.enter_context(nc.psum_tensor("ps_ct" + tag, [P, GROUPS * P], F32))
        ps_b = own.enter_context(nc.psum_tensor("ps_cb" + tag, [P, 4, 512], F32))
        zeroed, loaded, turned, staged, made, added = (
            sem("bo_zero"), sem("bo_in"), sem("c_turned"), sem("c_staged"), sem("cb_made"), sem("cb_added"))
        with nc.Block() as block:
            @block.sync
            def _(sp):
                sp.wait_ge(zeroed, 1)
                for q in range(4):
                    for v in range(4):
                        at = 32 * q + 8 * v
                        sp.dma_start(bo[at:at + 8, v, :], b_out).then_inc(loaded, 16)
                sp.wait_ge(loaded, 256)

            @block.vector
            def _(dve):
                nc.vector.memset(bo[:, :, :], 0.0).then_inc(zeroed, 1)
                for j in range(HALF2):
                    dve.wait_ge(made, j + 1)
                    nc.vector.tensor_tensor(g.x[:, 2 * j:2 * j + 2, :], g.x[:, 2 * j:2 * j + 2, :],
                                            ps_b[:, j % 4, :].rearrange("p (t d) -> p t d", t=2), ALU.add).then_inc(added, 1)

            @block.scalar
            def _(act):
                act.wait_ge(turned, GROUPS)
                nc.scalar.copy(ct[:, 0:GROUPS - 1, :].rearrange("p a b -> p (a b)"), ps_t[:, 0:(GROUPS - 1) * P]).then_inc(staged, 1)
                tail = NTP * 8 - (GROUPS - 1) * P
                nc.scalar.copy(ct[0:tail, GROUPS - 1, :], ps_t[0:tail, (GROUPS - 1) * P:GROUPS * P]).then_inc(staged, 1)

            @block.tensor
            def _(pe):
                for k in range(GROUPS):
                    n = min(P, NTP * 8 - k * P)
                    nc.tensor.transpose(ps_t[0:n, k * P:(k + 1) * P], comb[:, k * P:k * P + n], g.ident[:, :]).then_inc(turned, 1)
                pe.wait_ge(staged, 2)
                pe.wait_ge(loaded, 256)
                for j in range(HALF2):
                    if j >= 4:
                        pe.wait_ge(added, j - 3)
                    for r in range(2):
                        t = 2 * j + r
                        q, v, rows = (t % 16) // 4, t % 4, 32
                        if t // 16 == GROUPS - 1:
                            rows = min(32, NTP * 8 - (GROUPS - 1) * P - 32 * q)
                        last = nc.tensor.matmul(ps_b[:, j % 4, r * D:(r + 1) * D], ct[32 * q:32 * q + rows, t // 16, :],
                                                bo[32 * q:32 * q + rows, v, :], start=True, stop=True)
                    last.then_inc(made, 1)


def stage_moe(nc, g, comb, w1, b1, w2):
    with stage(nc) as own:
        def sb(name, shape, dt=F32):
            return own.enter_context(nc.sbuf_tensor(name, shape, dt))

        def sem(name):
            return own.enter_context(semaphore(nc, name))
        F_ = 4
        w1s = sb("w1s", [P, 2, 2, 512])
        w2s = sb("w2s", [P, 2, F_, D])
        b1s = sb("b1s", [P, EXPERTS * F_])
        b1e = sb("b1e", [P, 2, F_])
        b_own = sem("b1_own")
        ht = sb("ht_moe", [P, F_, SW])
        ps_h = own.enter_context(nc.psum_tensor("ps_hm", [P, 4, 512], F32))
        ps_y = own.enter_context(nc.psum_tensor("ps_ym", [P, 4, 512], F32))
        w_in = [sem("w_even_in"), sem("w_odd_in")]
        b_in, h_made, h_ready, y_made, y_used = sem("b1_in"), sem("hm_made"), sem("hm_ready"), sem("ym_made"), sem("ym_used")
        NH = 2 * F_
        with nc.Block() as block:
            @block.sync
            def _(sp):
                with nc.allow_non_contiguous_dma(reason="bias columns"):
                    sp.dma_start(b1s[:, :], b1.rearrange("e (f p) -> p (e f)", p=P)).then_inc(b_in, 16)
                w1v = w1.rearrange("e (c p) n -> (e c) p n", p=P)
                w2v = w2.rearrange("e (c p) n -> (e c) p n", p=P)

                def load(pair, par):
                    e = pair * 2 + par
                    for c in range(2):
                        sp.dma_start(w1s[:, par, c, :], w1v[ds(e * 2 + c, 1), :, :].rearrange("o p n -> (o p) n")).then_inc(w_in[par], 16)
                    for c in range(F_):
                        sp.dma_start(w2s[:, par, c, :], w2v[ds(e * F_ + c, 1), :, :].rearrange("o p n -> (o p) n")).then_inc(w_in[par], 16)
                load(0, 0)
                load(0, 1)
                with sp.Fori(1, EXPERTS // 2) as pair:
                    for par in range(2):
                        sp.wait_ge(y_made, (pair * 2 + par - 1) * NT)
                        load(pair, par)
                sp.wait_ge(b_in, 16)

            @block.tensor
            def _(pe):
                def step(pair, par, s):
                    q = (pair * 2 + par) * SUPS + s
                    for f in range(F_):
                        for hf in range(2):
                            j = f * 2 + hf
                            pe.wait_ge(h_ready, q * NH + (j + 1))
                            for c in range(2):
                                last = nc.tensor.matmul(ps_h[:, j % 4, 0:HW], w1s[:, par, c, f * P:(f + 1) * P],
                                                        g.xt[:, c, ds(s * SW + hf * HW, HW)], start=(c == 0), stop=(c == 1))
                            last.then_inc(h_made, 1)
                    pe.wait_ge(h_ready, q * NH + (NH + 4))
                    for k in range(SUP):
                        pe.wait_ge(y_used, q * SUP + (k + 1))
                        for f in range(F_):
                            last = nc.tensor.matmul(ps_y[:, k % 4, 0:D], ht[:, f, k * P:(k + 1) * P], w2s[:, par, f, :],
                                                    start=(f == 0), stop=(f == F_ - 1))
                        last.then_inc(y_made, 1)
                with pe.Fori(0, EXPERTS // 2) as pair:
                    for par in range(2):
                        pe.wait_ge(w_in[par], pair * (16 * (2 + F_)) + 16 * (2 + F_))
                        pe.nop(nofuse=True)
                        with pe.Fori(0, SUPS) as s:
                            step(pair, par, s)

            @block.scalar
            def _(act):
                act.sem_inc(h_ready, 4)
                act.wait_ge(b_in, 16)

                def step(pair, par, s, first):
                    q = (pair * 2 + par) * SUPS + s
                    if not first:
                        act.wait_ge(y_made, q * SUP)
                    for f in range(F_):
                        for hf in range(2):
                            j = f * 2 + hf
                            act.wait_ge(h_made, q * NH + (j + 1))
                            nc.scalar.activation(ht[:, f, hf * HW:(hf + 1) * HW], ps_h[:, j % 4, 0:HW], ACT.Relu,
                                                 bias=b1e[:, par, f:f + 1]).then_inc(h_ready, 1)

                def own_bias(pair, par):
                    e = pair * 2 + par
                    nc.scalar.copy(b1e[:, par, :], b1s[:, ds(e * F_, F_)]).then_inc(b_own, 1)
                    act.wait_ge(b_own, e + 1)
                    act.nop(nofuse=True)
                own_bias(0, 0)
                step(0, 0, 0, True)
                with act.Fori(1, SUPS) as s:
                    step(0, 0, s, False)
                own_bias(0, 1)
                with act.Fori(0, SUPS) as s:
                    step(0, 1, s, False)
                with act.Fori(1, EXPERTS // 2) as pair:
                    for par in range(2):
                        own_bias(pair, par)
                        with act.Fori(0, SUPS) as s:
                            step(pair, par, s, False)

            @block.vector
            def _(dve):
                dve.sem_inc(y_used, 3)

                def step(pair, par, s):
                    q = (pair * 2 + par) * SUPS + s
                    for k in range(SUP):
                        dve.wait_ge(y_made, q * SUP + (k + 1))
                        dve.wait_ge(y_used, q * SUP + (k + 2))
                        t = s * SUP + k
                        xr = g.x[:, ds(t, 1), :].rearrange("p t d -> p (t d)")
                        nc.vector.scalar_tensor_tensor(xr, ps_y[:, k % 4, 0:D], comb[:, ds(t * 8 + pair * 2 + par, 1)], xr,
                                                       ALU.mult, ALU.add).then_inc(y_used, 1)
                with dve.Fori(0, EXPERTS // 2) as pair:
                    for par in range(2):
                        with dve.Fori(0, SUPS) as s:
                            step(pair, par, s)


def fill_l1(nc, w, w_t, attn, gamma, beta, wg1, bg1):
    def fill(own, wl, bias):
        def sb(name, shape, dt=F32):
            return own.enter_context(nc.sbuf_tensor(name, shape, dt))

        def sem(name):
            return own.enter_context(semaphore(nc, name))
        wt = sb("wt1", [P, 2, 256])
        a = sb("a1", [P, 2, 8])
        gam = sb("gam1", [P, 2])
        bet = sb("bet1", [P, 2])
        bet_w = sb("bet_wide1", [P, 2, P])
        g1 = sb("g1raw", [P, 2, 64])
        bg = sb("bg1_bc", [P, 64])
        psa = own.enter_context(nc.psum_tensor("ps_a1", [P, 2, 512], F32))
        psb = own.enter_context(nc.psum_tensor("ps_b1", [P, 512], F32))
        zero, loaded, made, biased, wide = sem("a1_zero"), sem("l1_loaded"), sem("a1_made"), sem("b1_made"), sem("bet_spread")
        with nc.allow_non_contiguous_dma(reason="columns of weights"), nc.Block() as block:
            @block.sync
            def _(sp):
                sp.dma_start(wl[:, :, 0:D], w.rearrange("(c p) n -> p c n", p=P)).then_inc(loaded, 16)
                sp.dma_start(wt[:, :, :], w_t.rearrange("(c p) n -> p c n", p=P)).then_inc(loaded, 16)
                sp.dma_start(g1[:, :, :], wg1.rearrange("(c p) n -> p c n", p=P)).then_inc(loaded, 16)
                sp.dma_start(gam[:, :], gamma.rearrange("(c p) -> p c", p=P)).then_inc(loaded, 16)
                sp.dma_start(bet[:, :], beta.rearrange("(c p) -> p c", p=P)).then_inc(loaded, 16)
                sp.dma_start(bg[:, :], bg1.rearrange("(o n) -> o n", o=1).to_broadcast([P, 64])).then_inc(loaded, 16)
                sp.wait_ge(zero, 1)
                for h in range(4):
                    at = 64 * (h % 2)
                    sp.dma_start(a[at:at + 64, h // 2, h:h + 1], attn[h:h + 1, 64:128].rearrange("o d -> d o")).then_inc(loaded, 16)
                    sp.dma_start(a[at:at + 64, h // 2, 4 + h:5 + h], attn[h:h + 1, 0:64].rearrange("o d -> d o")).then_inc(loaded, 16)
                sp.wait_ge(loaded, 16 * 14)

            @block.tensor
            def _(pe):
                pe.wait_ge(loaded, 16 * 14)
                for c in range(2):
                    for j in range(2):
                        last = nc.tensor.matmul(psa[:, c, 0:8], wt[:, j, c * P:(c + 1) * P], a[:, j, :], start=(j == 0), stop=(j == 1))
                    last.then_inc(made, 1)
                pe.wait_ge(wide, 2)
                for c in range(2):
                    last = nc.tensor.matmul(psb[:, 0:64], bet_w[:, c, :], g1[:, c, :], start=(c == 0), stop=(c == 1))
                last.then_inc(biased, 1)

            @block.vector
            def _(dve):
                nc.vector.memset(a[:, :, :], 0.0).then_inc(zero, 1)
                nc.vector.memset(bias[:, 0:264], 0.0)
                dve.wait_ge(loaded, 16 * 14)
                for c in range(2):
                    nc.vector.tensor_copy(bet_w[:, c, :], bet[:, c:c + 1].to_broadcast([P, P])).then_inc(wide, 1)
                    nc.vector.tensor_scalar(wl[:, c, 264:328], g1[:, c, :], gam[:, c:c + 1], None, ALU.mult)
                dve.wait_ge(made, 2)
                nc.vector.tensor_copy(wl[:, :, D:264], psa[:, :, 0:8])
                dve.wait_ge(biased, 1)
                nc.vector.tensor_tensor(bias[:, 264:328], psb[:, 0:64], bg[:, :], ALU.add)
    return fill


def fill_folded(nc, gamma, beta, w, b):
    def fill(own, wl, bias):
        def sb(name, shape, dt=F32):
            return own.enter_context(nc.sbuf_tensor(name, shape, dt))

        def sem(name):
            return own.enter_context(semaphore(nc, name))
        raw = sb("w_raw", [P, 2, D])
        gam = sb("gam_f", [P, 2])
        bet = sb("bet_f", [P, 2])
        bet_w = sb("bet_wide_f", [P, 2, P])
        bb = sb("b_bc_f", [P, D])
        psb = own.enter_context(nc.psum_tensor("ps_bf", [P, 512], F32))
        loaded, biased, wide = sem("f_loaded"), sem("f_biased"), sem("f_spread")
        with nc.allow_non_contiguous_dma(reason="columns of weights"), nc.Block() as block:
            @block.sync
            def _(sp):
                sp.dma_start(raw[:, :, :], w.rearrange("(c p) n -> p c n", p=P)).then_inc(loaded, 16)
                sp.dma_start(gam[:, :], gamma.rearrange("(c p) -> p c", p=P)).then_inc(loaded, 16)
                sp.dma_start(bet[:, :], beta.rearrange("(c p) -> p c", p=P)).then_inc(loaded, 16)
                sp.dma_start(bb[:, :], b.rearrange("(o n) -> o n", o=1).to_broadcast([P, D])).then_inc(loaded, 16)
                sp.wait_ge(loaded, 64)

            @block.tensor
            def _(pe):
                pe.wait_ge(loaded, 64)
                pe.wait_ge(wide, 2)
                for c in range(2):
                    last = nc.tensor.matmul(psb[:, 0:D], bet_w[:, c, :], raw[:, c, :], start=(c == 0), stop=(c == 1))
                last.then_inc(biased, 1)

            @block.vector
            def _(dve):
                dve.wait_ge(loaded, 64)
                for c in range(2):
                    nc.vector.tensor_copy(bet_w[:, c, :], bet[:, c:c + 1].to_broadcast([P, P])).then_inc(wide, 1)
                    nc.vector.tensor_scalar(wl[:, c, :], raw[:, c, :], gam[:, c:c + 1], None, ALU.mult)
                dve.wait_ge(biased, 1)
                nc.vector.tensor_tensor(bias[:, :], psb[:, 0:D], bb[:, :], ALU.add)
    return fill


def stage_second_norm(nc, g, rstd2):
    with stage(nc) as own:
        chain, rooted = own.enter_context(semaphore(nc, "n2_chain")), own.enter_context(semaphore(nc, "n2_root"))
        with nc.Block() as block:
            @block.vector
            def _(dve):
                link = Chain(dve, chain)
                link(nc.vector.tensor_tensor(rstd2[:, :], g.rstd[:, :], g.rstd[:, :], ALU.mult))
                link(nc.vector.tensor_tensor(rstd2[:, :], rstd2[:, :], g.var[:, :], ALU.mult))
                link(nc.vector.tensor_scalar(rstd2[:, :], rstd2[:, :], 1e-5, None, ALU.add))
                dve.wait_ge(rooted, 1)
                link(nc.vector.reciprocal(rstd2[:, :], rstd2[:, :]))

            @block.scalar
            def _(act):
                act.wait_ge(chain, 3)
                nc.scalar.activation(rstd2[:, :], rstd2[:, :], ACT.Sqrt).then_inc(rooted, 1)


def stage_l1_mix(nc, g, hg, w_qkv, wq_t, w_proj, b_proj, wg2, bg2):
    FT_ = 512
    FULL = N // FT_
    REST = N - FULL * FT_
    with ExitStack() as mid:
        def sbm(name, shape, dt=F32):
            return mid.enter_context(nc.sbuf_tensor(name, shape, dt))
        wkv = sbm("wkv", [P, 2, 512])
        wqt = sbm("wqt", [P, 2, D])
        wp = sbm("wp", [P, 2, D])
        wg = sbm("wg2", [65, D])
        bp = sbm("bp", [P, D])
        kbc = sbm("kbc", [P, D])
        wqc = sbm("wqc", [P, 2, D])
        with stage(nc) as own:
            def sb(name, shape, dt=F32):
                return own.enter_context(nc.sbuf_tensor(name, shape, dt))

            def sem(name):
                return own.enter_context(semaphore(nc, name))
            km = sb("km", [P, 2, FULL + 1])
            kcol = sb("kcol", [P, 2])
            kwide = sb("kwide", [P, 2, P])
            pst = own.enter_context(nc.psum_tensor("ps_k", [P, 4, 512], F32))
            psb = own.enter_context(nc.psum_tensor("ps_kb", [P, 512], F32))
            loaded, made, seen, wide, spread = sem("mix_loaded"), sem("k_made"), sem("k_seen"), sem("k_wide"), sem("k_spread")
            chain, gelued = sem("k_chain"), sem("gelued")
            with nc.allow_non_contiguous_dma(reason="row of bias"), nc.Block() as block:
                @block.sync
                def _(sp):
                    sp.dma_start(wkv[:, :, :], w_qkv[:, D:3 * D].rearrange("(c p) n -> p c n", p=P)).then_inc(loaded, 16)
                    sp.dma_start(wqt[:, :, :], wq_t.rearrange("(c p) n -> p c n", p=P)).then_inc(loaded, 16)
                    sp.dma_start(wp[:, :, :], w_proj.rearrange("(c p) n -> p c n", p=P)).then_inc(loaded, 16)
                    sp.dma_start(wg[0:64, :], wg2).then_inc(loaded, 16)
                    sp.dma_start(wg[64:65, :], bg2.rearrange("(o n) -> o n", o=1)).then_inc(loaded, 16)
                    sp.dma_start(bp[:, :], b_proj.rearrange("(o n) -> o n", o=1).to_broadcast([P, D])).then_inc(loaded, 16)
                    sp.wait_ge(loaded, 96)

                @block.scalar
                def _(act):
                    nc.scalar.activation(hg[:, :], hg[:, :], ACT.Gelu)

                @block.tensor
                def _(pe):
                    pe.wait_ge(loaded, 96)

                    def tile(turn, width, first):
                        for m in range(2):
                            if not first:
                                pe.wait_ge(seen, turn * 2 + (m - 1))
                            for c in range(2):
                                last = nc.tensor.matmul(pst[:, m, 0:width], wkv[:, c, m * P:(m + 1) * P],
                                                        g.xt[:, c, ds(turn * FT_, width)], start=(c == 0), stop=(c == 1))
                            last.then_inc(made, 1)
                    tile(0, FT_, True)
                    with pe.Fori(1, FULL) as turn:
                        tile(turn, FT_, False)
                    tile(FULL, REST, False)
                    pe.wait_ge(wide, 2)
                    for m in range(2):
                        last = nc.tensor.matmul(psb[:, m * P:(m + 1) * P], kwide[:, m, :], g.ident[:, :], start=True, stop=True)
                    last.then_inc(spread, 1)

                @block.vector
                def _(dve):
                    def peak(turn, width):
                        for m in range(2):
                            dve.wait_ge(made, turn * 2 + (m + 1))
                            nc.vector.tensor_reduce(km[:, m, ds(turn, 1)], pst[:, m, 0:width], AX.X, ALU.max).then_inc(seen, 1)
                    with dve.Fori(0, FULL) as turn:
                        peak(turn, FT_)
                    peak(FULL, REST)
                    dve.wait_ge(seen, 2 * FULL + 2)
                    link = Chain(dve, chain)
                    link(nc.vector.tensor_reduce(kcol[:, :], km[:, :, :], AX.X, ALU.max))
                    for m in range(2):
                        nc.vector.tensor_copy(kwide[:, m, :], kcol[:, m:m + 1].to_broadcast([P, P])).then_inc(wide, 1)
                    dve.wait_ge(loaded, 96)
                    nc.vector.tensor_tensor(g.x[:, :, :], g.x[:, :, :], bp[:, :].unsqueeze(1).to_broadcast([P, NTP, D]), ALU.add)
                    dve.wait_ge(spread, 1)
                    nc.vector.tensor_copy(kbc[:, :], psb[:, 0:D])
        with stage(nc) as own:
            def sb(name, shape, dt=F32):
                return own.enter_context(nc.sbuf_tensor(name, shape, dt))

            def sem(name):
                return own.enter_context(semaphore(nc, name))
            st = sb("st_c", [P, 2, 2, P])
            kd = sb("kd", [P, 2, D])
            ke = sb("ke", [P, 2, D])
            vv = sb("vv", [P, 2, 2, P + 1])
            mask = sb("head_mask", [P, P])
            rk = sb("rk", [P, 2])
            cx = sb("cx", [P, 2, P])
            ps_kv = own.enter_context(nc.psum_tensor("ps_kv", [P, 2, 512], F32))
            ps_c = own.enter_context(nc.psum_tensor("ps_ctx", [P, 2, 512], F32))
            ps_w = own.enter_context(nc.psum_tensor("ps_wqc", [P, 2, 512], F32))
            staged, made, kd_ready, ke_ready, vv_ready, used = sem("c_staged"), sem("kv_made"), sem("kd_ready"), sem("ke_ready"), sem("vv_ready"), sem("kv_used")
            masked, chain, cxs, wqcs = sem("masked"), sem("cx_chain"), sem("cx_ready"), sem("wqc_made")
            TURNS = (NT - 1) // 2
            with nc.Block() as block:
                @block.gpsimd
                def _(pool):
                    nc.gpsimd.memset(vv[:, :, :, P:P + 1], 1.0).then_inc(masked, 1)
                    pool.wait_ge(masked, 1)

                    def stage(i, r, first):
                        if not first:
                            pool.wait_ge(made, i - 1)
                        nc.gpsimd.tensor_copy(st[:, r, :, :], g.xt[:, :, ds(i * P, P)]).then_inc(staged, 1)
                    stage(0, 0, True)
                    stage(1, 1, True)
                    with pool.Fori(1, TURNS) as turn:
                        stage(turn * 2, 0, False)
                        stage(turn * 2 + 1, 1, False)
                    stage(NT - 1, 0, False)

                @block.tensor
                def _(pe):
                    def keys(i, r, first):
                        pe.wait_ge(staged, i + 1)
                        if not first:
                            pe.wait_ge(vv_ready, i - 1)
                            pe.wait_ge(kd_ready, i - 1)
                        for c in range(2):
                            last = nc.tensor.matmul(ps_kv[:, r, :], st[:, r, c, :], wkv[:, c, :], start=(c == 0), stop=(c == 1))
                        last.then_inc(made, 1)

                    def context(i, r, first, last_one):
                        pe.wait_ge(ke_ready, i + 1)
                        pe.wait_ge(vv_ready, i + 1)
                        n = LAST if last_one else P
                        for m in range(2):
                            last = nc.tensor.matmul(ps_c[:, m, 0:P + 1], ke[0:n, r, m * P:(m + 1) * P], vv[0:n, r, m, :],
                                                    start=first, stop=last_one)
                        last.then_inc(used, 1)
                    keys(0, 0, True)
                    keys(1, 1, True)
                    context(0, 0, True, False)
                    context(1, 1, False, False)
                    with pe.Fori(1, TURNS) as turn:
                        keys(turn * 2, 0, False)
                        keys(turn * 2 + 1, 1, False)
                        context(turn * 2, 0, False, False)
                        context(turn * 2 + 1, 1, False, False)
                    keys(NT - 1, 0, False)
                    context(NT - 1, 0, False, True)
                    pe.wait_ge(cxs, 2)
                    for c in range(2):
                        for m in range(2):
                            nc.tensor.matmul(ps_w[:, c, m * P:(m + 1) * P], wqt[:, m, c * P:(c + 1) * P], cx[:, m, :],
                                             start=True, stop=True).then_inc(wqcs, 1)

                @block.scalar
                def _(act):
                    def step(i, r, first):
                        act.wait_ge(kd_ready, i + 1)
                        if not first:
                            act.wait_ge(used, i - 1)
                        nc.scalar.activation(ke[:, r, :], kd[:, r, :], ACT.Exp).then_inc(ke_ready, 1)
                    step(0, 0, True)
                    step(1, 1, True)
                    with act.Fori(1, TURNS) as turn:
                        step(turn * 2, 0, False)
                        step(turn * 2 + 1, 1, False)
                    step(NT - 1, 0, False)

                @block.vector
                def _(dve):
                    def step(i, r, first):
                        dve.wait_ge(made, i + 1)
                        if not first:
                            dve.wait_ge(ke_ready, i - 1)
                        nc.vector.tensor_tensor(kd[:, r, :], ps_kv[:, r, 0:D], kbc[:, :], ALU.subtract).then_inc(kd_ready, 1)
                        if not first:
                            dve.wait_ge(used, i - 1)
                        nc.vector.tensor_copy(vv[:, r, :, 0:P], ps_kv[:, r, D:2 * D].rearrange("p (m n) -> p m n", m=2)).then_inc(vv_ready, 1)
                    link = Chain(dve, chain)
                    dve.wait_ge(masked, 1)
                    link(nc.vector.memset(mask[:, :], 0.0))
                    for q in range(4):
                        link(nc.vector.memset(mask[32 * q:32 * q + 32, 32 * q:32 * q + 32], 1.0))
                    step(0, 0, True)
                    step(1, 1, True)
                    with dve.Fori(1, TURNS) as turn:
                        step(turn * 2, 0, False)
                        step(turn * 2 + 1, 1, False)
                    step(NT - 1, 0, False)
                    dve.wait_ge(used, NT)
                    link(nc.vector.reciprocal(rk[:, :], ps_c[:, :, P]))
                    for m in range(2):
                        nc.vector.scalar_tensor_tensor(cx[:, m, :], ps_c[:, m, 0:P], rk[:, m:m + 1], mask[:, :], ALU.mult, ALU.mult).then_inc(cxs, 1)
                    dve.wait_ge(wqcs, 4)
                    nc.vector.tensor_copy(wqc[:, :, :], ps_w[:, :, 0:D])
        with stage(nc) as own:
            def sb(name, shape, dt=F32):
                return own.enter_context(nc.sbuf_tensor(name, shape, dt))

            def sem(name):
                return own.enter_context(semaphore(nc, name))
            st = sb("st_o", [P, 2, 2, P])
            hs = sb("hs_o", [P, 2, P])
            ht = sb("ht_o", [65, 2, P])
            gate = sb("gate", [P, 2, D])
            og = sb("og", [P, 2, D])
            ogt = sb("ogt", [P, 2, D])
            ps_o = own.enter_context(nc.psum_tensor("ps_out", [P, 512], F32))
            ps_t = own.enter_context(nc.psum_tensor("ps_ht", [P, 512], F32))
            ps_g = own.enter_context(nc.psum_tensor("ps_gate", [P, 2, 512], F32))
            ps_r = own.enter_context(nc.psum_tensor("ps_ogt", [P, 2, 512], F32))
            ps_p = own.enter_context(nc.psum_tensor("ps_proj", [P, 2, 512], F32))
            staged, ht_made, ht_ready, out_made, gate_made, gate_ready = sem("o_staged"), sem("ht_made"), sem("ht_ready"), sem("out_made"), sem("gate_made"), sem("gate_ready")
            og_ready, og_turned, ogt_ready, proj, added, ones = sem("og_ready"), sem("og_turned"), sem("ogt_ready"), sem("proj_made"), sem("proj_added"), sem("ones_row")
            with nc.Block() as block:
                @block.gpsimd
                def _(pool):
                    def stage(turn, r, first):
                        i = turn * 2 + r
                        if not first:
                            pool.wait_ge(gate_made, i - 1)
                        nc.gpsimd.tensor_copy(hs[:, r, 0:64], hg[:, ds(i * 64, 64)])
                        nc.gpsimd.tensor_copy(st[:, r, :, :], g.xt[:, :, ds(i * P, P)]).then_inc(staged, 1)
                    nc.gpsimd.memset(hs[:, :, 64:P], 0.0).then_inc(ones, 1)
                    stage(0, 0, True)
                    stage(0, 1, True)
                    with pool.Fori(1, HALF2) as turn:
                        stage(turn, 0, False)
                        stage(turn, 1, False)

                @block.tensor
                def _(pe):
                    def front(turn, r, first):
                        i = turn * 2 + r
                        pe.wait_ge(staged, i + 1)
                        if not (first and r == 0):
                            pe.wait_ge(ht_ready, i)
                        nc.tensor.transpose(ps_t[:, 0:P], hs[:, r, :], g.ident[:, :]).then_inc(ht_made, 1)
                        if not (first and r == 0):
                            pe.wait_ge(og_ready, i)
                        for c in range(2):
                            last = nc.tensor.matmul(ps_o[:, 0:D], st[:, r, c, :], wqc[:, c, :], start=(c == 0), stop=(c == 1))
                        last.then_inc(out_made, 1)
                        pe.wait_ge(ht_ready, i + 1)
                        if not first:
                            pe.wait_ge(gate_ready, i - 1)
                        nc.tensor.matmul(ps_g[:, r, 0:D], ht[:, r, :], wg[:, :], start=True, stop=True).then_inc(gate_made, 1)

                    def back(turn, r, first):
                        i = turn * 2 + r
                        pe.wait_ge(og_ready, i + 1)
                        if not first:
                            pe.wait_ge(ogt_ready, i - 1)
                        for c in range(2):
                            last = nc.tensor.transpose(ps_r[:, r, c * P:(c + 1) * P], og[:, r, c * P:(c + 1) * P], g.ident[:, :])
                        last.then_inc(og_turned, 1)
                        pe.wait_ge(ogt_ready, i + 1)
                        if not first:
                            pe.wait_ge(added, i - 1)
                        for c in range(2):
                            last = nc.tensor.matmul(ps_p[:, r, 0:D], ogt[:, r, c * P:(c + 1) * P], wp[:, c, :], start=(c == 0), stop=(c == 1))
                        last.then_inc(proj, 1)

                    def both(turn, first):
                        front(turn, 0, first)
                        front(turn, 1, first)
                        back(turn, 0, first)
                        back(turn, 1, first)
                    pe.wait_ge(ones, 2)
                    both(0, True)
                    with pe.Fori(1, HALF2) as turn:
                        both(turn, False)

                @block.scalar
                def _(act):
                    def front(turn, r, first):
                        i = turn * 2 + r
                        act.wait_ge(ht_made, i + 1)
                        if not first:
                            act.wait_ge(gate_made, i - 1)
                        nc.scalar.copy(ht[0:64, r, :], ps_t[0:64, 0:P]).then_inc(ht_ready, 1)
                        act.wait_ge(gate_made, i + 1)
                        if not first:
                            act.wait_ge(og_ready, i - 1)
                        nc.scalar.activation(gate[:, r, :], ps_g[:, r, 0:D], ACT.Sigmoid).then_inc(gate_ready, 1)

                    def back(turn, r, first):
                        i = turn * 2 + r
                        act.wait_ge(og_turned, i + 1)
                        if not first:
                            act.wait_ge(proj, i - 1)
                        nc.scalar.copy(ogt[:, r, :], ps_r[:, r, 0:D]).then_inc(ogt_ready, 1)

                    def both(turn, first):
                        front(turn, 0, first)
                        front(turn, 1, first)
                        back(turn, 0, first)
                        back(turn, 1, first)
                    both(0, True)
                    with act.Fori(1, HALF2) as turn:
                        both(turn, False)

                @block.vector
                def _(dve):
                    nc.vector.memset(ht[64:65, :, :], 1.0).then_inc(ones, 1)

                    def both(turn, first):
                        for r in range(2):
                            i = turn * 2 + r
                            dve.wait_ge(gate_ready, i + 1)
                            dve.wait_ge(out_made, i + 1)
                            if not first:
                                dve.wait_ge(og_turned, i - 1)
                            nc.vector.tensor_tensor(og[:, r, :], ps_o[:, 0:D], gate[:, r, :], ALU.mult).then_inc(og_ready, 1)
                        for r in range(2):
                            i = turn * 2 + r
                            dve.wait_ge(proj, i + 1)
                            xr = g.x[:, ds(i, 1), :].rearrange("p t d -> p (t d)")
                            nc.vector.tensor_tensor(xr, xr, ps_p[:, r, 0:D], ALU.add).then_inc(added, 1)
                    both(0, True)
                    with dve.Fori(1, HALF2) as turn:
                        both(turn, False)


def stage_l1_messages(nc, g, acc, top, table):
    with stage(nc) as own:
        def sb(name, shape, dt=F32):
            return own.enter_context(nc.sbuf_tensor(name, shape, dt))

        def sem(name):
            return own.enter_context(semaphore(nc, name))
        gm = sb("gm", [P, 4])
        ga = sb("ga", [P, 4])
        ex = sb("ex", [P, NT, 4])
        wh = sb("wh", [P, 2, SUP, D])
        a3 = acc[:, :].rearrange("p (t w) -> p t w", w=AW)
        rows = g.rows[:, :].rearrange("p (t c) -> p t c", c=8)
        chain, peak, reduced, low, exped = sem("l1m_chain"), sem("peak"), sem("peak_all"), sem("ex_in"), sem("ex_out")
        wh_in, wh_used = [sem("wh_in0"), sem("wh_in1")], sem("wh_used")
        with nc.Block() as block:
            @block.sync
            def _(sp):
                for s in range(SUPS):
                    if s >= 2:
                        sp.wait_ge(wh_used, s - 1)
                    sp.dma_start(wh[:, s % 2, :, :], table[s * SW:(s + 1) * SW, 0:D].rearrange("(t p) d -> p t d", p=P)).then_inc(wh_in[s % 2], 16)

            @block.gpsimd
            def _(pool):
                pool.wait_ge(peak, 1)
                nc.gpsimd.partition_all_reduce(ga[:, :], gm[:, :], P, bass.bass_isa.ReduceOp.max).then_inc(reduced, 1)

            @block.scalar
            def _(act):
                act.wait_ge(low, 1)
                nc.scalar.activation(ex[:, :, :], ex[:, :, :], ACT.Exp).then_inc(exped, 1)

            @block.vector
            def _(dve):
                link = Chain(dve, chain)
                nc.vector.tensor_reduce(gm[:, :], top[:, :, :].rearrange("p k h -> p h k"), AX.X, ALU.max).then_inc(peak, 1)
                dve.wait_ge(reduced, 1)
                link(nc.vector.scalar_tensor_tensor(ga[:, :], ga[:, :], 0.2, ga[:, :], ALU.mult, ALU.max))
                link(nc.vector.tensor_tensor(ex[:, :, :], ga[:, :].unsqueeze(1).to_broadcast([P, NT, 4]), rows[:, 0:NT, 4:8], ALU.subtract))
                nc.vector.tensor_scalar(ex[:, :, :], ex[:, :, :], math.log(1e-15), 88.0, ALU.add, ALU.min).then_inc(low, 1)
                dve.wait_ge(exped, 1)
                link(nc.vector.tensor_tensor(ex[:, :, :], ex[:, :, :], a3[:, 0:NT, 256:AW], ALU.add))
                link(nc.vector.tensor_scalar(ex[:, :, :], ex[:, :, :], 1e-37, None, ALU.max))
                link(nc.vector.reciprocal(ex[:, :, :], ex[:, :, :]))
                for s in range(SUPS):
                    t = slice(s * SUP, (s + 1) * SUP)
                    part = a3[:, t, 0:256].rearrange("p t (h d) -> p t h d", h=4)
                    link(nc.vector.tensor_tensor(part, part, ex[:, t, :].unsqueeze(3).to_broadcast([P, SUP, 4, 64]), ALU.mult))
                    dve.wait_ge(wh_in[s % 2], 16 * (s // 2 + 1))
                    nc.vector.tensor_tensor(a3[:, t, 0:256], a3[:, t, 0:256], wh[:, s % 2, :, :], ALU.add).then_inc(wh_used, 1)


def stage_ffn(nc, g, comb, w1, w2, wo, bn1, bn2):
    EPS = 0.001
    with stage(nc) as own:
        def sb(name, shape, dt=F32):
            return own.enter_context(nc.sbuf_tensor(name, shape, dt))

        def sem(name):
            return own.enter_context(semaphore(nc, name))
        NC_ = EXPERTS * 2
        ws = sb("ws_f", [P, 2, 3, 2, D])
        par_in = sb("par_in", [P, 2, 5, NC_])
        scale = sb("scale_f", [P, 2, NC_])
        shift = sb("shift_f", [P, 2, NC_])
        own_s = sb("own_scale", [P, 2, 2, 2, 2])
        h1 = sb("h1t", [P, 2, SW])
        h2 = sb("h2t", [P, 2, SW])
        ps_h = own.enter_context(nc.psum_tensor("ps_hf", [P, 4, 512], F32))
        ps_y = own.enter_context(nc.psum_tensor("ps_yf", [P, 4, 512], F32))
        w_in = [sem("wf_even_in"), sem("wf_odd_in")]
        p_in, root, ready, chain = sem("bn_in"), sem("bnf_root"), sem("bnf_ready"), sem("bnf_chain")
        h_made, h_ready, y_made, y_used, o_own = sem("hf_made"), sem("hf_ready"), sem("yf_made"), sem("yf_used"), sem("own_ready")
        with nc.Block() as block:
            @block.sync
            def _(sp):
                with nc.allow_non_contiguous_dma(reason="channel columns"):
                    for layer, arrays in enumerate((bn1, bn2)):
                        for k, a in enumerate(arrays):
                            sp.dma_start(par_in[:, layer, k, :], a.rearrange("e (f p) -> p (e f)", p=P)).then_inc(p_in, 16)
                views = [w.rearrange("e (c p) n -> (e c) p n", p=P) for w in (w1, w2, wo)]

                def load(pair, par):
                    for k in range(3):
                        for c in range(2):
                            sp.dma_start(ws[:, par, k, c, :], views[k][ds((pair * 2 + par) * 2 + c, 1), :, :].rearrange("o p n -> (o p) n"))\
                              .then_inc(w_in[par], 16)
                load(0, 0)
                load(0, 1)
                with sp.Fori(1, EXPERTS // 2) as pair:
                    for par in range(2):
                        sp.wait_ge(y_made, (pair * 2 + par - 1) * NT)
                        load(pair, par)

            @block.tensor
            def _(pe):
                def layer(q, l, par, rhs):
                    for f in range(2):
                        for hf in range(2):
                            j = f * 2 + hf
                            pe.wait_ge(h_ready, q * 8 + (l * 4 + j + 1))
                            for c in range(2):
                                last = nc.tensor.matmul(ps_h[:, j, 0:HW], ws[:, par, l, c, f * P:(f + 1) * P], rhs(c, hf),
                                                        start=(c == 0), stop=(c == 1))
                            last.then_inc(h_made, 1)

                def step(pair, par, s):
                    q = (pair * 2 + par) * SUPS + s
                    layer(q, 0, par, lambda c, hf: g.xt[:, c, ds(s * SW + hf * HW, HW)])
                    pe.wait_ge(h_ready, q * 8 + 8)
                    layer(q, 1, par, lambda c, hf: h1[:, c, hf * HW:(hf + 1) * HW])
                    pe.wait_ge(h_ready, q * 8 + 12)
                    for k in range(SUP):
                        pe.wait_ge(y_used, q * SUP + (k + 1))
                        for c in range(2):
                            last = nc.tensor.matmul(ps_y[:, k % 4, 0:D], h2[:, c, k * P:(k + 1) * P], ws[:, par, 2, c, :],
                                                    start=(c == 0), stop=(c == 1))
                        last.then_inc(y_made, 1)
                with pe.Fori(0, EXPERTS // 2) as pair:
                    for par in range(2):
                        pe.wait_ge(w_in[par], pair * 96 + 96)
                        pe.nop(nofuse=True)
                        with pe.Fori(0, SUPS) as s:
                            step(pair, par, s)

            @block.scalar
            def _(act):
                act.wait_ge(chain, 1)
                nc.scalar.activation(scale[:, :, :], scale[:, :, :], ACT.Sqrt).then_inc(root, 1)
                act.sem_inc(h_ready, 4)
                act.wait_ge(ready, 2)

                def step(pair, par, s, first):
                    q = (pair * 2 + par) * SUPS + s
                    for l, h in enumerate((h1, h2)):
                        if l == 1 and not first:
                            act.wait_ge(y_made, q * SUP)
                        for f in range(2):
                            for hf in range(2):
                                j = f * 2 + hf
                                act.wait_ge(h_made, q * 8 + (l * 4 + j + 1))
                                nc.scalar.activation(h[:, f, hf * HW:(hf + 1) * HW], ps_h[:, j, 0:HW], ACT.Relu,
                                                     bias=own_s[:, par, 1, l, f:f + 1], scale=own_s[:, par, 0, l, f:f + 1])\
                                  .then_inc(h_ready, 1)

                def own_columns(pair, par):
                    e = pair * 2 + par
                    nc.scalar.copy(own_s[:, par, 0, :, :], scale[:, :, ds(e * 2, 2)]).then_inc(o_own, 1)
                    nc.scalar.copy(own_s[:, par, 1, :, :], shift[:, :, ds(e * 2, 2)]).then_inc(o_own, 1)
                    act.wait_ge(o_own, e * 2 + 2)
                    act.nop(nofuse=True)
                own_columns(0, 0)
                step(0, 0, 0, True)
                with act.Fori(1, SUPS) as s:
                    step(0, 0, s, False)
                own_columns(0, 1)
                with act.Fori(0, SUPS) as s:
                    step(0, 1, s, False)
                with act.Fori(1, EXPERTS // 2) as pair:
                    for par in range(2):
                        own_columns(pair, par)
                        with act.Fori(0, SUPS) as s:
                            step(pair, par, s, False)

            @block.vector
            def _(dve):
                dve.wait_ge(p_in, 160)
                link = Chain(dve, chain)
                link(nc.vector.tensor_scalar(scale[:, :, :], par_in[:, :, 4, :], EPS, None, ALU.add))
                dve.wait_ge(root, 1)
                link(nc.vector.reciprocal(scale[:, :, :], scale[:, :, :]))
                link(nc.vector.tensor_tensor(scale[:, :, :], scale[:, :, :], par_in[:, :, 1, :], ALU.mult))
                dve.sem_inc(ready, 1)
                link(nc.vector.tensor_tensor(shift[:, :, :], par_in[:, :, 0, :], par_in[:, :, 3, :], ALU.subtract))
                link(nc.vector.tensor_tensor(shift[:, :, :], shift[:, :, :], scale[:, :, :], ALU.mult))
                nc.vector.tensor_tensor(shift[:, :, :], shift[:, :, :], par_in[:, :, 2, :], ALU.add).then_inc(ready, 1)
                dve.sem_inc(y_used, 3)

                def step(pair, par, s):
                    q = (pair * 2 + par) * SUPS + s
                    for k in range(SUP):
                        dve.wait_ge(y_made, q * SUP + (k + 1))
                        dve.wait_ge(y_used, q * SUP + (k + 2))
                        t = s * SUP + k
                        xr = g.x[:, ds(t, 1), :].rearrange("p t d -> p (t d)")
                        nc.vector.scalar_tensor_tensor(xr, ps_y[:, k % 4, 0:D], comb[:, ds(t * 8 + pair * 2 + par, 1)], xr,
                                                       ALU.mult, ALU.add).then_inc(y_used, 1)
                with dve.Fori(0, EXPERTS // 2) as pair:
                    for par in range(2):
                        with dve.Fori(0, SUPS) as s:
                            step(pair, par, s)


def build_all(nc, A, out):
    edge_list = nc.dram_tensor("edge_list", [TILES * P, 2], I32).ap()
    table0 = nc.dram_tensor("table0", [NPAD, 68], F32).ap()
    table1 = nc.dram_tensor("table1", [NPAD, AW], F32).ap()
    with ExitStack() as ctx:
        g = Space()
        stage_constants(nc, g, ctx)
        g.rows = ctx.enter_context(nc.sbuf_tensor("rows", [P, NTP * 8], F32))
        g.top = ctx.enter_context(nc.sbuf_tensor("top", [P, KT, 4], F32))
        stage_load(nc, g, A["x"], ctx)
        with stage(nc) as own:
            stage_places(nc, g, A["src"], A["dst"], ctx, own, edge_list)
            g.xt = own.enter_context(nc.sbuf_tensor("xt0", [P, 2, NPAD], F32))
            stage_ln_stats(nc, g, "_0")
            stage_l0_gnn_table(nc, g, A["L0_gnn_W"], A["L0_gnn_W_t"], A["L0_gnn_b"], A["L0_gnn_a_src_t"], A["L0_gnn_a_dst_t"], table0)
            stage_l0_mix(nc, g, A["L0_mix_w_qkv_t"], A["L0_mix_bn_gamma"], A["L0_mix_bn_beta"], A["L0_mix_w_dw_mid"], A["L0_mix_w_pw_t"],
                         A["L0_mix_w_res_t"], A["L0_mix_b_res"])
            stage_list(nc, g, SCATTERS["ball"][1])
        with ExitStack() as own:
            acc = own.enter_context(nc.sbuf_tensor("acc0", [P, NTP * AW], F32))
            stage_aggregate(nc, g, "_0", table0, 68, True, g.rows, acc, g.top)
            stage_add_messages(nc, g, acc, "_0")
        with ExitStack() as own:
            g.xt = own.enter_context(nc.sbuf_tensor("xt1", [P, 2, NPAD], F32))
            comb = own.enter_context(nc.sbuf_tensor("comb0", [P, NTP * 8], F32))
            stage_ln_stats(nc, g, "_1")

            def fill(own, wl, bias):
                load_wide(nc, own, "_1", [(wl[:, :, :], A["L0_ffn_Wg"].rearrange("(c p) n -> p c n", p=P))],
                          [A["L0_ffn_bg"], A["L0_ffn_bias"]], bias)
            stage_turn(nc, g, "_1", fill, 8, out=comb)
            stage_top2(nc, g, comb)
            stage_expert_bias(nc, g, "_1", comb, A["L0_ffn_b2"])
            stage_moe(nc, g, comb, A["L0_ffn_W1"], A["L0_ffn_b1"], A["L0_ffn_W2"])
        with ExitStack() as own:
            g.xt = own.enter_context(nc.sbuf_tensor("xt2", [P, 2, NPAD], F32))
            hg = own.enter_context(nc.sbuf_tensor("hg", [P, NTP * 64], F32))
            rstd2 = own.enter_context(nc.sbuf_tensor("rstd2", [P, NTP], F32))
            stage_ln_stats(nc, g, "_2")
            stage_second_norm(nc, g, rstd2)
            stage_turn(nc, g, "_2", fill_l1(nc, A["L1_gnn_W"], A["L1_gnn_W_t"], A["L1_gnn_attn_fc"], A["L1_mix_ln_g"], A["L1_mix_ln_b"],
                                            A["L1_mix_Wg1"], A["L1_mix_bg1"]), 328, table=table1, gate=(hg, rstd2))
            stage_l1_mix(nc, g, hg, A["L1_mix_Wqkv"], A["L1_mix_Wq_t"], A["L1_mix_Wproj"], A["L1_mix_bproj"], A["L1_mix_Wg2"], A["L1_mix_bg2"])
        with ExitStack() as own:
            acc = own.enter_context(nc.sbuf_tensor("acc1", [P, NTP * AW], F32))

            def new_row(i):
                return acc[:, ds(i * AW, D)]
            stage_aggregate(nc, g, "_1", table1, AW, False, g.rows, acc, g.top)
            stage_l1_messages(nc, g, acc, g.top, table1)
            stage_ln_stats(nc, g, "_3", source=new_row)
            stage_turn(nc, g, "_3", fill_folded(nc, A["L1_gnn_ln_gamma"], A["L1_gnn_ln_beta"], A["L1_gnn_ffn_w"], A["L1_gnn_ffn_b"]), D,
                       source=new_row, keep_xt=False)
        with ExitStack() as own:
            g.xt = own.enter_context(nc.sbuf_tensor("xt3", [P, 2, NPAD], F32))
            comb = own.enter_context(nc.sbuf_tensor("comb1", [P, NTP * 8], F32))
            stage_ln_stats(nc, g, "_4")

            def fill(own, wl, bias):
                load_wide(nc, own, "_4", [(wl[:, :, :], A["L1_ffn_Wr"].rearrange("(c p) n -> p c n", p=P))], [A["L1_ffn_br"]], bias)
            stage_turn(nc, g, "_4", fill, 8, out=comb)
            stage_softmax8(nc, g, comb)
            stage_expert_bias(nc, g, "_4", comb, A["L1_ffn_bo"])
            stage_ffn(nc, g, comb, A["L1_ffn_W1"], A["L1_ffn_W2"], A["L1_ffn_Wo"],
                      [A["L1_ffn_" + k] for k in ("b1", "g1", "be1", "m1", "v1")],
                      [A["L1_ffn_" + k] for k in ("b2", "g2", "be2", "m2", "v2")])
        saved = ctx.enter_context(semaphore(nc, "saved"))
        with nc.Block() as block:
            @block.sync
            def _(sp):
                sp.dma_start(out[0:(NT - 1) * P, :].rearrange("(t p) d -> p t d", p=P), g.x[:, 0:NT - 1, :]).then_inc(saved, 16)
                sp.dma_start(out[(NT - 1) * P:N, :], g.x[0:LAST, NT - 1, :]).then_inc(saved, 16)
                sp.wait_ge(saved, 32)


def kernel(**inputs):
    import numpy as _np
    import concourse.bacc as _bacc
    from concourse import mybir as _mybir
    from concourse.bass_utils import run_bass_kernel_spmd as _run

    laid = {name: a for name, a in inputs.items()
            if name not in ("L0_mix_w_qkv", "L0_mix_w_dw", "L0_mix_w_pw", "L0_mix_w_res", "L0_gnn_a_src", "L0_gnn_a_dst")}
    laid["L0_gnn_W_t"] = _np.asarray(inputs["L0_gnn_W"]).T
    laid["L0_gnn_a_src_t"] = _np.asarray(inputs["L0_gnn_a_src"]).T
    laid["L0_gnn_a_dst_t"] = _np.asarray(inputs["L0_gnn_a_dst"]).T
    laid["L0_mix_w_qkv_t"] = _np.asarray(inputs["L0_mix_w_qkv"])[:, :, 2].T
    laid["L0_mix_w_dw_mid"] = _np.asarray(inputs["L0_mix_w_dw"])[:, 0, 2]
    laid["L0_mix_w_pw_t"] = _np.asarray(inputs["L0_mix_w_pw"])[:, :, 0].T
    laid["L0_mix_w_res_t"] = _np.asarray(inputs["L0_mix_w_res"])[:, :, 0].T
    laid["L1_gnn_W_t"] = _np.asarray(inputs["L1_gnn_W"]).T
    laid["L1_mix_Wq_t"] = _np.asarray(inputs["L1_mix_Wqkv"])[:, :256].T
    nc = _bacc.Bacc("TRN2", target_bir_lowering=False, num_devices=1)
    arrays, dram = {}, {}
    for name, a in laid.items():
        a = _np.ascontiguousarray(a)
        arrays[f"in_{name}_dram"] = a
        dram[name] = nc.dram_tensor(f"in_{name}_dram", a.shape, _mybir.dt.from_np(a.dtype), kind="ExternalInput").ap()
    out = nc.dram_tensor("out_0_dram", (6250, 256), _mybir.dt.from_np(_np.dtype("float32")), kind="ExternalOutput").ap()
    build_all(nc, dram, out)
    r = _run(nc, [arrays], core_ids=[0])
    return r.results[0]["out_0_dram"]
```

```python
import math

import numpy as np
import concourse.bass as bass
from concourse import mybir
from contextlib import ExitStack, contextmanager

F32 = mybir.dt.float32
BF16 = mybir.dt.bfloat16
I32 = mybir.dt.int32
U32 = mybir.dt.uint32
ALU = mybir.AluOpType
ACT = mybir.ActivationFunctionType
AX = mybir.AxisListType
ds = bass.ds

P = 128
N = 6250
NT = -(-N // P)
LAST = N - (NT - 1) * P
E = 200000
EC = E // P
ER = E - EC * P
EJ = EC + 1
KT = 8
STEP_RING = 4
UNIT = 2 * P
TILES = -(-((E + NT * (UNIT - 1)) // UNIT) * 2 // (STEP_RING * KT)) * STEP_RING * KT
PAIRS = TILES // 2
D = 256
NTP = NT + NT % 2
NPAD = NTP * P
HALF2 = NTP // 2
AW = 260
BIG = 1.0e30
HEADROOM = 60.0
LEAST = 1e-20
LOWER = 100.0
MOST_PASSES = 1 << 20


class Space:
    pass


class Chain:

    def __init__(self, eng, sem, per=0, turn=None):
        self.eng, self.sem, self.n, self.per, self.turn = eng, sem, 0, per, turn

    def __call__(self, ins):
        self.n += 1
        ins.then_inc(self.sem, 1)
        self.wait()

    def wait(self):
        if self.turn is None:
            self.eng.wait_ge(self.sem, self.n)
        else:
            self.eng.wait_ge(self.sem, self.turn * self.per + self.n)

    def end(self):
        assert self.turn is None or self.n == self.per, (self.n, self.per)

@contextmanager
def semaphore(nc, name):
    handle = nc.alloc_semaphore(name)
    yield handle
    nc.clear_and_free_semaphores([handle])

@contextmanager
def stage(nc):
    with ExitStack() as own:
        own.callback(nc.all_engine_barrier)
        yield own


def count_passes(nc, g, link, peaks):
    link(nc.vector.tensor_tensor(peaks[:, 0:4], peaks[:, 0:4], peaks[:, 4:8], ALU.add))
    link(nc.vector.tensor_reduce(peaks[:, 4:5], peaks[:, 0:4], AX.X, ALU.max))
    link(nc.vector.tensor_scalar(peaks[:, 4:5], peaks[:, 4:5], 1.0 / LOWER, 0.95, ALU.mult, ALU.add))
    link(nc.vector.tensor_scalar(g.passes[:, :], peaks[0:1, 4:5], 1.0, float(MOST_PASSES), ALU.max, ALU.min))


def stage_constants(nc, g, ctx):
    def sb(name, shape, dt=F32):
        return ctx.enter_context(nc.sbuf_tensor(name, shape, dt))
    g.iota_row = sb("iota_row", [P, P])
    g.lane = sb("lane", [P, 1])
    g.ident = sb("ident", [P, P])
    g.before = sb("before", [P, P])
    g.ones = sb("ones", [P, P])
    g.passes = sb("passes", [1, 1], I32)
    with stage(nc) as own:
        made = own.enter_context(semaphore(nc, "iotas_made"))
        chain = own.enter_context(semaphore(nc, "const_chain"))
        with nc.Block() as block:
            @block.gpsimd
            def _(pool):
                nc.gpsimd.iota(g.iota_row[:, :], pattern=[[1, P]], base=0, channel_multiplier=0,
                               allow_small_or_imprecise_dtypes=True).then_inc(made, 1)
                nc.gpsimd.iota(g.lane[:, :], pattern=[[0, 1]], base=0, channel_multiplier=1,
                               allow_small_or_imprecise_dtypes=True).then_inc(made, 1)
                nc.gpsimd.memset(g.ones[:, :], 1.0).then_inc(made, 1)

            @block.vector
            def _(dve):
                dve.wait_ge(made, 3)
                nc.vector.tensor_scalar(g.ident[:, :], g.iota_row[:, :], g.lane[:, :], None, ALU.is_equal)
                nc.vector.tensor_scalar(g.before[:, :], g.iota_row[:, :], g.lane[:, :], None, ALU.is_gt)

HALF = 11
SCATTER_TURNS = EC // (2 * HALF)
FIRST = 16 * 2 * HALF
assert SCATTER_TURNS * 2 * HALF == EC


def scatter_edges(nc, g, pool, lo, hi):
    def one_turn(turn, first):
        for half in range(2):
            if not first:
                pool.wait_ge(g.scattered[half], turn * (16 * HALF))
            k = half * HALF
            nc.gpsimd.tensor_copy(g.st_addr[:, k:k + HALF], g.addr[:, ds(turn * (2 * HALF) + k, HALF)]).then_inc(g.pairs_staged, 1)
            nc.gpsimd.tensor_copy(g.st_pair[:, k:k + HALF, :].rearrange("p k w -> p (k w)"),
                                  g.pair[:, :, :].rearrange("p k w -> p (k w)")[:, ds(turn * (4 * HALF) + 2 * k, 2 * HALF)])\
                .then_inc(g.pairs_staged, 1)
            pool.wait_ge(g.pairs_staged, turn * 4 + 2 * half + 2)
            pool.nop(nofuse=True)
            for k in range(half * HALF, half * HALF + HALF):
                pool.indirect_dma_start(g.edge_list, bass.IndirectOffsetOnAxis(ap=g.st_addr[:, k:k + 1], axis=0),
                                        g.st_pair[:, k, :], None).then_inc(g.scattered[half], 16)
    if lo == 0:
        one_turn(0, True)
        lo = 1
    if lo == hi:
        return
    with pool.Fori(lo, hi) as turn:
        one_turn(turn, False)


def stage_places(nc, g, x, src, dst, ctx, lists, edge_list, slots_in, scatters):
    def sbp(name, shape, dt=F32):
        return ctx.enter_context(nc.sbuf_tensor(name, shape, dt))
    g.col_idx = sbp("col_idx", [P, TILES], I32)
    g.row_loc = sbp("row_loc", [P, TILES])
    g.empty_bias = sbp("empty_bias", [P, TILES])
    g.pair_block = sbp("pair_block", [1, PAIRS], I32)
    g.edge_list = edge_list
    g.addr = lists.enter_context(nc.sbuf_tensor("addr", [P, EJ], I32))
    g.pair = lists.enter_context(nc.sbuf_tensor("pair", [P, EJ, 2], I32))
    g.st_addr = lists.enter_context(nc.sbuf_tensor("st_addr", [P, 2 * HALF], U32))
    g.st_pair = lists.enter_context(nc.sbuf_tensor("st_pair", [P, 2 * HALF, 2], I32))
    g.pairs_staged = lists.enter_context(semaphore(nc, "pairs_staged"))
    g.scattered = [lists.enter_context(semaphore(nc, "scattered_even")), lists.enter_context(semaphore(nc, "scattered_odd"))]
    addr, pair = g.addr, g.pair
    with stage(nc) as own:
        def sb(name, shape, dt=F32):
            return own.enter_context(nc.sbuf_tensor(name, shape, dt))

        def sem(name):
            return own.enter_context(semaphore(nc, name))
        srcs = sb("srcs", [P, EJ], I32)
        dsts = sb("dsts", [P, EJ], I32)
        blk_i = sb("blk_i", [P, EJ], I32)
        blk = sb("blk", [P, EJ])
        blk_h = sb("blk_h", [P, EJ + 1], BF16)
        hit_h = sb("hit_h", [P, 2, EJ + 1], BF16)
        hit = sb("hit", [P, EJ])
        cum = sb("cum", [P, 2, EJ])
        own_cum = sb("own_cum", [P, 2, EJ])
        pos = sb("pos", [P, EJ])
        zero = sb("zero", [P, EJ])
        blocks = sb("blocks", [P, NT])
        cnt = sb("cnt", [P, NT])
        tot_i = sb("tot_i", [P, NT], I32)
        npair = sb("npair", [P, NT])
        pair_end = sb("pair_end", [P, NT])
        base = sb("base", [P, NT])
        base_rest = sb("base_rest", [P, NT])
        end_col = sb("end_col", [NT, P])
        pair_no = sb("pair_no", [NT, PAIRS])
        past = sb("past", [NT, PAIRS])
        empty = sb("empty", [P, TILES, 2], I32)
        ps_a = own.enter_context(nc.psum_tensor("ps_sort_a", [P, 512], F32))
        ps_t = own.enter_context(nc.psum_tensor("ps_sort_t", [P, 512], F32))
        ps_b = own.enter_context(nc.psum_tensor("ps_sort_b", [P, 4, 512], F32))
        cleared, loaded, iotas, counted, chain = sem("last_cleared"), sem("edges_loaded"), sem("sort_iotas"), sem("blocks_counted"), sem("sort_chain")
        sums, ends, ends_t, past_ready, blocks_of = sem("count_sums"), sem("ends_made"), sem("ends_turned"), sem("past_ready"), sem("pair_blocks")
        nought = sb("nought", [P, D])
        nought_made, slots_clear = sem("nought_made"), sem("slots_clear")
        x_blank, x_loaded = sem("x_blank"), sem("x_loaded")
        blank, blanked, hit_ready, scanned = sem("blank_made"), sem("list_blanked"), sem("block_hit"), sem("block_scanned")
        chain_rest, chain_v = sem("rest_chain"), sem("rest_steps")
        ranked, placed, pos_zero = sem("block_ranked"), sem("block_placed"), sem("pos_zero")

        def addresses(link, lo, hi):
            c = slice(lo, hi)
            link(nc.vector.tensor_copy(addr[:, c], pos[:, c]))
            link(nc.vector.tensor_single_scalar(blk_i[:, c], addr[:, c], P - 1, ALU.bitwise_and))
            link(nc.vector.tensor_copy(hit[:, c], blk_i[:, c]))
            link(nc.vector.tensor_single_scalar(blk_i[:, c], addr[:, c], 7, ALU.logical_shift_right))
            link(nc.vector.tensor_copy(cum[:, 0, c], blk_i[:, c]))
            link(nc.vector.scalar_tensor_tensor(addr[:, c], hit[:, c], float(TILES), cum[:, 0, c], ALU.mult, ALU.add))
        first_part = ExitStack()
        order = first_part.enter_context(nc.Block())

        @order.sync
        def _(sp):
            sp.wait_ge(cleared, 2)
            sp.dma_start(srcs[:, 0:EC], src[0:EC * P].rearrange("(p j) -> p j", p=P)).then_inc(loaded, 16)
            sp.dma_start(dsts[:, 0:EC], dst[0:EC * P].rearrange("(p j) -> p j", p=P)).then_inc(loaded, 16)
            sp.dma_start(srcs[0:ER, EC:EJ], src[EC * P:E].rearrange("(p j) -> p j", j=1)).then_inc(loaded, 16)
            sp.dma_start(dsts[0:ER, EC:EJ], dst[EC * P:E].rearrange("(p j) -> p j", j=1)).then_inc(loaded, 16)
            sp.dma_start(g.x[:, 0:NT - 1, :], x[0:(NT - 1) * P, :].rearrange("(t p) d -> p t d", p=P)).then_inc(x_loaded, 16)
            sp.wait_ge(x_blank, 1)
            sp.dma_start(g.x[0:LAST, NT - 1, :], x[(NT - 1) * P:N, :]).then_inc(x_loaded, 16)
            sp.wait_ge(blank, 2)
            sp.dma_start(edge_list.rearrange("(p t) w -> p (t w)", p=P),
                         empty[:, :, :].rearrange("p t w -> p (t w)")).then_inc(blanked, 16)
            sp.wait_ge(nought_made, 1)
            sp.dma_start(slots_in.rearrange("(t p) d -> p t d", p=P),
                         nought[:, :].unsqueeze(1).to_broadcast([P, slots_in.shape[0] // P, D])).then_inc(slots_clear, 16)
            sp.wait_ge(blanked, 16)
            sp.wait_ge(slots_clear, 16)
            sp.wait_ge(x_loaded, 32)

        @order.gpsimd
        def _(pool):
            nc.gpsimd.iota(blocks[:, :], pattern=[[1, NT]], base=0, channel_multiplier=0,
                           allow_small_or_imprecise_dtypes=True).then_inc(iotas, 1)
            nc.gpsimd.iota(pair_no[:, :], pattern=[[1, PAIRS]], base=0, channel_multiplier=0,
                           allow_small_or_imprecise_dtypes=True).then_inc(iotas, 1)
            nc.gpsimd.memset(empty[:, :, 0], 0).then_inc(blank, 1)
            nc.gpsimd.memset(nought[:, :], 0.0).then_inc(nought_made, 1)
            nc.gpsimd.memset(g.x[:, NT - 1:NTP, :], 0.0).then_inc(x_blank, 1)
            nc.gpsimd.memset(empty[:, :, 1], -1).then_inc(blank, 1)
            nc.gpsimd.memset(pos[:, :], 0.0).then_inc(pos_zero, 1)
            pool.wait_ge(pos_zero, 1)

            def place(turn, r, first):
                v = turn * 2 + r
                pool.wait_ge(ranked, v + 1)
                if not (first and r == 0):
                    pool.wait_ge(placed, v)
                nc.gpsimd.tensor_tensor(pos[:, 0:FIRST], pos[:, 0:FIRST], own_cum[:, r, 0:FIRST], ALU.add).then_inc(placed, 1)
            place(0, 0, True)
            place(0, 1, True)
            with pool.Fori(1, NT // 2) as turn:
                place(turn, 0, False)
                place(turn, 1, False)
            if NT % 2:
                place(NT // 2, 0, False)
        @order.vector
        def _(dve):
            nc.vector.memset(srcs[:, EC:EJ], 0).then_inc(cleared, 1)
            nc.vector.memset(dsts[:, EC:EJ], 0).then_inc(cleared, 1)
            nc.vector.memset(zero[:, :], 0.0)
            link = Chain(dve, chain)
            dve.wait_ge(loaded, 64)
            dve.wait_ge(iotas, 2)
            nc.vector.tensor_copy(pair[:, :, 0], dsts[:, :])
            nc.vector.tensor_single_scalar(pair[:, :, 1], srcs[:, :], P - 1, ALU.bitwise_and)
            link(nc.vector.tensor_single_scalar(blk_i[:, :], srcs[:, :], 7, ALU.logical_shift_right))
            link(nc.vector.tensor_copy(blk[:, :], blk_i[:, :]))
            link(nc.vector.memset(blk[ER:P, EC:EJ], -1.0))
            link(nc.vector.memset(blk_h[:, EJ:EJ + 1], -1.0))
            link(nc.vector.tensor_copy(blk_h[:, 0:EJ], blk[:, :]))
            def count(v, r, first):
                if not first:
                    dve.wait_ge(counted, v - 1)
                nc.vector.tensor_scalar(hit_h[:, r, :], blk_h[:, :], blocks[:, ds(v, 1)], 0.0, ALU.is_equal, ALU.add,
                                        accum_out=cnt[:, ds(v, 1)]).then_inc(counted, 1)
            assert NT % 2 == 1
            count(0, 0, True)
            count(1, 1, True)
            with dve.Fori(1, NT // 2) as turn:
                count(turn * 2, 0, False)
                count(turn * 2 + 1, 1, False)
            count(NT - 1, 0, False)
            dve.wait_ge(counted, NT)
            dve.wait_ge(sums, 1)
            link(nc.vector.tensor_scalar(tot_i[:, :], ps_a[:, 0:NT], float(UNIT - 1), None, ALU.add))
            link(nc.vector.tensor_single_scalar(tot_i[:, :], tot_i[:, :], 8, ALU.logical_shift_right))
            link(nc.vector.tensor_copy(npair[:, :], tot_i[:, :]))
            link(nc.vector.tensor_tensor_scan(pair_end[:, :], npair[:, :], zero[:, 0:NT], 0.0, ALU.add, ALU.add))
            nc.vector.tensor_copy(end_col[0:1, 0:1], pair_end[0:1, 0:1]).then_inc(ends, 1)
            link(nc.vector.tensor_tensor(base[:, :], pair_end[:, :], npair[:, :], ALU.subtract))
            link(nc.vector.tensor_scalar(base[:, :], base[:, :], float(UNIT), -1.0, ALU.mult, ALU.add))
            link(nc.vector.tensor_tensor(base[:, :], base[:, :], ps_a[:, NT:2 * NT], ALU.add))
            dve.wait_ge(ends_t, 1)
            link(nc.vector.tensor_copy(end_col[:, :], ps_t[0:NT, 0:P]))
            nc.vector.tensor_scalar(past[:, :], pair_no[:, :], end_col[:, 0:1], None, ALU.is_ge).then_inc(past_ready, 1)
            dve.wait_ge(blocks_of, 1)
            link(nc.vector.tensor_scalar(g.pair_block[:, :].rearrange("a (c n) -> a c n", c=4),
                                         ps_b[0:1, :, 0:PAIRS // 4], float(NT - 1), None, ALU.min))
            def hits(v, r):
                nc.vector.tensor_scalar(hit_h[:, r, 0:FIRST], blk_h[:, 0:FIRST], blocks[:, ds(v, 1)], None, ALU.is_equal).then_inc(hit_ready, 1)

            def ranks(v, r, first, last=False):
                dve.wait_ge(hit_ready, v + 1)
                nc.vector.tensor_tensor_scan(cum[:, r, 0:FIRST], hit_h[:, r, 0:FIRST], zero[:, 0:FIRST], base[:, ds(v, 1)],
                                             ALU.add, ALU.add).then_inc(scanned, 1)
                if not last:
                    hits(v + 1, 1 - r)
                dve.wait_ge(scanned, v + 1)
                nc.vector.tensor_copy(base_rest[:, ds(v, 1)], cum[:, r, FIRST - 1:FIRST])
                if not first:
                    dve.wait_ge(placed, v - 1)
                nc.vector.scalar_tensor_tensor(own_cum[:, r, 0:FIRST], blk[:, 0:FIRST], blocks[:, ds(v, 1)], cum[:, r, 0:FIRST],
                                               ALU.is_equal, ALU.mult).then_inc(ranked, 1)
            hits(0, 0)
            ranks(0, 0, True)
            ranks(1, 1, True)
            with dve.Fori(1, NT // 2) as turn:
                ranks(turn * 2, 0, False)
                ranks(turn * 2 + 1, 1, False)
            ranks(NT - 1, 0, False, last=True)
            dve.wait_ge(placed, NT)
            addresses(link, 0, FIRST)

        @order.tensor
        def _(pe):
            pe.wait_ge(counted, NT)
            nc.tensor.matmul(ps_a[:, 0:NT], g.ones[:, :], cnt[:, :], start=True, stop=True)
            nc.tensor.matmul(ps_a[:, NT:2 * NT], g.before[:, :], cnt[:, :], start=True, stop=True).then_inc(sums, 1)
            pe.wait_ge(ends, 1)
            nc.tensor.transpose(ps_t[0:NT, 0:P], pair_end[:, :], g.ident[:, :]).then_inc(ends_t, 1)
            pe.wait_ge(past_ready, 1)
            for c in range(4):
                last = nc.tensor.matmul(ps_b[:, c, 0:PAIRS // 4], g.ones[0:NT, :],
                                        past[:, c * (PAIRS // 4):(c + 1) * (PAIRS // 4)], start=True, stop=True)
            last.then_inc(blocks_of, 1)
        first_part.close()
        with nc.Block() as block:
            @block.gpsimd
            def _(pool):
                scatter_edges(nc, g, pool, *scatters)

            @block.vector
            def _(dve):
                c = slice(FIRST, EJ)
                STEPS = 4
                with dve.Fori(0, NT) as v:
                    step = Chain(dve, chain_v, STEPS, v)
                    step(nc.vector.tensor_scalar(hit_h[:, 0, c], blk_h[:, c], blocks[:, ds(v, 1)], None, ALU.is_equal))
                    step(nc.vector.tensor_tensor_scan(cum[:, 0, c], hit_h[:, 0, c], zero[:, c], base_rest[:, ds(v, 1)], ALU.add, ALU.add))
                    step(nc.vector.scalar_tensor_tensor(own_cum[:, 0, c], blk[:, c], blocks[:, ds(v, 1)], cum[:, 0, c],
                                                        ALU.is_equal, ALU.mult))
                    step(nc.vector.tensor_tensor(pos[:, c], pos[:, c], own_cum[:, 0, c], ALU.add))
                    step.end()
                addresses(Chain(dve, chain_rest), FIRST, EJ)


def stage_list(nc, g, lo):
    with stage(nc) as own:
        back = own.enter_context(nc.sbuf_tensor("list_back", [P, TILES, 2], I32))
        listed, chain = own.enter_context(semaphore(nc, "list_read")), own.enter_context(semaphore(nc, "list_chain"))
        with nc.Block() as block:
            @block.gpsimd
            def _(pool):
                if lo < SCATTER_TURNS:
                    scatter_edges(nc, g, pool, lo, SCATTER_TURNS)
                pool.wait_ge(g.scattered[0], SCATTER_TURNS * (16 * HALF))
                nc.gpsimd.tensor_copy(g.st_addr[:, 0:1], g.addr[:, EC:EJ]).then_inc(g.pairs_staged, 1)
                nc.gpsimd.tensor_copy(g.st_pair[:, 0, :], g.pair[:, EC, :]).then_inc(g.pairs_staged, 1)
                pool.wait_ge(g.pairs_staged, 4 * SCATTER_TURNS + 2)
                pool.nop(nofuse=True)
                pool.indirect_dma_start(g.edge_list, bass.IndirectOffsetOnAxis(ap=g.st_addr[0:ER, 0:1], axis=0),
                                        g.st_pair[0:ER, 0, :], None).then_inc(g.scattered[0], 16)

            @block.sync
            def _(sp):
                sp.wait_ge(g.scattered[0], 16 * HALF * SCATTER_TURNS + 16)
                sp.wait_ge(g.scattered[1], 16 * HALF * SCATTER_TURNS)
                sp.dma_start(back[:, :, :].rearrange("p t w -> p (t w)"),
                             g.edge_list.rearrange("(p t) w -> p (t w)", p=P)).then_inc(listed, 16)

            @block.vector
            def _(dve):
                dve.wait_ge(listed, 16)
                nc.vector.tensor_copy(g.col_idx[:, :], back[:, :, 0])
                link = Chain(dve, chain)
                link(nc.vector.tensor_copy(g.row_loc[:, :], back[:, :, 1]))
                nc.vector.tensor_scalar(g.empty_bias[:, :], g.row_loc[:, :], 0.0, -BIG, ALU.is_lt, ALU.mult)


def stage_aggregate(nc, g, tag, table, width, shared, rows, acc, top):
    STEPS = TILES // KT
    TURNS = STEPS // STEP_RING
    VW = width - 4
    KP = KT // 2
    with stage(nc) as own:
        def sb(name, shape, dt=F32):
            return own.enter_context(nc.sbuf_tensor(name + tag, shape, dt))

        def sem(name):
            return own.enter_context(semaphore(nc, name + tag))
        got = sb("got", [P, STEP_RING, KT, width])
        st_idx = sb("st_idx", [P, STEP_RING, KT], I32)
        hot = sb("hot", [P, STEP_RING, KT, P])
        hot_t = sb("hot_t", [P, 2, KT, P])
        weighted = sb("weighted", [P, 2, KT, AW])
        z = sb("z", [P, KT, 4])
        z2 = sb("z2", [P, KT, 4])
        ps_t = own.enter_context(nc.psum_tensor("ps_hot" + tag, [P, KT * P], F32))
        ps_s = own.enter_context(nc.psum_tensor("ps_score" + tag, [P, 2, 512], F32))
        ps_g = own.enter_context(nc.psum_tensor("ps_sum" + tag, [P, KP, 512], F32))
        idx_staged, hot_ready, hot_turned, hot_copied = sem("idx_staged"), sem("hot_ready"), sem("hot_turned"), sem("hot_copied")
        scored, z_ready, w_ready, scaled = sem("scored"), sem("z_ready"), sem("w_ready"), sem("scaled")
        summed, added, chain, cleared = sem("summed"), sem("added"), sem("z_chain"), sem("acc_cleared")
        gathered = [sem(f"gathered{r}") for r in range(STEP_RING)]
        block = own.enter_context(nc.Block())

        def scores(r):
            return ps_s[:, r % 2, 0:KT * 8].rearrange("p (k c) -> p k c", c=8)

        def blocks_of(pair, count, engine):
            _, values = nc.values_load_multi_w_load_instructions(g.pair_block[0:1, ds(pair, count)], engines=(engine,),
                                                                 min_val=0, max_val=NT - 1)
            return values

        def later(turn, r, by):
            return turn + (r + by) // STEP_RING, (r + by) % STEP_RING

        def exists(last, r, by):
            return not last or r + by < STEP_RING

        def all_turns(eng, one_turn):
            one_turn(0, True, False)
            with eng.Fori(1, TURNS - 1) as turn:
                one_turn(turn, False, False)
            one_turn(TURNS - 1, False, True)

        @block.gpsimd
        def _(pool):
            def gather(turn, r, first):
                j = turn * STEP_RING + r
                pool.wait_ge(idx_staged, j + 1)
                if not first:
                    pool.wait_ge(scaled, j - (STEP_RING - 1))
                pool.nop(nofuse=True)
                for k in range(KT):
                    pool.indirect_dma_start(got[:, r, k, :], None, table,
                                            bass.IndirectOffsetOnAxis(ap=st_idx[:, r, k:k + 1], axis=0))\
                        .then_inc(gathered[r], 16)
            for r in range(STEP_RING):
                gather(0, r, True)
            with pool.Fori(1, TURNS) as turn:
                for r in range(STEP_RING):
                    gather(turn, r, False)

        @block.scalar
        def _(act):
            def weigh(turn, r, first):
                i = turn * STEP_RING + r
                act.wait_ge(z_ready, i + 1)
                if not (first and r < 2):
                    act.wait_ge(summed, (i - 1) * KP)
                nc.scalar.activation(weighted[:, r % 2, :, 256:AW], z[:, :, :], ACT.Exp).then_inc(w_ready, 1)

            def keep_turned(turn, r, first):
                i = turn * STEP_RING + r
                act.wait_ge(hot_turned, i + 1)
                if not (first and r < 2):
                    act.wait_ge(scored, i - 1)
                for c in range(2):
                    last = nc.scalar.copy(hot_t[:, r % 2, :, :].rearrange("p k n -> p (k n)")[:, c * 512:(c + 1) * 512],
                                          ps_t[:, c * 512:(c + 1) * 512])
                last.then_inc(hot_copied, 1)

            def one_turn(turn, first, last):
                for r in range(STEP_RING):
                    if exists(last, r, 2):
                        t, q = later(turn, r, 2)
                        keep_turned(t, q, first and r + 2 < STEP_RING)
                    if exists(last, r, 1):
                        t, q = later(turn, r, 1)
                        weigh(t, q, first and r + 1 < STEP_RING)
            keep_turned(0, 0, True)
            keep_turned(0, 1, True)
            weigh(0, 0, True)
            all_turns(act, one_turn)

        @block.tensor
        def _(pe):
            def turn_and_score(turn, r, first):
                i = turn * STEP_RING + r
                pe.wait_ge(hot_ready, i + 1)
                if not (first and r == 0):
                    pe.wait_ge(hot_copied, i)
                for k in range(KT):
                    last = nc.tensor.transpose(ps_t[:, k * P:(k + 1) * P], hot[:, r, k, :], g.ident[:, :])
                last.then_inc(hot_turned, 1)
                blocks = blocks_of(i * KP, KP, mybir.EngineType.PE)
                if not (first and r < 2):
                    pe.wait_ge(z_ready, i - 1)
                pe.wait_ge(hot_copied, i + 1)
                for k in range(KT):
                    b = blocks[k // 2]
                    last = nc.tensor.matmul(ps_s[:, r % 2, k * 8:(k + 1) * 8], hot_t[:, r % 2, k, :], rows[:, ds(b * 8, 8)],
                                            start=True, stop=True)
                last.then_inc(scored, 1)

            def sum_up(turn, r, first, half):
                i = turn * STEP_RING + r
                pe.wait_ge(scaled, i + 1)
                for p in half:
                    if not (first and r == 0):
                        pe.wait_ge(added, i * KP + (p - KP + 1))
                    for k in (2 * p, 2 * p + 1):
                        last = nc.tensor.matmul(ps_g[:, p, 0:AW], hot[:, r, k, :], weighted[:, r % 2, k, :],
                                                start=(k == 2 * p), stop=(k == 2 * p + 1))
                    last.then_inc(summed, 1)

            def one_turn(turn, first, last):
                for r in range(STEP_RING):
                    sum_up(turn, r, first, range(KP // 2))
                    if exists(last, r, 2):
                        t, q = later(turn, r, 2)
                        turn_and_score(t, q, first and r + 2 < STEP_RING)
                    sum_up(turn, r, first, range(KP // 2, KP))
            turn_and_score(0, 0, True)
            turn_and_score(0, 1, True)
            all_turns(pe, one_turn)

        @block.vector
        def _(dve):
            def stage_idx(turn, r):
                nc.vector.tensor_copy(st_idx[:, r, :], g.col_idx[:, ds((turn * STEP_RING + r) * KT, KT)]).then_inc(idx_staged, 1)

            def one_hot(turn, r):
                j = (turn * STEP_RING + r) * KT
                nc.vector.tensor_tensor(hot[:, r, :, :], g.iota_row[:, :].unsqueeze(1).to_broadcast([P, KT, P]),
                                        g.row_loc[:, ds(j, KT)].unsqueeze(2).to_broadcast([P, KT, P]),
                                        ALU.is_equal).then_inc(hot_ready, 1)

            def exponents(turn, r):
                i = turn * STEP_RING + r
                link = Chain(dve, chain, 4, i)
                dve.wait_ge(gathered[r], turn * (16 * KT) + 16 * KT)
                link(nc.vector.tensor_tensor(z2[:, :, :], got[:, r, :, VW:width],
                                             g.empty_bias[:, ds(i * KT, KT)].unsqueeze(2).to_broadcast([P, KT, 4]), ALU.add))
                dve.wait_ge(scored, i + 1)
                link(nc.vector.tensor_tensor(z2[:, :, :], z2[:, :, :], scores(r)[:, :, 0:4], ALU.add))
                link(nc.vector.tensor_tensor(top[:, :, :], top[:, :, :], z2[:, :, :], ALU.max))
                link(nc.vector.scalar_tensor_tensor(z2[:, :, :], z2[:, :, :], 0.2, z2[:, :, :], ALU.mult, ALU.max))
                nc.vector.tensor_tensor(z[:, :, :], z2[:, :, :], scores(r)[:, :, 4:8], ALU.subtract).then_inc(z_ready, 1)
                link.end()

            def scale(turn, r):
                i = turn * STEP_RING + r
                dve.wait_ge(w_ready, i + 1)
                w = weighted[:, r % 2, :, 256:AW].unsqueeze(3).to_broadcast([P, KT, 4, 64])
                out = weighted[:, r % 2, :, 0:256].rearrange("p k (h d) -> p k h d", h=4)
                if shared:
                    v = got[:, r, :, 0:64].unsqueeze(2).to_broadcast([P, KT, 4, 64])
                else:
                    v = got[:, r, :, 0:256].rearrange("p k (h d) -> p k h d", h=4)
                nc.vector.tensor_tensor(out, v, w, ALU.mult).then_inc(scaled, 1)

            def add(turn, r, first, half, blocks):
                i = turn * STEP_RING + r
                for p, b in zip(half, blocks):
                    dve.wait_ge(summed, i * KP + p + 1)
                    if not (first and r == 0 and p == 0):
                        dve.wait_ge(added, i * KP + p)
                    nc.vector.tensor_tensor(acc[:, ds(b * AW, AW)], acc[:, ds(b * AW, AW)], ps_g[:, p, 0:AW],
                                            ALU.add).then_inc(added, 1)
            LOW, HIGH = range(KP // 2), range(KP // 2, KP)
            DVE = mybir.EngineType.DVE

            def one_turn(turn, first, last):
                for r in range(STEP_RING):
                    i = turn * STEP_RING + r
                    t, q = (turn, r - 1) if r else (turn - 1, STEP_RING - 1)
                    if first and r == 0:
                        blocks = (None,) * len(HIGH) + tuple(blocks_of(i * KP, len(LOW), DVE))
                    else:
                        blocks = blocks_of(i * KP - len(HIGH), KP, DVE)
                    if not last:
                        stage_idx(turn + 1, r)
                    scale(turn, r)
                    if not (first and r == 0):
                        add(t, q, first, HIGH, blocks[:len(HIGH)])
                    if exists(last, r, 3):
                        one_hot(*later(turn, r, 3))
                    if exists(last, r, 1):
                        exponents(*later(turn, r, 1))
                    add(turn, r, first, LOW, blocks[len(HIGH):])
                if last:
                    add(turn, STEP_RING - 1, False, HIGH, blocks_of(turn * STEP_RING * KP + (STEP_RING - 1) * KP + len(LOW), len(HIGH), DVE))
            for r in range(STEP_RING):
                stage_idx(0, r)
            for r in range(3):
                one_hot(0, r)
            nc.vector.memset(top[:, :, :], -BIG).then_inc(cleared, 1)
            nc.vector.memset(acc[:, :], 0.0).then_inc(cleared, 1)
            dve.wait_ge(cleared, 2)
            exponents(0, 0)
            all_turns(dve, one_turn)


def stage_lower(nc, g, tag, acc):
    with stage(nc) as own:
        low = own.enter_context(nc.sbuf_tensor("low" + tag, [P, NT, 4], F32))
        chain = own.enter_context(semaphore(nc, "lower_chain" + tag))
        with nc.Block() as block:
            @block.vector
            def _(dve):
                link = Chain(dve, chain)
                sums = acc[:, :].rearrange("p (t w) -> p t w", w=AW)[:, 0:NT, 256:AW]
                bounds = g.rows[:, :].rearrange("p (t c) -> p t c", c=8)[:, 0:NT, 4:8]
                link(nc.vector.tensor_scalar(low[:, :, :], sums, LEAST, LOWER, ALU.is_lt, ALU.mult))
                nc.vector.tensor_tensor(bounds, bounds, low[:, :, :], ALU.subtract)


def aggregate_passes(nc, g, tag, table, width, shared, acc, top):
    _, passes = nc.values_load_multi_w_load_instructions(g.passes[0:1, 0:1], min_val=1, max_val=MOST_PASSES)
    with nc.Fori(0, passes[0]):
        stage_aggregate(nc, g, tag, table, width, shared, g.rows, acc, top)
        stage_lower(nc, g, tag, acc)

SCATTERS = {"places": (0, 12), "stats": (12, 13), "table": (13, 19), "moments": (19, 25), "mix": (25, 65), "ball": (65, 69)}
LIM = 0.9999899864196777
ATANH_LIM = 0.5 * math.log((1.0 + LIM) / (1.0 - LIM))


def stage_ln_stats(nc, g, tag, eps=1e-5, source=None, scatters=None):
    if source is None:
        def source(i):
            return g.x[:, ds(i, 1), :].rearrange("p t d -> p (t d)")
    assert NTP % 10 == 0
    with stage(nc) as own:
        def sem(name):
            return own.enter_context(semaphore(nc, name + tag))
        stats = own.enter_context(nc.sbuf_tensor("stats" + tag, [P, NTP * 6], F32))
        sd = own.enter_context(nc.sbuf_tensor("sd" + tag, [P, NTP], F32))
        got, spread, chain, rooted = sem("stat_got"), sem("spread"), sem("stat_chain"), sem("rooted")
        with nc.Block() as block:
            @block.vector
            def _(dve):
                with dve.Fori(0, NTP // 10) as turn:
                    for r in range(10):
                        i = turn * 10 + r
                        nc.vector.bn_stats(stats[:, ds(i * 6, 6)], source(i)).then_inc(got, 1)
                dve.wait_ge(got, NTP)
                half = stats[:, :].rearrange("p (t c) -> p t c", c=6)
                link = Chain(dve, chain)
                link(nc.vector.tensor_tensor(g.mean[:, :], half[:, :, 1], half[:, :, 4], ALU.add))
                link(nc.vector.tensor_scalar(g.mean[:, :], g.mean[:, :], 0.5, None, ALU.mult))
                link(nc.vector.tensor_tensor(sd[:, :], half[:, :, 1], g.mean[:, :], ALU.subtract))
                link(nc.vector.tensor_tensor(sd[:, :], sd[:, :], sd[:, :], ALU.mult))
                link(nc.vector.tensor_tensor(g.var[:, :], half[:, :, 2], half[:, :, 5], ALU.add))
                link(nc.vector.scalar_tensor_tensor(g.var[:, :], g.var[:, :], 1.0 / D, sd[:, :], ALU.mult, ALU.add))
                nc.vector.tensor_scalar(sd[:, :], g.var[:, :], eps, None, ALU.add).then_inc(spread, 1)
                dve.wait_ge(rooted, 1)
                nc.vector.reciprocal(g.rstd[:, :], sd[:, :])

            if scatters is not None:
                @block.gpsimd
                def _(pool):
                    scatter_edges(nc, g, pool, *scatters)

            @block.scalar
            def _(act):
                act.wait_ge(spread, 1)
                nc.scalar.activation(sd[:, :], sd[:, :], ACT.Sqrt).then_inc(rooted, 1)


def stage_l0_gnn_table(nc, g, w, w_t, b, a_src, a_dst, table):
    with stage(nc) as own:
        def sb(name, shape, dt=F32):
            return own.enter_context(nc.sbuf_tensor(name, shape, dt))

        def sem(name):
            return own.enter_context(semaphore(nc, name))

        def pb(name, shape):
            return own.enter_context(nc.psum_tensor(name, shape, F32))
        wl = sb("wl", [P, 2, 72])
        wt = sb("wt", [64, 256])
        eye_a = sb("eye_a", [64, 72])
        b_col = sb("b_col", [64, 1])
        b_wide = sb("b_wide", [64, P])
        bias = sb("bias_bc", [P, 72])
        n = sb("n0", [P, NTP])
        f = sb("f0", [P, NTP])
        inv_f = sb("inv_f0", [P, NTP])
        q = sb("q0", [P, NTP])
        lo = sb("lo0", [P, NTP])
        hi = sb("hi0", [P, NTP])
        small = sb("small0", [P, NTP], I32)
        scl = sb("scl0", [P, NTP])
        xs = sb("xs", [P, 2, D])
        st = sb("st0", [P, 2, 2, P])
        row = sb("row0", [P, 2, 72])
        colmax = sb("colmax", [P, 8])
        allmax = sb("allmax", [P, 8])
        ps_x = pb("ps_x0", [P, 2, 512])
        ps_r = pb("ps_r0", [P, 2, 512])
        ps_w = pb("ps_w0", [P, 2, 512])
        loaded, chain, prepared, biased = sem("w0_loaded"), sem("f0_chain"), sem("w0_prepared"), sem("b0_ready")
        rooted, logged, tail, wide = sem("n0_rooted"), sem("n0_logged"), sem("log_in"), sem("b_wide_ready")
        xs_ready, turned, staged, kept = sem("xs_ready"), sem("xs_turned"), sem("xs_staged"), sem("xt_kept")
        rowed, row_ready, written, factors = sem("row_mm"), sem("row_ready"), [sem("row_out0"), sem("row_out1")], sem("factors")
        reduced, maxed, maxes = sem("max_reduced"), sem("max_ready"), sem("run_max")
        wl_ready = sem("wl_ready")
        with nc.Block() as block:
            @block.sync
            def _(sp):
                with nc.allow_non_contiguous_dma(reason="small columns"):
                    sp.dma_start(wl[:, :, 0:64], w.rearrange("(c p) n -> p c n", p=P)).then_inc(loaded, 16)
                    sp.dma_start(wt[:, :], w_t).then_inc(loaded, 16)
                    sp.dma_start(eye_a[:, 64:68], a_dst).then_inc(loaded, 16)
                    sp.dma_start(eye_a[:, 68:72], a_src).then_inc(loaded, 16)
                    sp.dma_start(b_col[:, :], b.rearrange("(p o) -> p o", o=1)).then_inc(loaded, 16)

                def put(turn, r):
                    sp.wait_ge(row_ready, turn * 2 + (r + 1))
                    sp.dma_start(table[ds((turn * 2 + r) * P, P), :], row[:, r, 0:68]).then_inc(written[r], 16)
                with sp.Fori(0, HALF2) as turn:
                    put(turn, 0)
                    put(turn, 1)
                for r in range(2):
                    sp.wait_ge(written[r], 16 * HALF2)

            @block.scalar
            def _(act):
                act.wait_ge(chain, 2)
                nc.scalar.activation(n[:, :], q[:, :], ACT.Sqrt).then_inc(rooted, 1)
                act.wait_ge(tail, 1)
                nc.scalar.activation(lo[:, :], lo[:, :], ACT.Ln).then_inc(logged, 1)

                def stage(turn, r, first):
                    i = turn * 2 + r
                    act.wait_ge(turned, i + 1)
                    if not first:
                        act.wait_ge(rowed, i - 1)
                        act.wait_ge(kept, i - 1)
                    nc.scalar.copy(st[:, r, :, :].rearrange("p c n -> p (c n)"), ps_x[:, r, 0:256]).then_inc(staged, 1)
                stage(0, 0, True)
                stage(0, 1, True)
                with act.Fori(1, HALF2) as turn:
                    stage(turn, 0, False)
                    stage(turn, 1, False)

            @block.gpsimd
            def _(pool):
                scatter_edges(nc, g, pool, *SCATTERS["table"])
                pool.wait_ge(maxes, NTP)
                nc.gpsimd.partition_all_reduce(allmax[:, :], colmax[:, :], P, bass.bass_isa.ReduceOp.max).then_inc(reduced, 1)

            @block.tensor
            def _(pe):
                pe.wait_ge(loaded, 80)
                for c in range(2):
                    nc.tensor.matmul(ps_w[:, c, 0:8], wt[:, c * P:(c + 1) * P], eye_a[:, 64:72],
                                     start=True, stop=True).then_inc(prepared, 1)
                pe.wait_ge(wide, 2)
                nc.tensor.matmul(ps_x[:, 0, 0:72], b_wide[:, :], eye_a[:, :], start=True, stop=True).then_inc(biased, 1)
                pe.wait_ge(factors, 1)

                def turn_tile(turn, r, first):
                    i = turn * 2 + r
                    pe.wait_ge(xs_ready, i + 1)
                    if not first:
                        pe.wait_ge(staged, i - 1)
                    for c in range(2):
                        last = nc.tensor.transpose(ps_x[:, r, c * P:(c + 1) * P], xs[:, r, c * P:(c + 1) * P], g.ident[:, :])
                    last.then_inc(turned, 1)

                def row_tile(turn, r, first):
                    i = turn * 2 + r
                    pe.wait_ge(staged, i + 1)
                    if not first:
                        pe.wait_ge(row_ready, i - 1)
                    for c in range(2):
                        last = nc.tensor.matmul(ps_r[:, r, 0:72], st[:, r, c, :], wl[:, c, :], start=(c == 0), stop=(c == 1))
                    last.then_inc(rowed, 1)
                for first in (True, False):
                    def both(turn):
                        turn_tile(turn, 0, first)
                        turn_tile(turn, 1, first)
                        row_tile(turn, 0, first)
                        row_tile(turn, 1, first)
                    if first:
                        pe.wait_ge(wl_ready, 2)
                        both(0)
                    else:
                        with pe.Fori(1, HALF2) as turn:
                            both(turn)

            @block.vector
            def _(dve):
                link = Chain(dve, chain)
                link(nc.vector.tensor_tensor(q[:, :], g.rstd[:, :], g.rstd[:, :], ALU.mult))
                link(nc.vector.scalar_tensor_tensor(q[:, :], g.var[:, :], float(D), q[:, :], ALU.mult, ALU.mult))
                dve.wait_ge(rooted, 1)
                link(nc.vector.tensor_scalar(n[:, :], n[:, :], 1e-15, None, ALU.max))
                link(nc.vector.tensor_scalar(q[:, :], n[:, :], LIM, None, ALU.min))
                link(nc.vector.tensor_scalar(hi[:, :], q[:, :], -1.0, 1.0, ALU.mult, ALU.add))
                link(nc.vector.reciprocal(hi[:, :], hi[:, :]))
                link(nc.vector.scalar_tensor_tensor(lo[:, :], q[:, :], 1.0, hi[:, :], ALU.add, ALU.mult))
                nc.vector.tensor_scalar(small[:, :], q[:, :], 0.25, None, ALU.is_lt).then_inc(tail, 1)
                link(nc.vector.tensor_tensor(scl[:, :], q[:, :], q[:, :], ALU.mult))
                link(nc.vector.tensor_scalar(hi[:, :], scl[:, :], 1.0 / 15, 1.0 / 13, ALU.mult, ALU.add))
                for k in (11, 9, 7, 5, 3, 1):
                    link(nc.vector.tensor_tensor(hi[:, :], hi[:, :], scl[:, :], ALU.mult))
                    link(nc.vector.tensor_scalar(hi[:, :], hi[:, :], 1.0 / k, None, ALU.add))
                link(nc.vector.tensor_tensor(hi[:, :], hi[:, :], q[:, :], ALU.mult))
                dve.wait_ge(logged, 1)
                link(nc.vector.tensor_scalar(lo[:, :], lo[:, :], 0.5, None, ALU.mult))
                link(nc.vector.copy_predicated(lo[:, :], small[:, :], hi[:, :]))
                link(nc.vector.reciprocal(n[:, :], n[:, :]))
                link(nc.vector.tensor_tensor(f[:, :], lo[:, :], n[:, :], ALU.mult))
                link(nc.vector.reciprocal(inv_f[:, :], f[:, :]))
                link(nc.vector.tensor_tensor(scl[:, :], f[:, :], g.rstd[:, :], ALU.mult))
                dve.wait_ge(loaded, 80)
                nc.vector.tensor_copy(eye_a[:, 0:64], g.ident[0:64, 0:64]).then_inc(wide, 1)
                nc.vector.tensor_copy(b_wide[:, :], b_col[:, :].to_broadcast([64, P])).then_inc(wide, 1)
                for c in range(2):
                    dve.wait_ge(prepared, c + 1)
                    nc.vector.tensor_copy(wl[:, c, 64:72], ps_w[:, c, 0:8]).then_inc(wl_ready, 1)
                dve.wait_ge(biased, 1)
                nc.vector.tensor_copy(bias[:, :], ps_x[:, 0, 0:72]).then_inc(factors, 1)
                link(nc.vector.memset(colmax[:, :], -BIG))
                dve.wait_ge(factors, 1)

                def norm(turn, r, first):
                    i = turn * 2 + r
                    if not first:
                        dve.wait_ge(turned, i - 1)
                    nc.vector.tensor_scalar(xs[:, r, :], g.x[:, ds(i, 1), :].rearrange("p t d -> p (t d)"),
                                            g.mean[:, ds(i, 1)], scl[:, ds(i, 1)], ALU.subtract, ALU.mult).then_inc(xs_ready, 1)

                def finish(turn, r, first):
                    i = turn * 2 + r
                    dve.wait_ge(staged, i + 1)
                    nc.vector.tensor_copy(g.xt[:, :, ds(i * P, P)], st[:, r, :, :]).then_inc(kept, 1)
                    dve.wait_ge(rowed, i + 1)
                    if not first:
                        dve.wait_ge(written[r], turn * 16)
                    nc.vector.scalar_tensor_tensor(row[:, r, :], ps_r[:, r, 0:72], inv_f[:, ds(i, 1)], bias[:, :],
                                                   ALU.mult, ALU.add).then_inc(row_ready, 1)
                    dve.wait_ge(row_ready, i + 1)
                    nc.vector.tensor_copy(g.rows[:, ds(i * 8, 4)], row[:, r, 68:72])
                    if not (first and r == 0):
                        dve.wait_ge(maxes, i)
                    nc.vector.scalar_tensor_tensor(colmax[:, 4:8], row[:, r, 64:68], -1.0, colmax[:, 4:8], ALU.mult, ALU.max)
                    nc.vector.tensor_tensor(colmax[:, 0:4], colmax[:, 0:4], row[:, r, 64:68], ALU.max).then_inc(maxes, 1)
                norm(0, 0, True)
                norm(0, 1, True)
                finish(0, 0, True)
                finish(0, 1, True)
                with dve.Fori(1, HALF2) as turn:
                    norm(turn, 0, False)
                    norm(turn, 1, False)
                    finish(turn, 0, False)
                    finish(turn, 1, False)
                dve.wait_ge(maxes, NTP)
                dve.wait_ge(reduced, 1)
                rows = g.rows[:, :].rearrange("p (t c) -> p t c", c=8)
                link(nc.vector.tensor_tensor(rows[:, :, 4:8], rows[:, :, 0:4],
                                             allmax[:, 0:4].unsqueeze(1).to_broadcast([P, NTP, 4]), ALU.add))
                link(nc.vector.scalar_tensor_tensor(rows[:, :, 4:8], rows[:, :, 4:8], 0.2, rows[:, :, 4:8], ALU.mult, ALU.max))
                link(nc.vector.tensor_scalar(rows[:, :, 4:8], rows[:, :, 4:8], -HEADROOM, None, ALU.add))
                count_passes(nc, g, link, allmax)


def stage_l0_mix(nc, g, w_qkv, bn_g, bn_b, w_dw, w_pw, w_res, b_res):
    M = 6
    with ExitStack() as mid:
        def sbm(name, shape, dt=F32):
            return mid.enter_context(nc.sbuf_tensor(name, shape, dt))
        wq = sbm("wq", [P, 2, M * P])
        gam = sbm("bn_gamma", [P, M])
        bet = sbm("bn_beta", [P, M])
        dw = sbm("dw", [P, M])
        pw = sbm("pw", [P, M, 32])
        bd = sbm("bd", [P, M, P])
        wr = sbm("wr", [P, 4, D])
        br = sbm("br", [P, D])

        def ft(i):
            return g.xt[:, :, ds(i * P, P)]

        def two(ap):
            return ap.rearrange("p (c n) -> p c n", c=2)
        s3 = sbm("s3", [P, NTP])
        s4 = sbm("s4", [P, NTP])
        FT_ = 512
        FULL = N // FT_
        REST = N - FULL * FT_
        with stage(nc) as own:
            def sb(name, shape, dt=F32):
                return own.enter_context(nc.sbuf_tensor(name, shape, dt))

            def sem(name):
                return own.enter_context(semaphore(nc, name))
            st6 = sb("st6", [P, M, (FULL + 1) * 6])
            mv = sb("mv6", [P, M, 2])
            tmp = sb("tmp6", [P, M])
            pst = own.enter_context(nc.psum_tensor("ps_bn", [P, M, 512], F32))
            ps_b = own.enter_context(nc.psum_tensor("ps_bd", [P, 512], F32))
            loaded, made, seen, chain, root = sem("wq_loaded"), sem("bn_h"), sem("bn_seen"), sem("bn_chain"), sem("bn_root")
            pw_t, bd0 = sem("pw_spread"), sem("bd_zero")
            own.enter_context(nc.allow_non_contiguous_dma(reason="per channel columns"))
            with nc.Block() as block:
                @block.sync
                def _(sp):
                    sp.dma_start(wq[:, :, :], w_qkv.rearrange("(c p) n -> p c n", p=P)).then_inc(loaded, 16)
                    for t, a in ((gam, bn_g), (bet, bn_b), (dw, w_dw)):
                        sp.dma_start(t[:, :], a.rearrange("(m p) -> p m", p=P)).then_inc(loaded, 16)
                    sp.dma_start(wr[:, :, :], w_res.rearrange("(c p) n -> p c n", p=P)).then_inc(loaded, 16)
                    sp.dma_start(br[:, :], b_res.rearrange("(o n) -> o n", o=1).to_broadcast([P, D])).then_inc(loaded, 16)
                    sp.wait_ge(bd0, 1)
                    for m in range(M):
                        for q in range(4):
                            c = m * P + 32 * q
                            sp.dma_start(bd[32 * q:32 * q + 32, m, 32 * q:32 * q + 32], w_pw[:, c:c + 32]).then_inc(loaded, 16)

                @block.gpsimd
                def _(pool):
                    nc.gpsimd.memset(bd[:, :, :], 0.0).then_inc(bd0, 1)
                    scatter_edges(nc, g, pool, *SCATTERS["moments"])

                @block.tensor
                def _(pe):
                    pe.wait_ge(loaded, 16 * (6 + 4 * M))

                    def tile(at, width, first, turn):
                        for m in range(M):
                            if not first:
                                pe.wait_ge(seen, turn * M + (m + 1 - M))
                            for c in range(2):
                                last = nc.tensor.matmul(pst[:, m, 0:width], wq[:, c, m * P:(m + 1) * P],
                                                        g.xt[:, c, ds(at, width)], start=(c == 0), stop=(c == 1))
                            last.then_inc(made, 1)
                    tile(0, FT_, True, 0)
                    with pe.Fori(1, FULL) as turn:
                        tile(turn * FT_, FT_, False, turn)
                    tile(FULL * FT_, REST, False, FULL)

                @block.scalar
                def _(act):
                    act.wait_ge(root, 1)
                    nc.scalar.activation(tmp[:, :], tmp[:, :], ACT.Sqrt).then_inc(root, 1)

                @block.vector
                def _(dve):
                    link = Chain(dve, chain)

                    def stat(turn, width):
                        for m in range(M):
                            dve.wait_ge(made, turn * M + (m + 1))
                            nc.vector.bn_stats(st6[:, m, ds(turn * 6, 6)], pst[:, m, 0:width]).then_inc(seen, 1)
                    with dve.Fori(0, FULL) as turn:
                        stat(turn, FT_)
                    stat(FULL, REST)
                    dve.wait_ge(seen, (FULL + 1) * M)
                    for m in range(M):
                        link(nc.vector.bn_aggr(mv[:, m, :], st6[:, m, :]))
                    nc.vector.tensor_scalar(tmp[:, :], mv[:, :, 1], 1e-5, None, ALU.add).then_inc(root, 1)
                    dve.wait_ge(root, 2)
                    dve.wait_ge(loaded, 16 * (6 + 4 * M))
                    link(nc.vector.reciprocal(tmp[:, :], tmp[:, :]))
                    link(nc.vector.tensor_tensor(gam[:, :], gam[:, :], tmp[:, :], ALU.mult))
                    link(nc.vector.tensor_tensor(tmp[:, :], mv[:, :, 0], gam[:, :], ALU.mult))
                    link(nc.vector.tensor_tensor(bet[:, :], bet[:, :], tmp[:, :], ALU.subtract))
                    link(nc.vector.tensor_tensor(bd[:, :, :], bd[:, :, :], dw[:, :].unsqueeze(2).to_broadcast([P, M, P]), ALU.mult))
        with stage(nc) as own:
            def sb(name, shape, dt=F32):
                return own.enter_context(nc.sbuf_tensor(name, shape, dt))

            def sem(name):
                return own.enter_context(semaphore(nc, name))
            ut = sb("ut", [P, M, 2 * P])
            junk = sb("junk_sq", [P, 1536])
            qk = sb("qk", [P, 2, 16, 2, 32])
            qs = sb("qs", [P, 16, 32])
            ks = sb("ks", [P, 16])
            v = sb("v_s", [P, 2, 512])
            den = sb("den_v", [P, 512])
            o = sb("o_s", [P, 2, 512])
            ot = sb("ot", [P, 2, 512])
            s2 = sb("s2", [P, 2])
            f2 = sb("f2", [P, 2])
            fr = sb("fr", [P, 2])
            ps_h = own.enter_context(nc.psum_tensor("ps_h", [P, M * 2 * P], F32))
            ps_c = own.enter_context(nc.psum_tensor("ps_cat", [P, 2 * M * P], F32))
            ps_o = own.enter_context(nc.psum_tensor("ps_o", [P, 512], F32))
            ps_g = own.enter_context(nc.psum_tensor("ps_g", [P, 512], F32))
            h_made, u_ready, cat_made, sq_ready = sem("h_made"), sem("u_ready"), sem("cat_made"), sem("sq_ready")
            f2_ready, f_ready, v_ready = sem("f2_ready"), sem("f_ready"), sem("v_ready")
            o_ready, o_turned, ot_ready, g_made, g_kept, chain, s3_ready = (
                sem("o_ready"), sem("o_turned"), sem("ot_ready"), sem("g_made"), sem("g_kept"), sem("mix_chain"), sem("s3_ready"))
            grp = ps_c[:, :].rearrange("p (g s e) -> p g s e", s=3, e=32)
            with nc.Block() as block:
                @block.gpsimd
                def _(pool):
                    scatter_edges(nc, g, pool, *SCATTERS["mix"])

                @block.tensor
                def _(pe):
                    def heads(turn, first):
                        if not first:
                            pe.wait_ge(u_ready, turn * M)
                        for m in range(M):
                            for c in range(2):
                                last = nc.tensor.matmul(ps_h[:, m * 2 * P:(m + 1) * 2 * P], wq[:, c, m * P:(m + 1) * P],
                                                        g.xt[:, c, ds(turn * (2 * P), 2 * P)], start=(c == 0), stop=(c == 1))
                            last.then_inc(h_made, 1)

                    def cat(turn, r, first):
                        i = turn * 2 + r
                        if not (first and r == 0):
                            pe.wait_ge(v_ready, i)
                        for m in range(M):
                            nc.tensor.transpose(ps_c[:, m * P:(m + 1) * P], ut[:, m, r * P:(r + 1) * P], g.ident[:, :])
                        for m in range(M):
                            last = nc.tensor.matmul(ps_c[:, (M + m) * P:(M + m + 1) * P], ut[:, m, r * P:(r + 1) * P],
                                                    bd[:, m, :], start=True, stop=True)
                        last.then_inc(cat_made, 1)

                    def out(turn, r, first):
                        i = turn * 2 + r
                        pe.wait_ge(o_ready, i + 1)
                        if not (first and r == 0):
                            pe.wait_ge(ot_ready, i)
                        for c in range(4):
                            last = nc.tensor.transpose(ps_o[:, c * P:(c + 1) * P], o[:, r, c * P:(c + 1) * P], g.ident[:, :])
                        last.then_inc(o_turned, 1)
                        pe.wait_ge(ot_ready, i + 1)
                        if not (first and r == 0):
                            pe.wait_ge(g_kept, i)
                        for c in range(4):
                            last = nc.tensor.matmul(ps_g[:, 0:D], ot[:, r, c * P:(c + 1) * P], wr[:, c, :],
                                                    start=(c == 0), stop=(c == 3))
                        last.then_inc(g_made, 1)

                    def both(turn, first):
                        heads(turn, first)
                        pe.wait_ge(u_ready, turn * M + M)
                        cat(turn, 0, first)
                        cat(turn, 1, first)
                        out(turn, 0, first)
                        out(turn, 1, first)
                    both(0, True)
                    with pe.Fori(1, HALF2) as turn:
                        both(turn, False)

                @block.scalar
                def _(act):
                    def both(turn, first):
                        if not first:
                            act.wait_ge(cat_made, turn * 2)
                        for m in range(M):
                            act.wait_ge(h_made, turn * M + (m | 1) + 1)
                            nc.scalar.activation(ut[:, m, :], ps_h[:, m * 2 * P:(m + 1) * 2 * P], ACT.Relu,
                                                 bias=bet[:, m:m + 1], scale=gam[:, m:m + 1]).then_inc(u_ready, 1)
                        for r in range(2):
                            i = turn * 2 + r
                            act.wait_ge(cat_made, i + 1)
                            if not (first and r == 0):
                                act.wait_ge(s3_ready, i)
                            nc.scalar.activation(junk[:, :], ps_c[:, :], ACT.Square, accum_out=s2[:, r:r + 1]).then_inc(sq_ready, 1)
                            if not first:
                                act.wait_ge(o_ready, i - 1)
                            nc.scalar.activation(qk[:, r, :, :, :], grp[:, :, 0:2, :], ACT.Relu).then_inc(sq_ready, 1)
                            act.wait_ge(f2_ready, i + 1)
                            nc.scalar.activation(fr[:, r:r + 1], f2[:, r:r + 1], ACT.Sqrt).then_inc(f_ready, 1)
                            act.wait_ge(f_ready, i + 1)
                            nc.scalar.activation(v[:, r, :].rearrange("p (g e) -> p g e", e=32), grp[:, :, 2, :], ACT.Copy,
                                                 scale=fr[:, r:r + 1]).then_inc(v_ready, 1)
                            act.wait_ge(o_ready, i + 1)
                            nc.scalar.activation(junk[:, 0:512], o[:, r, :], ACT.Square, accum_out=s3[:, ds(i, 1)]).then_inc(s3_ready, 1)
                            act.wait_ge(o_turned, i + 1)
                            if not first:
                                act.wait_ge(g_made, i - 1)
                            nc.scalar.copy(ot[:, r, :], ps_o[:, :]).then_inc(ot_ready, 1)
                    both(0, True)
                    with act.Fori(1, HALF2) as turn:
                        both(turn, False)

                @block.vector
                def _(dve):
                    def both(turn, first):
                        for r in range(2):
                            i = turn * 2 + r
                            link = Chain(dve, chain, 8, i)
                            dve.wait_ge(sq_ready, i * 2 + 1)
                            link(nc.vector.tensor_scalar(f2[:, r:r + 1], s2[:, r:r + 1], 1e-30, None, ALU.max))
                            link(nc.vector.reciprocal(f2[:, r:r + 1], f2[:, r:r + 1]))
                            nc.vector.tensor_scalar(f2[:, r:r + 1], f2[:, r:r + 1], ATANH_LIM ** 2, 1.0,
                                                    ALU.mult, ALU.min).then_inc(f2_ready, 1)
                            dve.wait_ge(sq_ready, i * 2 + 2)
                            link(nc.vector.tensor_reduce(ks[:, :], qk[:, r, :, 1, :], AX.X, ALU.add))
                            dve.wait_ge(f2_ready, i + 1)
                            link(nc.vector.tensor_scalar(ks[:, :], ks[:, :], f2[:, r:r + 1], None, ALU.mult))
                            link(nc.vector.tensor_tensor(qs[:, :, :], qk[:, r, :, 0, :],
                                                         ks[:, :].unsqueeze(2).to_broadcast([P, 16, 32]), ALU.mult))
                            dve.wait_ge(v_ready, i + 1)
                            link(nc.vector.tensor_scalar(den[:, :], v[:, r, :], 1e-15, None, ALU.add))
                            link(nc.vector.reciprocal(den[:, :], den[:, :]))
                            if not first:
                                dve.wait_ge(o_turned, i - 1)
                            link(nc.vector.tensor_tensor(den[:, :], den[:, :], v[:, r, :], ALU.mult))
                            nc.vector.tensor_tensor(o[:, r, :].rearrange("p (g e) -> p g e", e=32),
                                                    den[:, :].rearrange("p (g e) -> p g e", e=32),
                                                    qs[:, :, :], ALU.mult).then_inc(o_ready, 1)
                            link.end()
                            dve.wait_ge(g_made, i + 1)
                            nc.vector.tensor_copy(ft(i), two(ps_g[:, 0:D])).then_inc(g_kept, 1)
                    both(0, True)
                    with dve.Fori(1, HALF2) as turn:
                        both(turn, False)
        with stage(nc) as own:
            def sem(name):
                return own.enter_context(semaphore(nc, name))
            junk = own.enter_context(nc.sbuf_tensor("junk4", [P, D], F32))
            f3, f3r, n4, th, chain = sem("f3"), sem("f3r"), sem("n4"), sem("th"), sem("fx_chain")
            ft_ready, sq = sem("ft_ready"), sem("ft_sq")
            with nc.Block() as block:
                @block.gpsimd
                def _(pool):
                    scatter_edges(nc, g, pool, *SCATTERS["ball"])

                @block.vector
                def _(dve):
                    link = Chain(dve, chain)
                    link(nc.vector.tensor_scalar(s3[:, :], s3[:, :], 1e-30, None, ALU.max))
                    link(nc.vector.reciprocal(s3[:, :], s3[:, :]))
                    nc.vector.tensor_scalar(s3[:, :], s3[:, :], ATANH_LIM ** 2, 1.0, ALU.mult, ALU.min).then_inc(f3, 1)
                    dve.wait_ge(f3r, 1)
                    with dve.Fori(0, NTP) as i:
                        row = ft(i)
                        nc.vector.scalar_tensor_tensor(row, row, s3[:, ds(i, 1)], two(br[:, :]), ALU.mult, ALU.add).then_inc(ft_ready, 1)
                    dve.wait_ge(sq, NTP)
                    nc.vector.tensor_scalar(s4[:, :], s4[:, :], 1e-30, None, ALU.max).then_inc(n4, 1)
                    dve.wait_ge(th, 2)
                    link(nc.vector.reciprocal(s4[:, :], s4[:, :]))
                    link(nc.vector.tensor_scalar(s3[:, :], s3[:, :], LIM, None, ALU.min))
                    link(nc.vector.tensor_tensor(s3[:, :], s3[:, :], s4[:, :], ALU.mult))
                    with dve.Fori(0, NTP) as i:
                        row = ft(i)
                        xr = g.x[:, ds(i, 1), :].rearrange("p t (c n) -> p (t c) n", c=2)
                        nc.vector.scalar_tensor_tensor(xr, row, s3[:, ds(i, 1)], xr, ALU.mult, ALU.add)

                @block.scalar
                def _(act):
                    act.wait_ge(f3, 1)
                    nc.scalar.activation(s3[:, :], s3[:, :], ACT.Sqrt).then_inc(f3r, 1)
                    with act.Fori(0, NTP) as i:
                        act.wait_ge(ft_ready, i + 1)
                        nc.scalar.activation(two(junk[:, :]), ft(i), ACT.Square,
                                             accum_out=s4[:, ds(i, 1)]).then_inc(sq, 1)
                        act.wait_ge(sq, i + 1)
                    act.wait_ge(n4, 1)
                    nc.scalar.activation(s4[:, :], s4[:, :], ACT.Sqrt).then_inc(th, 1)
                    act.wait_ge(th, 1)
                    nc.scalar.activation(s3[:, :], s4[:, :], ACT.Tanh).then_inc(th, 1)

SUP = 7
SW = SUP * P
HW = SW // 2
SUPS = NT // SUP
EXPERTS = 8
assert SUPS * SUP == NT and HW <= 512


def stage_add_messages(nc, g, acc, tag, eps_term=None):
    with stage(nc) as own:
        chain = own.enter_context(semaphore(nc, "msg_chain" + tag))
        rden = own.enter_context(nc.sbuf_tensor("rden" + tag, [P, NT, 4], F32))
        a3 = acc[:, :].rearrange("p (t w) -> p t w", w=AW)
        with nc.Block() as block:
            @block.vector
            def _(dve):
                link = Chain(dve, chain)
                link(nc.vector.tensor_scalar(rden[:, :, :], a3[:, 0:NT, 256:AW], 1e-35, None, ALU.max))
                link(nc.vector.reciprocal(rden[:, :, :], rden[:, :, :]))
                for s in range(SUPS):
                    t = slice(s * SUP, (s + 1) * SUP)
                    part = a3[:, t, 0:256].rearrange("p t (h d) -> p t h d", h=4)
                    link(nc.vector.tensor_tensor(part, part, rden[:, t, :].unsqueeze(3).to_broadcast([P, SUP, 4, 64]), ALU.mult))
                    nc.vector.tensor_tensor(g.x[:, t, :], g.x[:, t, :], a3[:, t, 0:256], ALU.add)


def stage_turn(nc, g, tag, fill, width, out=None, table=None, source=None, keep_xt=True, gate=None):
    AT = D
    if source is None:
        def source(i):
            return g.x[:, ds(i, 1), :].rearrange("p t d -> p (t d)")
    with stage(nc) as own:
        def sb(name, shape, dt=F32):
            return own.enter_context(nc.sbuf_tensor(name + tag, shape, dt))

        def sem(name):
            return own.enter_context(semaphore(nc, name + tag))

        def pb(name, shape):
            return own.enter_context(nc.psum_tensor(name + tag, shape, F32))
        wl = sb("wl", [P, 2, width])
        bias = sb("bias_bc", [P, width])
        fill(own, wl, bias)
        xs = sb("xs", [P, 2, D])
        st = sb("st", [P, 2, 2, P])
        row = sb("row", [P, 2, width])
        colmax = sb("colmax", [P, 8])
        allmax = sb("allmax", [P, 8])
        ps_x = pb("ps_x", [P, 2, 512])
        ps_r = pb("ps_r", [P, 2, 512])
        xs_ready, turned, staged, kept = sem("xs_ready"), sem("xs_turned"), sem("xs_staged"), sem("xt_kept")
        rowed, row_ready, written = sem("row_mm"), sem("row_ready"), [sem("row_out0"), sem("row_out1")]
        reduced, maxes, chain = sem("max_reduced"), sem("run_max"), sem("turn_chain")
        with nc.Block() as block:
            if table is not None:
                @block.sync
                def _(sp):
                    def put(turn, r):
                        sp.wait_ge(row_ready, turn * 2 + (r + 1))
                        sp.dma_start(table[ds((turn * 2 + r) * P, P), :], row[:, r, 0:AT + 4]).then_inc(written[r], 16)
                    with sp.Fori(0, HALF2) as turn:
                        put(turn, 0)
                        put(turn, 1)
                    for r in range(2):
                        sp.wait_ge(written[r], 16 * HALF2)

            @block.scalar
            def _(act):
                def stage(turn, r, first):
                    i = turn * 2 + r
                    act.wait_ge(turned, i + 1)
                    if not first:
                        act.wait_ge(rowed, i - 1)
                        if keep_xt:
                            act.wait_ge(kept, i - 1)
                    nc.scalar.copy(st[:, r, :, :].rearrange("p c n -> p (c n)"), ps_x[:, r, 0:256]).then_inc(staged, 1)
                stage(0, 0, True)
                stage(0, 1, True)
                with act.Fori(1, HALF2) as turn:
                    stage(turn, 0, False)
                    stage(turn, 1, False)

            @block.gpsimd
            def _(pool):
                def keep(turn, r):
                    i = turn * 2 + r
                    pool.wait_ge(staged, i + 1)
                    nc.gpsimd.tensor_copy(g.xt[:, :, ds(i * P, P)], st[:, r, :, :]).then_inc(kept, 1)
                if keep_xt:
                    with pool.Fori(0, HALF2) as turn:
                        keep(turn, 0)
                        keep(turn, 1)
                if table is not None:
                    pool.wait_ge(maxes, NTP)
                    nc.gpsimd.partition_all_reduce(allmax[:, :], colmax[:, :], P, bass.bass_isa.ReduceOp.max).then_inc(reduced, 1)

            @block.tensor
            def _(pe):
                def turn_tile(turn, r, first):
                    i = turn * 2 + r
                    pe.wait_ge(xs_ready, i + 1)
                    if not first:
                        pe.wait_ge(staged, i - 1)
                    for c in range(2):
                        last = nc.tensor.transpose(ps_x[:, r, c * P:(c + 1) * P], xs[:, r, c * P:(c + 1) * P], g.ident[:, :])
                    last.then_inc(turned, 1)

                def row_tile(turn, r, first):
                    i = turn * 2 + r
                    pe.wait_ge(staged, i + 1)
                    if not first:
                        pe.wait_ge(row_ready, i - 1)
                    for c in range(2):
                        last = nc.tensor.matmul(ps_r[:, r, 0:width], st[:, r, c, :], wl[:, c, :], start=(c == 0), stop=(c == 1))
                    last.then_inc(rowed, 1)

                def both(turn, first, last=False):
                    for r in range(2):
                        row_tile(turn, r, first)
                        if not last:
                            turn_tile(turn + 1, r, False)
                turn_tile(0, 0, True)
                turn_tile(0, 1, True)
                both(0, True)
                with pe.Fori(1, HALF2 - 1) as turn:
                    both(turn, False)
                both(HALF2 - 1, False, last=True)

            @block.vector
            def _(dve):
                def norm(turn, r, first):
                    i = turn * 2 + r
                    if not first:
                        dve.wait_ge(turned, i - 1)
                    nc.vector.tensor_scalar(xs[:, r, :], source(i),
                                            g.mean[:, ds(i, 1)], g.rstd[:, ds(i, 1)], ALU.subtract, ALU.mult).then_inc(xs_ready, 1)

                def finish(turn, r, first):
                    i = turn * 2 + r
                    dve.wait_ge(rowed, i + 1)
                    if table is None and out is None:
                        nc.vector.tensor_tensor(row[:, r, :], ps_r[:, r, 0:width], bias[:, :], ALU.add).then_inc(row_ready, 1)
                        dve.wait_ge(row_ready, i + 1)
                        xr = g.x[:, ds(i, 1), :].rearrange("p t d -> p (t d)")
                        nc.vector.scalar_tensor_tensor(xr, row[:, r, :], 0.0, xr, ALU.max, ALU.add)
                        return
                    if table is None:
                        nc.vector.tensor_tensor(out[:, ds(i * width, width)], ps_r[:, r, 0:width], bias[:, :],
                                                ALU.add).then_inc(row_ready, 1)
                        return
                    if not first:
                        dve.wait_ge(written[r], turn * 16)
                    if gate is not None:
                        nc.vector.scalar_tensor_tensor(gate[0][:, ds(i * 64, 64)], ps_r[:, r, AT + 8:width], gate[1][:, ds(i, 1)],
                                                       bias[:, AT + 8:width], ALU.mult, ALU.add)
                    nc.vector.tensor_copy(row[:, r, 0:AT + 8], ps_r[:, r, 0:AT + 8]).then_inc(row_ready, 1)
                    dve.wait_ge(row_ready, i + 1)
                    nc.vector.tensor_copy(g.rows[:, ds(i * 8, 4)], row[:, r, AT + 4:AT + 8])
                    if not (first and r == 0):
                        dve.wait_ge(maxes, i)
                    nc.vector.scalar_tensor_tensor(colmax[:, 4:8], row[:, r, AT:AT + 4], -1.0, colmax[:, 4:8], ALU.mult, ALU.max)
                    nc.vector.tensor_tensor(colmax[:, 0:4], colmax[:, 0:4], row[:, r, AT:AT + 4], ALU.max).then_inc(maxes, 1)
                link = Chain(dve, chain)
                link(nc.vector.memset(colmax[:, :], -BIG))
                def both(turn, first, last=False):
                    for r in range(2):
                        if not last:
                            norm(turn + 1, r, False)
                        finish(turn, r, first)
                norm(0, 0, True)
                norm(0, 1, True)
                both(0, True)
                with dve.Fori(1, HALF2 - 1) as turn:
                    both(turn, False)
                both(HALF2 - 1, False, last=True)
                if table is not None:
                    dve.wait_ge(maxes, NTP)
                    dve.wait_ge(reduced, 1)
                    rows = g.rows[:, :].rearrange("p (t c) -> p t c", c=8)
                    link(nc.vector.tensor_tensor(rows[:, :, 4:8], rows[:, :, 0:4],
                                                 allmax[:, 0:4].unsqueeze(1).to_broadcast([P, NTP, 4]), ALU.add))
                    link(nc.vector.scalar_tensor_tensor(rows[:, :, 4:8], rows[:, :, 4:8], 0.2, rows[:, :, 4:8], ALU.mult, ALU.max))
                    link(nc.vector.tensor_scalar(rows[:, :, 4:8], rows[:, :, 4:8], -HEADROOM, None, ALU.add))
                    count_passes(nc, g, link, allmax)


def load_wide(nc, own, tag, pairs, biases=(), bias=None):
    loaded = own.enter_context(semaphore(nc, "wide_loaded" + tag))
    chain = own.enter_context(semaphore(nc, "wide_chain" + tag))
    parts = [own.enter_context(nc.sbuf_tensor(f"wide_part{k}" + tag, [P, b.shape[0]], F32)) for k, b in enumerate(biases)]
    with nc.allow_non_contiguous_dma(reason="columns of weights"), nc.Block() as block:
        @block.sync
        def _(sp):
            for to, of in pairs:
                sp.dma_start(to, of).then_inc(loaded, 16)
            for to, of in zip(parts, biases):
                sp.dma_start(to[:, :], of.rearrange("(o n) -> o n", o=1).to_broadcast([P, of.shape[0]])).then_inc(loaded, 16)
            sp.wait_ge(loaded, 16 * (len(pairs) + len(parts)))

        @block.vector
        def _(dve):
            if bias is not None:
                link = Chain(dve, chain)
                if not parts:
                    nc.vector.memset(bias[:, :], 0.0)
                    return
                dve.wait_ge(loaded, 16 * (len(pairs) + len(parts)))
                link(nc.vector.tensor_copy(bias[:, :], parts[0][:, :]))
                for part in parts[1:]:
                    link(nc.vector.tensor_tensor(bias[:, :], bias[:, :], part[:, :], ALU.add))


def stage_softmax8(nc, g, comb):
    with stage(nc) as own:
        m = own.enter_context(nc.sbuf_tensor("m_soft", [P, NTP], F32))
        chain = own.enter_context(semaphore(nc, "soft_chain"))
        dif, exped = own.enter_context(semaphore(nc, "soft_dif")), own.enter_context(semaphore(nc, "soft_exp"))
        lg = comb[:, :].rearrange("p (t e) -> p t e", e=8)
        wide = m[:, :].unsqueeze(2).to_broadcast([P, NTP, 8])
        with nc.Block() as block:
            @block.vector
            def _(dve):
                link = Chain(dve, chain)
                link(nc.vector.tensor_reduce(m[:, :], lg, AX.X, ALU.max))
                nc.vector.tensor_tensor(lg, lg, wide, ALU.subtract).then_inc(dif, 1)
                dve.wait_ge(exped, 1)
                link(nc.vector.tensor_reduce(m[:, :], lg, AX.X, ALU.add))
                link(nc.vector.reciprocal(m[:, :], m[:, :]))
                link(nc.vector.tensor_tensor(lg, lg, wide, ALU.mult))

            @block.scalar
            def _(act):
                act.wait_ge(dif, 1)
                nc.scalar.activation(lg, lg, ACT.Exp).then_inc(exped, 1)


class ExpertBias:

    def __init__(self, nc, g, own, tag, comb, b_out):
        self.nc, self.g, self.comb, self.b_out = nc, g, comb, b_out
        self.groups = -(-NTP // 16)
        self.bo = own.enter_context(nc.sbuf_tensor("bo" + tag, [P, 4, D], F32))
        self.ct = own.enter_context(nc.sbuf_tensor("ct" + tag, [P, self.groups, P], F32))
        self.ps_t = own.enter_context(nc.psum_tensor("ps_ct" + tag, [P, self.groups * P], F32))
        self.ps_b = own.enter_context(nc.psum_tensor("ps_cb" + tag, [P, 2, 512], F32))
        self.zeroed, self.loaded, self.turned, self.staged, self.made, self.added = (
            own.enter_context(semaphore(nc, n + tag)) for n in ("bo_zero", "bo_in", "c_turned", "c_staged", "cb_made", "cb_added"))

    def load(self, sp):
        sp.wait_ge(self.zeroed, 1)
        for q in range(4):
            for v in range(4):
                at = 32 * q + 8 * v
                sp.dma_start(self.bo[at:at + 8, v, :], self.b_out).then_inc(self.loaded, 16)
        sp.wait_ge(self.loaded, 256)

    def keep(self, act):
        nc, n = self.nc, self.groups
        act.wait_ge(self.turned, n)
        nc.scalar.copy(self.ct[:, 0:n - 1, :].rearrange("p a b -> p (a b)"), self.ps_t[:, 0:(n - 1) * P]).then_inc(self.staged, 1)
        tail = NTP * 8 - (n - 1) * P
        nc.scalar.copy(self.ct[0:tail, n - 1, :], self.ps_t[0:tail, (n - 1) * P:n * P]).then_inc(self.staged, 1)

    def make(self, pe):
        nc = self.nc
        for k in range(self.groups):
            n = min(P, NTP * 8 - k * P)
            nc.tensor.transpose(self.ps_t[0:n, k * P:(k + 1) * P], self.comb[:, k * P:k * P + n], self.g.ident[:, :]).then_inc(self.turned, 1)
        pe.wait_ge(self.staged, 2)
        pe.wait_ge(self.loaded, 256)
        for j in range(HALF2):
            if j >= 2:
                pe.wait_ge(self.added, j - 1)
            for r in range(2):
                t = 2 * j + r
                q, v, rows = (t % 16) // 4, t % 4, 32
                if t // 16 == self.groups - 1:
                    rows = min(32, NTP * 8 - (self.groups - 1) * P - 32 * q)
                last = nc.tensor.matmul(self.ps_b[:, j % 2, r * D:(r + 1) * D], self.ct[32 * q:32 * q + rows, t // 16, :],
                                        self.bo[32 * q:32 * q + rows, v, :], start=True, stop=True)
            last.then_inc(self.made, 1)

    def clear(self):
        self.nc.vector.memset(self.bo[:, :, :], 0.0).then_inc(self.zeroed, 1)

    def add(self, dve, j, bank):
        dve.wait_ge(self.made, j + 1)
        two = self.g.x[:, ds(2 * j, 2), :]
        self.nc.vector.tensor_tensor(two, two, self.ps_b[:, bank, :].rearrange("p (t d) -> p t d", t=2), ALU.add).then_inc(self.added, 1)


def stage_expert_bias(nc, g, tag, comb, b_out):
    with stage(nc) as own:
        bias = ExpertBias(nc, g, own, tag, comb, b_out)
        with nc.Block() as block:
            @block.sync
            def _(sp):
                bias.load(sp)

            @block.scalar
            def _(act):
                bias.keep(act)

            @block.tensor
            def _(pe):
                bias.make(pe)

            @block.vector
            def _(dve):
                bias.clear()
                for j in range(HALF2):
                    bias.add(dve, j, j % 2)

SLOT_TILES = -(-((2 * N + EXPERTS * (P - 1)) // P) // 4) * 4
WIDE_E = 512


def stage_route(nc, g, comb):
    with stage(nc) as own:
        def sb(name, shape, dt=F32):
            return own.enter_context(nc.sbuf_tensor(name, shape, dt))

        def sem(name):
            return own.enter_context(semaphore(nc, name))
        back8 = sb("back8", [P, 8])
        eq = sb("eq8", [P, NTP, 8])
        hot = [sb("first8", [P, NTP, 8]), sb("second8", [P, NTP, 8])]
        m = [g.share[:, 0, :], g.share[:, 1, :]]
        at = sb("at8", [P, NTP])
        member = sb("member8", [P, NTP, 8])
        cum = sb("cum8", [P, NTP, 8])
        zero = sb("zero50", [P, NTP])
        real = sb("real_lane", [P, 1])
        tot_i = sb("tot8_i", [P, 8], I32)
        tiles = sb("tiles8", [P, 8])
        end = sb("end8", [P, 8])
        base = sb("base8", [P, 8])
        end_col = sb("end8_col", [8, P])
        tile_no = sb("slot_tile_no", [8, SLOT_TILES])
        past = sb("past8", [8, SLOT_TILES])
        ps_a = own.enter_context(nc.psum_tensor("ps_route_a", [P, 512], F32))
        ps_t = own.enter_context(nc.psum_tensor("ps_route_t", [P, 512], F32))
        ps_b = own.enter_context(nc.psum_tensor("ps_route_b", [P, 512], F32))
        chain, dif, exped, iotas, counted = sem("top_chain"), sem("top_dif"), sem("top_exp"), sem("route_iota"), sem("counted8")
        sums, ends, turned, past_made, tiles_of = sem("sums8"), sem("ends8"), sem("ends8_turned"), sem("past8_made"), sem("experts_of")
        lg = comb[:, :].rearrange("p (t e) -> p t e", e=8)

        def wide(a):
            return a.unsqueeze(2).to_broadcast([P, NTP, 8])
        with nc.Block() as block:
            @block.gpsimd
            def _(pool):
                nc.gpsimd.iota(tile_no[:, :], pattern=[[1, SLOT_TILES]], base=0, channel_multiplier=0,
                               allow_small_or_imprecise_dtypes=True).then_inc(iotas, 1)

            @block.scalar
            def _(act):
                act.wait_ge(dif, 1)
                nc.scalar.activation(m[1], m[1], ACT.Exp).then_inc(exped, 1)

            @block.tensor
            def _(pe):
                pe.wait_ge(counted, 1)
                nc.tensor.matmul(ps_a[:, 0:8], g.ones[:, :], cum[:, NTP - 1, :], start=True, stop=True)
                nc.tensor.matmul(ps_a[:, 8:16], g.before[:, :], cum[:, NTP - 1, :], start=True, stop=True).then_inc(sums, 1)
                pe.wait_ge(ends, 1)
                nc.tensor.transpose(ps_t[0:8, 0:P], end[:, :], g.ident[:, :]).then_inc(turned, 1)
                pe.wait_ge(past_made, 1)
                nc.tensor.matmul(ps_b[:, 0:SLOT_TILES], g.ones[0:8, :], past[:, :], start=True, stop=True).then_inc(tiles_of, 1)

            @block.vector
            def _(dve):
                link = Chain(dve, chain)
                link(nc.vector.tensor_scalar(back8[:, :], g.iota_row[:, 0:8], -1.0, 8.0, ALU.mult, ALU.add))
                for k in range(2):
                    link(nc.vector.tensor_reduce(m[k], lg, AX.X, ALU.max))
                    link(nc.vector.tensor_tensor(eq[:, :, :], lg, wide(m[k]), ALU.is_equal))
                    back = back8[:, :].unsqueeze(1).to_broadcast([P, NTP, 8])
                    link(nc.vector.tensor_tensor(eq[:, :, :], eq[:, :, :], back, ALU.mult))
                    link(nc.vector.tensor_reduce(at[:, :], eq[:, :, :], AX.X, ALU.max))
                    link(nc.vector.tensor_tensor(hot[k][:, :, :], eq[:, :, :], wide(at[:, :]), ALU.is_equal))
                    if k == 0:
                        link(nc.vector.scalar_tensor_tensor(lg, hot[0][:, :, :], -BIG, lg, ALU.mult, ALU.add))
                nc.vector.tensor_tensor(m[1], m[1], m[0], ALU.subtract).then_inc(dif, 1)
                nc.vector.memset(zero[:, :], 0.0)
                nc.vector.tensor_scalar(real[:, :], g.lane[:, :], float(LAST), None, ALU.is_lt)
                link(nc.vector.tensor_tensor(member[:, :, :], hot[0][:, :, :], hot[1][:, :, :], ALU.add))
                link(nc.vector.memset(member[:, NT:NTP, :], 0.0))
                link(nc.vector.tensor_scalar(member[:, NT - 1, :], member[:, NT - 1, :], real[:, 0:1], None, ALU.mult))
                for e in range(EXPERTS):
                    link(nc.vector.tensor_tensor_scan(cum[:, :, e], member[:, :, e], zero[:, :], 0.0, ALU.add, ALU.add))
                dve.sem_inc(counted, 1)
                dve.wait_ge(sums, 1)
                link(nc.vector.tensor_scalar(tot_i[:, :], ps_a[:, 0:8], float(P - 1), None, ALU.add))
                link(nc.vector.tensor_single_scalar(tot_i[:, :], tot_i[:, :], 7, ALU.logical_shift_right))
                link(nc.vector.tensor_copy(tiles[:, :], tot_i[:, :]))
                link(nc.vector.tensor_tensor_scan(end[:, :], tiles[:, :], zero[:, 0:8], 0.0, ALU.add, ALU.add))
                dve.sem_inc(ends, 1)
                link(nc.vector.tensor_tensor(base[:, :], end[:, :], tiles[:, :], ALU.subtract))
                link(nc.vector.tensor_scalar(base[:, :], base[:, :], float(P), None, ALU.mult))
                link(nc.vector.tensor_tensor(base[:, :], base[:, :], ps_a[:, 8:16], ALU.add))
                link(nc.vector.tensor_tensor(cum[:, :, :], cum[:, :, :], member[:, :, :], ALU.subtract))
                link(nc.vector.tensor_tensor(cum[:, :, :], cum[:, :, :], base[:, :].unsqueeze(1).to_broadcast([P, NTP, 8]), ALU.add))
                for k in range(2):
                    link(nc.vector.tensor_tensor(eq[:, :, :], cum[:, :, :], hot[k][:, :, :], ALU.mult))
                    link(nc.vector.tensor_reduce(at[:, :], eq[:, :, :], AX.X, ALU.add))
                    link(nc.vector.tensor_copy(g.slot[:, k, :], at[:, :]))
                dve.wait_ge(turned, 1)
                dve.wait_ge(iotas, 1)
                link(nc.vector.tensor_copy(end_col[:, :], ps_t[0:8, 0:P]))
                nc.vector.tensor_scalar(past[:, :], tile_no[:, :], end_col[:, 0:1], None, ALU.is_ge).then_inc(past_made, 1)
                dve.wait_ge(tiles_of, 1)
                nc.vector.tensor_scalar(g.tile_expert[:, :], ps_b[0:1, 0:SLOT_TILES], float(EXPERTS - 1), None, ALU.min)
                dve.wait_ge(exped, 1)
                link(nc.vector.tensor_scalar(m[0], m[1], 1.0, None, ALU.add))
                link(nc.vector.reciprocal(m[0], m[0]))
                link(nc.vector.tensor_tensor(m[1], m[1], m[0], ALU.mult))
                link(nc.vector.tensor_tensor(hot[0][:, :, :], hot[0][:, :, :], wide(m[0]), ALU.mult))
                link(nc.vector.tensor_tensor(hot[1][:, :, :], hot[1][:, :, :], wide(m[1]), ALU.mult))
                link(nc.vector.tensor_tensor(lg, hot[0][:, :, :], hot[1][:, :, :], ALU.add))


def stage_send(nc, g, w1, b1, w2, slots_in):
    RING = 4
    TURNS = (NT - 1) // RING
    assert TURNS * RING == NT - 1
    with stage(nc) as own:
        def sem(name):
            return own.enter_context(semaphore(nc, name))
        xn = own.enter_context(nc.sbuf_tensor("xn_send", [P, RING, D], F32))
        st = own.enter_context(nc.sbuf_tensor("slot_send", [P, RING, 2], U32))
        ready, weights = sem("row_to_send"), sem("expert_weights_in")
        sent = [sem(f"row_sent{r}") for r in range(RING)]
        with nc.Block() as block:
            @block.sync
            def _(sp):
                for e in range(EXPERTS):
                    sp.dma_start(g.w1s[:, e * 2:e * 2 + 2, :], w1[e].rearrange("(c p) n -> p c n", p=P)).then_inc(weights, 16)
                    sp.dma_start(g.w2s[:, e * 4:e * 4 + 4, :], w2[e].rearrange("(c p) n -> p c n", p=P)).then_inc(weights, 16)
                    sp.dma_start(g.b1s[:, e, :], b1[e:e + 1, :].to_broadcast([P, WIDE_E])).then_inc(weights, 16)
                sp.wait_ge(weights, 16 * 3 * EXPERTS)
                for r in range(RING):
                    sp.wait_ge(sent[r], 32 * TURNS + (32 if r == 0 else 0))

            @block.vector
            def _(dve):
                def row(turn, r, first):
                    t = turn * RING + r
                    if not first:
                        dve.wait_ge(sent[r], turn * 32)
                    nc.vector.tensor_copy(st[:, r, :].unsqueeze(2), g.slot[:, :, ds(t, 1)]).then_inc(ready, 1)
                    nc.vector.tensor_scalar(xn[:, r, :], g.x[:, ds(t, 1), :].rearrange("p t d -> p (t d)"),
                                            g.mean[:, ds(t, 1)], g.rstd[:, ds(t, 1)], ALU.subtract, ALU.mult).then_inc(ready, 1)
                for r in range(RING):
                    row(0, r, True)
                with dve.Fori(1, TURNS) as turn:
                    for r in range(RING):
                        row(turn, r, False)
                row(TURNS, 0, False)

            @block.gpsimd
            def _(pool):
                def send(turn, r, lanes):
                    pool.wait_ge(ready, turn * (2 * RING) + (2 * r + 2))
                    pool.nop(nofuse=True)
                    for k in range(2):
                        pool.indirect_dma_start(slots_in, bass.IndirectOffsetOnAxis(ap=st[0:lanes, r, k:k + 1], axis=0),
                                                xn[0:lanes, r, :], None).then_inc(sent[r], 16)
                with pool.Fori(0, TURNS) as turn:
                    for r in range(RING):
                        send(turn, r, P)
                send(TURNS, 0, LAST)


def stage_experts(nc, g, slots_in, slots_out):
    RING = 4
    TURNS = SLOT_TILES // RING
    PE_, DVE_ = mybir.EngineType.PE, mybir.EngineType.DVE
    with stage(nc) as own:
        def sb(name, shape, dt=F32):
            return own.enter_context(nc.sbuf_tensor(name, shape, dt))

        def sem(name):
            return own.enter_context(semaphore(nc, name))

        def pb(name):
            return own.enter_context(nc.psum_tensor(name, [P, 2, 512], F32))
        xin = sb("xin_e", [P, RING, D])
        xt = sb("xt_e", [P, 2, 2, P])
        h = sb("h_e", [P, 2, WIDE_E])
        ht = sb("ht_e", [P, 2, 4, P])
        y = sb("y_e", [P, RING, D])
        ps_x, ps_h, ps_ht, ps_y = pb("ps_xe"), pb("ps_he"), pb("ps_hte"), pb("ps_ye")
        loaded = [sem(f"x_in{r}") for r in range(RING)]
        out = [sem(f"y_out{r}") for r in range(RING)]
        x_turned, x_kept, h_made, h_ready = sem("x_turned_e"), sem("x_kept_e"), sem("h_made_e"), sem("h_ready_e")
        h_turned, ht_ready, y_made, y_kept = sem("h_turned_e"), sem("ht_ready_e"), sem("y_made_e"), sem("y_kept_e")

        def later(turn, r, by):
            return turn + (r + by) // RING, (r + by) % RING

        def all_turns(eng, steps):
            def one(turn, first, last):
                for r in range(RING):
                    for by, what in steps:
                        if not last or r + by < RING:
                            t, q = later(turn, r, by)
                            what(t, q, first and r + by < 2, first and r + by < RING)
            for by, what in steps:
                for r in range(by):
                    what(0, r, r < 2, True)
            one(0, True, False)
            with eng.Fori(1, TURNS - 1) as turn:
                one(turn, False, False)
            one(TURNS - 1, False, True)

        def expert_of(i, engine):
            _, values = nc.values_load_multi_w_load_instructions(g.tile_expert[0:1, ds(i, 1)], engines=(engine,),
                                                                 min_val=0, max_val=EXPERTS - 1)
            return values[0]
        with nc.Block() as block:
            @block.sync
            def _(sp):
                def load(turn, r, new, first):
                    j = turn * RING + r
                    if not first:
                        sp.wait_ge(x_turned, j - (RING - 1))
                    sp.dma_start(xin[:, r, :], slots_in[ds(j * P, P), :]).then_inc(loaded[r], 16)
                all_turns(sp, [(0, load)])

            @block.gpsimd
            def _(pool):
                def put(turn, r, new, first):
                    j = turn * RING + r
                    pool.wait_ge(y_kept, j + 1)
                    pool.dma_start(slots_out[ds(j * P, P), :], y[:, r, :]).then_inc(out[r], 16)
                all_turns(pool, [(0, put)])
                for r in range(RING):
                    pool.wait_ge(out[r], 16 * TURNS)

            @block.tensor
            def _(pe):
                def turn_x(turn, r, new, first):
                    j = turn * RING + r
                    pe.wait_ge(loaded[r], turn * 16 + 16)
                    if not new:
                        pe.wait_ge(x_kept, j - 1)
                    for c in range(2):
                        last = nc.tensor.transpose(ps_x[:, r % 2, c * P:(c + 1) * P], xin[:, r, c * P:(c + 1) * P], g.ident[:, :])
                    last.then_inc(x_turned, 1)

                def widen(turn, r, new, first):
                    j = turn * RING + r
                    e = expert_of(j, PE_)
                    pe.wait_ge(x_kept, j + 1)
                    if not new:
                        pe.wait_ge(h_ready, j - 1)
                    for c in range(2):
                        last = nc.tensor.matmul(ps_h[:, r % 2, :], xt[:, r % 2, c, :],
                                                g.w1s[:, :, :].rearrange("p a n -> p (a n)")[:, ds(e * (2 * WIDE_E) + c * WIDE_E, WIDE_E)],
                                                start=(c == 0), stop=(c == 1))
                    last.then_inc(h_made, 1)

                def turn_h(turn, r, new, first):
                    j = turn * RING + r
                    pe.wait_ge(h_ready, j + 1)
                    if not new:
                        pe.wait_ge(ht_ready, j - 1)
                    for c in range(4):
                        last = nc.tensor.transpose(ps_ht[:, r % 2, c * P:(c + 1) * P], h[:, r % 2, c * P:(c + 1) * P], g.ident[:, :])
                    last.then_inc(h_turned, 1)

                def narrow(turn, r, new, first):
                    j = turn * RING + r
                    e = expert_of(j, PE_)
                    pe.wait_ge(ht_ready, j + 1)
                    if not new:
                        pe.wait_ge(y_kept, j - 1)
                    for c in range(4):
                        last = nc.tensor.matmul(ps_y[:, r % 2, 0:D], ht[:, r % 2, c, :],
                                                g.w2s[:, :, :].rearrange("p a n -> p (a n)")[:, ds(e * (4 * D) + c * D, D)],
                                                start=(c == 0), stop=(c == 3))
                    last.then_inc(y_made, 1)
                all_turns(pe, [(3, turn_x), (2, widen), (1, turn_h), (0, narrow)])

            @block.scalar
            def _(act):
                def keep_x(turn, r, new, first):
                    j = turn * RING + r
                    act.wait_ge(x_turned, j + 1)
                    if not new:
                        act.wait_ge(h_made, j - 1)
                    nc.scalar.copy(xt[:, r % 2, :, :].rearrange("p c n -> p (c n)"), ps_x[:, r % 2, 0:D]).then_inc(x_kept, 1)

                def relu(turn, r, new, first):
                    j = turn * RING + r
                    act.wait_ge(h_turned, j + 1)
                    if not new:
                        act.wait_ge(y_made, j - 1)
                    nc.scalar.activation(ht[:, r % 2, :, :].rearrange("p c n -> p (c n)"), ps_ht[:, r % 2, :], ACT.Relu).then_inc(ht_ready, 1)
                all_turns(act, [(3, keep_x), (1, relu)])

            @block.vector
            def _(dve):
                def bias(turn, r, new, first):
                    j = turn * RING + r
                    e = expert_of(j, DVE_)
                    dve.wait_ge(h_made, j + 1)
                    if not new:
                        dve.wait_ge(h_turned, j - 1)
                    nc.vector.tensor_tensor(h[:, r % 2, :], ps_h[:, r % 2, :],
                                            g.b1s[:, :, :].rearrange("p a n -> p (a n)")[:, ds(e * WIDE_E, WIDE_E)], ALU.add).then_inc(h_ready, 1)

                def keep_y(turn, r, new, first):
                    j = turn * RING + r
                    dve.wait_ge(y_made, j + 1)
                    if not first:
                        dve.wait_ge(out[r], turn * 16)
                    nc.vector.tensor_copy(y[:, r, :], ps_y[:, r % 2, 0:D]).then_inc(y_kept, 1)
                all_turns(dve, [(2, bias), (0, keep_y)])


def stage_collect(nc, g, comb, b2, slots_out):
    RING = 4
    TURNS = (NT - 1) // RING
    with stage(nc) as own:
        def sem(name):
            return own.enter_context(semaphore(nc, name))
        got = own.enter_context(nc.sbuf_tensor("got_y", [P, RING, 2, D], F32))
        st = own.enter_context(nc.sbuf_tensor("slot_back", [P, RING, 2], U32))
        bias = ExpertBias(nc, g, own, "_1", comb, b2)
        ready, added = sem("slots_ready"), sem("y_added")
        back = [sem(f"y_back{r}") for r in range(RING)]
        with nc.Block() as block:
            @block.sync
            def _(sp):
                bias.load(sp)

            @block.scalar
            def _(act):
                bias.keep(act)

            @block.tensor
            def _(pe):
                bias.make(pe)

            @block.gpsimd
            def _(pool):
                def fetch(turn, r, lanes):
                    pool.wait_ge(ready, turn * RING + (r + 1))
                    pool.nop(nofuse=True)
                    for k in range(2):
                        pool.indirect_dma_start(got[0:lanes, r, k, :], None, slots_out,
                                                bass.IndirectOffsetOnAxis(ap=st[0:lanes, r, k:k + 1], axis=0)).then_inc(back[r], 16)
                with pool.Fori(0, TURNS) as turn:
                    for r in range(RING):
                        fetch(turn, r, P)
                fetch(TURNS, 0, LAST)

            @block.vector
            def _(dve):
                def slots(turn, r):
                    nc.vector.tensor_copy(st[:, r, :].unsqueeze(2), g.slot[:, :, ds(turn * RING + r, 1)]).then_inc(ready, 1)

                def add(turn, r, lanes):
                    t = turn * RING + r
                    dve.wait_ge(back[r], turn * 32 + 32)
                    xr = g.x[0:lanes, ds(t, 1), :].rearrange("p t d -> p (t d)")
                    for k in range(2):
                        nc.vector.scalar_tensor_tensor(xr, got[0:lanes, r, k, :], g.share[0:lanes, k, ds(t, 1)], xr,
                                                       ALU.mult, ALU.add).then_inc(added, 1)
                        dve.wait_ge(added, t * 2 + (k + 1))
                bias.clear()
                for r in range(RING):
                    slots(0, r)
                with dve.Fori(0, TURNS - 1) as turn:
                    for r in range(RING):
                        add(turn, r, P)
                        slots(turn + 1, r)
                        if r % 2:
                            bias.add(dve, turn * (RING // 2) + r // 2, r // 2)
                            dve.wait_ge(bias.added, turn * (RING // 2) + (r // 2 + 1))
                for r in range(RING):
                    add(TURNS - 1, r, P)
                    if r == 0:
                        slots(TURNS, 0)
                    if r % 2:
                        bias.add(dve, (TURNS - 1) * (RING // 2) + r // 2, r // 2)
                add(TURNS, 0, LAST)
                bias.add(dve, HALF2 - 1, 0)


def fill_l1(nc, w, w_t, attn, gamma, beta, wg1, bg1):
    def fill(own, wl, bias):
        def sb(name, shape, dt=F32):
            return own.enter_context(nc.sbuf_tensor(name, shape, dt))

        def sem(name):
            return own.enter_context(semaphore(nc, name))
        wt = sb("wt1", [P, 2, 256])
        a = sb("a1", [P, 2, 8])
        gam = sb("gam1", [P, 2])
        bet = sb("bet1", [P, 2])
        bet_w = sb("bet_wide1", [P, 2, P])
        g1 = sb("g1raw", [P, 2, 64])
        bg = sb("bg1_bc", [P, 64])
        psa = own.enter_context(nc.psum_tensor("ps_a1", [P, 2, 512], F32))
        psb = own.enter_context(nc.psum_tensor("ps_b1", [P, 512], F32))
        zero, loaded, made, biased, wide = sem("a1_zero"), sem("l1_loaded"), sem("a1_made"), sem("b1_made"), sem("bet_spread")
        with nc.allow_non_contiguous_dma(reason="columns of weights"), nc.Block() as block:
            @block.sync
            def _(sp):
                sp.dma_start(wl[:, :, 0:D], w.rearrange("(c p) n -> p c n", p=P)).then_inc(loaded, 16)
                sp.dma_start(wt[:, :, :], w_t.rearrange("(c p) n -> p c n", p=P)).then_inc(loaded, 16)
                sp.dma_start(g1[:, :, :], wg1.rearrange("(c p) n -> p c n", p=P)).then_inc(loaded, 16)
                sp.dma_start(gam[:, :], gamma.rearrange("(c p) -> p c", p=P)).then_inc(loaded, 16)
                sp.dma_start(bet[:, :], beta.rearrange("(c p) -> p c", p=P)).then_inc(loaded, 16)
                sp.dma_start(bg[:, :], bg1.rearrange("(o n) -> o n", o=1).to_broadcast([P, 64])).then_inc(loaded, 16)
                sp.wait_ge(zero, 1)
                for h in range(4):
                    at = 64 * (h % 2)
                    sp.dma_start(a[at:at + 64, h // 2, h:h + 1], attn[h:h + 1, 64:128].rearrange("o d -> d o")).then_inc(loaded, 16)
                    sp.dma_start(a[at:at + 64, h // 2, 4 + h:5 + h], attn[h:h + 1, 0:64].rearrange("o d -> d o")).then_inc(loaded, 16)
                sp.wait_ge(loaded, 16 * 14)

            @block.tensor
            def _(pe):
                pe.wait_ge(loaded, 16 * 14)
                for c in range(2):
                    for j in range(2):
                        last = nc.tensor.matmul(psa[:, c, 0:8], wt[:, j, c * P:(c + 1) * P], a[:, j, :], start=(j == 0), stop=(j == 1))
                    last.then_inc(made, 1)
                pe.wait_ge(wide, 2)
                for c in range(2):
                    last = nc.tensor.matmul(psb[:, 0:64], bet_w[:, c, :], g1[:, c, :], start=(c == 0), stop=(c == 1))
                last.then_inc(biased, 1)

            @block.vector
            def _(dve):
                nc.vector.memset(a[:, :, :], 0.0).then_inc(zero, 1)
                nc.vector.memset(bias[:, 0:264], 0.0)
                dve.wait_ge(loaded, 16 * 14)
                for c in range(2):
                    nc.vector.tensor_copy(bet_w[:, c, :], bet[:, c:c + 1].to_broadcast([P, P])).then_inc(wide, 1)
                    nc.vector.tensor_scalar(wl[:, c, 264:328], g1[:, c, :], gam[:, c:c + 1], None, ALU.mult)
                dve.wait_ge(made, 2)
                nc.vector.tensor_copy(wl[:, :, D:264], psa[:, :, 0:8])
                dve.wait_ge(biased, 1)
                nc.vector.tensor_tensor(bias[:, 264:328], psb[:, 0:64], bg[:, :], ALU.add)
    return fill


def fill_folded(nc, gamma, beta, w, b):
    def fill(own, wl, bias):
        def sb(name, shape, dt=F32):
            return own.enter_context(nc.sbuf_tensor(name, shape, dt))

        def sem(name):
            return own.enter_context(semaphore(nc, name))
        raw = sb("w_raw", [P, 2, D])
        gam = sb("gam_f", [P, 2])
        bet = sb("bet_f", [P, 2])
        bet_w = sb("bet_wide_f", [P, 2, P])
        bb = sb("b_bc_f", [P, D])
        psb = own.enter_context(nc.psum_tensor("ps_bf", [P, 512], F32))
        loaded, biased, wide = sem("f_loaded"), sem("f_biased"), sem("f_spread")
        with nc.allow_non_contiguous_dma(reason="columns of weights"), nc.Block() as block:
            @block.sync
            def _(sp):
                sp.dma_start(raw[:, :, :], w.rearrange("(c p) n -> p c n", p=P)).then_inc(loaded, 16)
                sp.dma_start(gam[:, :], gamma.rearrange("(c p) -> p c", p=P)).then_inc(loaded, 16)
                sp.dma_start(bet[:, :], beta.rearrange("(c p) -> p c", p=P)).then_inc(loaded, 16)
                sp.dma_start(bb[:, :], b.rearrange("(o n) -> o n", o=1).to_broadcast([P, D])).then_inc(loaded, 16)
                sp.wait_ge(loaded, 64)

            @block.tensor
            def _(pe):
                pe.wait_ge(loaded, 64)
                pe.wait_ge(wide, 2)
                for c in range(2):
                    last = nc.tensor.matmul(psb[:, 0:D], bet_w[:, c, :], raw[:, c, :], start=(c == 0), stop=(c == 1))
                last.then_inc(biased, 1)

            @block.vector
            def _(dve):
                dve.wait_ge(loaded, 64)
                for c in range(2):
                    nc.vector.tensor_copy(bet_w[:, c, :], bet[:, c:c + 1].to_broadcast([P, P])).then_inc(wide, 1)
                    nc.vector.tensor_scalar(wl[:, c, :], raw[:, c, :], gam[:, c:c + 1], None, ALU.mult)
                dve.wait_ge(biased, 1)
                nc.vector.tensor_tensor(bias[:, :], psb[:, 0:D], bb[:, :], ALU.add)
    return fill


def stage_second_norm(nc, g, rstd2):
    with stage(nc) as own:
        chain, rooted = own.enter_context(semaphore(nc, "n2_chain")), own.enter_context(semaphore(nc, "n2_root"))
        with nc.Block() as block:
            @block.vector
            def _(dve):
                link = Chain(dve, chain)
                link(nc.vector.tensor_tensor(rstd2[:, :], g.rstd[:, :], g.rstd[:, :], ALU.mult))
                link(nc.vector.tensor_tensor(rstd2[:, :], rstd2[:, :], g.var[:, :], ALU.mult))
                link(nc.vector.tensor_scalar(rstd2[:, :], rstd2[:, :], 1e-5, None, ALU.add))
                dve.wait_ge(rooted, 1)
                link(nc.vector.reciprocal(rstd2[:, :], rstd2[:, :]))

            @block.scalar
            def _(act):
                act.wait_ge(chain, 3)
                nc.scalar.activation(rstd2[:, :], rstd2[:, :], ACT.Sqrt).then_inc(rooted, 1)


def stage_l1_mix(nc, g, hg, w_qkv, wq_t, w_proj, b_proj, wg2, bg2):
    FT_ = 512
    FULL = N // FT_
    REST = N - FULL * FT_
    with ExitStack() as mid:
        def sbm(name, shape, dt=F32):
            return mid.enter_context(nc.sbuf_tensor(name, shape, dt))
        wkv = sbm("wkv", [P, 2, 512])
        wqt = sbm("wqt", [P, 2, D])
        wp = sbm("wp", [P, 2, D])
        wg = sbm("wg2", [65, D])
        bp = sbm("bp", [P, D])
        kbc = sbm("kbc", [P, D])
        wqc = sbm("wqc", [P, 2, D])
        with stage(nc) as own:
            def sb(name, shape, dt=F32):
                return own.enter_context(nc.sbuf_tensor(name, shape, dt))

            def sem(name):
                return own.enter_context(semaphore(nc, name))
            km = sb("km", [P, 2, FULL + 1])
            kcol = sb("kcol", [P, 2])
            kwide = sb("kwide", [P, 2, P])
            pst = own.enter_context(nc.psum_tensor("ps_k", [P, 4, 512], F32))
            psb = own.enter_context(nc.psum_tensor("ps_kb", [P, 512], F32))
            loaded, made, seen, wide, spread = sem("mix_loaded"), sem("k_made"), sem("k_seen"), sem("k_wide"), sem("k_spread")
            chain, gelued = sem("k_chain"), sem("gelued")
            with nc.allow_non_contiguous_dma(reason="row of bias"), nc.Block() as block:
                @block.sync
                def _(sp):
                    sp.dma_start(wkv[:, :, :], w_qkv[:, D:3 * D].rearrange("(c p) n -> p c n", p=P)).then_inc(loaded, 16)
                    sp.dma_start(wqt[:, :, :], wq_t.rearrange("(c p) n -> p c n", p=P)).then_inc(loaded, 16)
                    sp.dma_start(wp[:, :, :], w_proj.rearrange("(c p) n -> p c n", p=P)).then_inc(loaded, 16)
                    sp.dma_start(wg[0:64, :], wg2).then_inc(loaded, 16)
                    sp.dma_start(wg[64:65, :], bg2.rearrange("(o n) -> o n", o=1)).then_inc(loaded, 16)
                    sp.dma_start(bp[:, :], b_proj.rearrange("(o n) -> o n", o=1).to_broadcast([P, D])).then_inc(loaded, 16)
                    sp.wait_ge(loaded, 96)

                @block.scalar
                def _(act):
                    nc.scalar.activation(hg[:, :], hg[:, :], ACT.Gelu)

                @block.tensor
                def _(pe):
                    pe.wait_ge(loaded, 96)

                    def tile(turn, width, first):
                        for m in range(2):
                            if not first:
                                pe.wait_ge(seen, turn * 2 + (m - 1))
                            for c in range(2):
                                last = nc.tensor.matmul(pst[:, m, 0:width], wkv[:, c, m * P:(m + 1) * P],
                                                        g.xt[:, c, ds(turn * FT_, width)], start=(c == 0), stop=(c == 1))
                            last.then_inc(made, 1)
                    tile(0, FT_, True)
                    with pe.Fori(1, FULL) as turn:
                        tile(turn, FT_, False)
                    tile(FULL, REST, False)
                    pe.wait_ge(wide, 2)
                    for m in range(2):
                        last = nc.tensor.matmul(psb[:, m * P:(m + 1) * P], kwide[:, m, :], g.ident[:, :], start=True, stop=True)
                    last.then_inc(spread, 1)

                @block.vector
                def _(dve):
                    def peak(turn, width):
                        for m in range(2):
                            dve.wait_ge(made, turn * 2 + (m + 1))
                            nc.vector.tensor_reduce(km[:, m, ds(turn, 1)], pst[:, m, 0:width], AX.X, ALU.max).then_inc(seen, 1)
                    with dve.Fori(0, FULL) as turn:
                        peak(turn, FT_)
                    peak(FULL, REST)
                    dve.wait_ge(seen, 2 * FULL + 2)
                    link = Chain(dve, chain)
                    link(nc.vector.tensor_reduce(kcol[:, :], km[:, :, :], AX.X, ALU.max))
                    for m in range(2):
                        nc.vector.tensor_copy(kwide[:, m, :], kcol[:, m:m + 1].to_broadcast([P, P])).then_inc(wide, 1)
                    dve.wait_ge(loaded, 96)
                    nc.vector.tensor_tensor(g.x[:, :, :], g.x[:, :, :], bp[:, :].unsqueeze(1).to_broadcast([P, NTP, D]), ALU.add)
                    dve.wait_ge(spread, 1)
                    nc.vector.tensor_copy(kbc[:, :], psb[:, 0:D])
        with stage(nc) as own:
            def sb(name, shape, dt=F32):
                return own.enter_context(nc.sbuf_tensor(name, shape, dt))

            def sem(name):
                return own.enter_context(semaphore(nc, name))
            st = sb("st_c", [P, 2, 2, P])
            kd = sb("kd", [P, 2, D])
            ke = sb("ke", [P, 2, D])
            vv = sb("vv", [P, 2, 2, P + 1])
            mask = sb("head_mask", [P, P])
            rk = sb("rk", [P, 2])
            cx = sb("cx", [P, 2, P])
            ps_kv = own.enter_context(nc.psum_tensor("ps_kv", [P, 2, 512], F32))
            ps_c = own.enter_context(nc.psum_tensor("ps_ctx", [P, 2, 512], F32))
            ps_w = own.enter_context(nc.psum_tensor("ps_wqc", [P, 2, 512], F32))
            staged, made, kd_ready, ke_ready, vv_ready, used = sem("c_staged"), sem("kv_made"), sem("kd_ready"), sem("ke_ready"), sem("vv_ready"), sem("kv_used")
            masked, chain, cxs, wqcs = sem("masked"), sem("cx_chain"), sem("cx_ready"), sem("wqc_made")
            TURNS = (NT - 1) // 2
            with nc.Block() as block:
                @block.gpsimd
                def _(pool):
                    nc.gpsimd.memset(vv[:, :, :, P:P + 1], 1.0).then_inc(masked, 1)
                    pool.wait_ge(masked, 1)

                    def stage(i, r, first):
                        if not first:
                            pool.wait_ge(made, i - 1)
                        nc.gpsimd.tensor_copy(st[:, r, :, :], g.xt[:, :, ds(i * P, P)]).then_inc(staged, 1)
                    stage(0, 0, True)
                    stage(1, 1, True)
                    with pool.Fori(1, TURNS) as turn:
                        stage(turn * 2, 0, False)
                        stage(turn * 2 + 1, 1, False)
                    stage(NT - 1, 0, False)

                @block.tensor
                def _(pe):
                    def keys(i, r, first):
                        pe.wait_ge(staged, i + 1)
                        if not first:
                            pe.wait_ge(vv_ready, i - 1)
                            pe.wait_ge(kd_ready, i - 1)
                        for c in range(2):
                            last = nc.tensor.matmul(ps_kv[:, r, :], st[:, r, c, :], wkv[:, c, :], start=(c == 0), stop=(c == 1))
                        last.then_inc(made, 1)

                    def context(i, r, first, last_one):
                        pe.wait_ge(ke_ready, i + 1)
                        pe.wait_ge(vv_ready, i + 1)
                        n = LAST if last_one else P
                        for m in range(2):
                            last = nc.tensor.matmul(ps_c[:, m, 0:P + 1], ke[0:n, r, m * P:(m + 1) * P], vv[0:n, r, m, :],
                                                    start=first, stop=last_one)
                        last.then_inc(used, 1)
                    keys(0, 0, True)
                    keys(1, 1, True)
                    context(0, 0, True, False)
                    context(1, 1, False, False)
                    with pe.Fori(1, TURNS) as turn:
                        keys(turn * 2, 0, False)
                        keys(turn * 2 + 1, 1, False)
                        context(turn * 2, 0, False, False)
                        context(turn * 2 + 1, 1, False, False)
                    keys(NT - 1, 0, False)
                    context(NT - 1, 0, False, True)
                    pe.wait_ge(cxs, 2)
                    for c in range(2):
                        for m in range(2):
                            nc.tensor.matmul(ps_w[:, c, m * P:(m + 1) * P], wqt[:, m, c * P:(c + 1) * P], cx[:, m, :],
                                             start=True, stop=True).then_inc(wqcs, 1)

                @block.scalar
                def _(act):
                    def step(i, r, first):
                        act.wait_ge(kd_ready, i + 1)
                        if not first:
                            act.wait_ge(used, i - 1)
                        nc.scalar.activation(ke[:, r, :], kd[:, r, :], ACT.Exp).then_inc(ke_ready, 1)
                    step(0, 0, True)
                    step(1, 1, True)
                    with act.Fori(1, TURNS) as turn:
                        step(turn * 2, 0, False)
                        step(turn * 2 + 1, 1, False)
                    step(NT - 1, 0, False)

                @block.vector
                def _(dve):
                    def step(i, r, first):
                        dve.wait_ge(made, i + 1)
                        if not first:
                            dve.wait_ge(ke_ready, i - 1)
                        nc.vector.tensor_tensor(kd[:, r, :], ps_kv[:, r, 0:D], kbc[:, :], ALU.subtract).then_inc(kd_ready, 1)
                        if not first:
                            dve.wait_ge(used, i - 1)
                        nc.vector.tensor_copy(vv[:, r, :, 0:P], ps_kv[:, r, D:2 * D].rearrange("p (m n) -> p m n", m=2)).then_inc(vv_ready, 1)
                    link = Chain(dve, chain)
                    dve.wait_ge(masked, 1)
                    link(nc.vector.memset(mask[:, :], 0.0))
                    for q in range(4):
                        link(nc.vector.memset(mask[32 * q:32 * q + 32, 32 * q:32 * q + 32], 1.0))
                    step(0, 0, True)
                    step(1, 1, True)
                    with dve.Fori(1, TURNS) as turn:
                        step(turn * 2, 0, False)
                        step(turn * 2 + 1, 1, False)
                    step(NT - 1, 0, False)
                    dve.wait_ge(used, NT)
                    link(nc.vector.reciprocal(rk[:, :], ps_c[:, :, P]))
                    for m in range(2):
                        nc.vector.scalar_tensor_tensor(cx[:, m, :], ps_c[:, m, 0:P], rk[:, m:m + 1], mask[:, :], ALU.mult, ALU.mult).then_inc(cxs, 1)
                    dve.wait_ge(wqcs, 4)
                    nc.vector.tensor_copy(wqc[:, :, :], ps_w[:, :, 0:D])
        with stage(nc) as own:
            def sb(name, shape, dt=F32):
                return own.enter_context(nc.sbuf_tensor(name, shape, dt))

            def sem(name):
                return own.enter_context(semaphore(nc, name))
            st = sb("st_o", [P, 2, 2, P])
            hs = sb("hs_o", [P, 2, P])
            ht = sb("ht_o", [65, 2, P])
            gate = sb("gate", [P, 2, D])
            og = sb("og", [P, 2, D])
            ogt = sb("ogt", [P, 2, D])
            ps_o = own.enter_context(nc.psum_tensor("ps_out", [P, 512], F32))
            ps_t = own.enter_context(nc.psum_tensor("ps_ht", [P, 512], F32))
            ps_g = own.enter_context(nc.psum_tensor("ps_gate", [P, 2, 512], F32))
            ps_r = own.enter_context(nc.psum_tensor("ps_ogt", [P, 2, 512], F32))
            ps_p = own.enter_context(nc.psum_tensor("ps_proj", [P, 2, 512], F32))
            staged, ht_made, ht_ready, out_made, gate_made, gate_ready = sem("o_staged"), sem("ht_made"), sem("ht_ready"), sem("out_made"), sem("gate_made"), sem("gate_ready")
            og_ready, og_turned, ogt_ready, proj, added, ones = sem("og_ready"), sem("og_turned"), sem("ogt_ready"), sem("proj_made"), sem("proj_added"), sem("ones_row")
            with nc.Block() as block:
                @block.gpsimd
                def _(pool):
                    def stage(turn, r, first):
                        i = turn * 2 + r
                        if not first:
                            pool.wait_ge(gate_made, i - 1)
                        nc.gpsimd.tensor_copy(hs[:, r, 0:64], hg[:, ds(i * 64, 64)])
                        nc.gpsimd.tensor_copy(st[:, r, :, :], g.xt[:, :, ds(i * P, P)]).then_inc(staged, 1)
                    nc.gpsimd.memset(hs[:, :, 64:P], 0.0).then_inc(ones, 1)
                    stage(0, 0, True)
                    stage(0, 1, True)
                    with pool.Fori(1, HALF2) as turn:
                        stage(turn, 0, False)
                        stage(turn, 1, False)

                @block.tensor
                def _(pe):
                    def front(turn, r, first):
                        i = turn * 2 + r
                        pe.wait_ge(staged, i + 1)
                        if not (first and r == 0):
                            pe.wait_ge(ht_ready, i)
                        nc.tensor.transpose(ps_t[:, 0:P], hs[:, r, :], g.ident[:, :]).then_inc(ht_made, 1)
                        if not (first and r == 0):
                            pe.wait_ge(og_ready, i)
                        for c in range(2):
                            last = nc.tensor.matmul(ps_o[:, 0:D], st[:, r, c, :], wqc[:, c, :], start=(c == 0), stop=(c == 1))
                        last.then_inc(out_made, 1)
                        pe.wait_ge(ht_ready, i + 1)
                        if not first:
                            pe.wait_ge(gate_ready, i - 1)
                        nc.tensor.matmul(ps_g[:, r, 0:D], ht[:, r, :], wg[:, :], start=True, stop=True).then_inc(gate_made, 1)

                    def turn_back(turn, r, first):
                        i = turn * 2 + r
                        pe.wait_ge(og_ready, i + 1)
                        if not first:
                            pe.wait_ge(ogt_ready, i - 1)
                        for c in range(2):
                            last = nc.tensor.transpose(ps_r[:, r, c * P:(c + 1) * P], og[:, r, c * P:(c + 1) * P], g.ident[:, :])
                        last.then_inc(og_turned, 1)

                    def project(turn, r, first):
                        i = turn * 2 + r
                        pe.wait_ge(ogt_ready, i + 1)
                        if not first:
                            pe.wait_ge(added, i - 1)
                        for c in range(2):
                            last = nc.tensor.matmul(ps_p[:, r, 0:D], ogt[:, r, c * P:(c + 1) * P], wp[:, c, :], start=(c == 0), stop=(c == 1))
                        last.then_inc(proj, 1)

                    def both(turn, first, last=False):
                        for r in range(2):
                            turn_back(turn, r, first)
                            if not last:
                                front(turn + 1, r, False)
                            project(turn, r, first)
                    pe.wait_ge(ones, 2)
                    front(0, 0, True)
                    front(0, 1, True)
                    both(0, True)
                    with pe.Fori(1, HALF2 - 1) as turn:
                        both(turn, False)
                    both(HALF2 - 1, False, last=True)

                @block.scalar
                def _(act):
                    def front(turn, r, first):
                        i = turn * 2 + r
                        act.wait_ge(ht_made, i + 1)
                        if not first:
                            act.wait_ge(gate_made, i - 1)
                        nc.scalar.copy(ht[0:64, r, :], ps_t[0:64, 0:P]).then_inc(ht_ready, 1)
                        act.wait_ge(gate_made, i + 1)
                        if not first:
                            act.wait_ge(og_ready, i - 1)
                        nc.scalar.activation(gate[:, r, :], ps_g[:, r, 0:D], ACT.Sigmoid).then_inc(gate_ready, 1)

                    def back(turn, r, first):
                        i = turn * 2 + r
                        act.wait_ge(og_turned, i + 1)
                        if not first:
                            act.wait_ge(proj, i - 1)
                        nc.scalar.copy(ogt[:, r, :], ps_r[:, r, 0:D]).then_inc(ogt_ready, 1)

                    def both(turn, first, last=False):
                        for r in range(2):
                            back(turn, r, first)
                            if not last:
                                front(turn + 1, r, False)
                    front(0, 0, True)
                    front(0, 1, True)
                    both(0, True)
                    with act.Fori(1, HALF2 - 1) as turn:
                        both(turn, False)
                    both(HALF2 - 1, False, last=True)

                @block.vector
                def _(dve):
                    nc.vector.memset(ht[64:65, :, :], 1.0).then_inc(ones, 1)

                    def gated(turn, r, first):
                        i = turn * 2 + r
                        dve.wait_ge(gate_ready, i + 1)
                        dve.wait_ge(out_made, i + 1)
                        if not first:
                            dve.wait_ge(og_turned, i - 1)
                        nc.vector.tensor_tensor(og[:, r, :], ps_o[:, 0:D], gate[:, r, :], ALU.mult).then_inc(og_ready, 1)

                    def add(turn, r):
                        i = turn * 2 + r
                        dve.wait_ge(proj, i + 1)
                        xr = g.x[:, ds(i, 1), :].rearrange("p t d -> p (t d)")
                        nc.vector.tensor_tensor(xr, xr, ps_p[:, r, 0:D], ALU.add).then_inc(added, 1)
                    gated(0, 0, True)
                    gated(0, 1, True)
                    with dve.Fori(0, HALF2 - 1) as turn:
                        for r in range(2):
                            gated(turn + 1, r, False)
                            add(turn, r)
                    add(HALF2 - 1, 0)
                    add(HALF2 - 1, 1)


def stage_l1_messages(nc, g, acc, top, table):
    with stage(nc) as own:
        def sb(name, shape, dt=F32):
            return own.enter_context(nc.sbuf_tensor(name, shape, dt))

        def sem(name):
            return own.enter_context(semaphore(nc, name))
        gm = sb("gm", [P, 4])
        ga = sb("ga", [P, 4])
        ex = sb("ex", [P, NT, 4])
        wh = sb("wh", [P, 2, SUP, D])
        a3 = acc[:, :].rearrange("p (t w) -> p t w", w=AW)
        rows = g.rows[:, :].rearrange("p (t c) -> p t c", c=8)
        chain, peak, reduced, low, exped = sem("l1m_chain"), sem("peak"), sem("peak_all"), sem("ex_in"), sem("ex_out")
        wh_in, wh_used = [sem("wh_in0"), sem("wh_in1")], sem("wh_used")
        with nc.Block() as block:
            @block.sync
            def _(sp):
                for s in range(SUPS):
                    if s >= 2:
                        sp.wait_ge(wh_used, s - 1)
                    sp.dma_start(wh[:, s % 2, :, :], table[s * SW:(s + 1) * SW, 0:D].rearrange("(t p) d -> p t d", p=P)).then_inc(wh_in[s % 2], 16)

            @block.gpsimd
            def _(pool):
                pool.wait_ge(peak, 1)
                nc.gpsimd.partition_all_reduce(ga[:, :], gm[:, :], P, bass.bass_isa.ReduceOp.max).then_inc(reduced, 1)

            @block.scalar
            def _(act):
                act.wait_ge(low, 1)
                nc.scalar.activation(ex[:, :, :], ex[:, :, :], ACT.Exp).then_inc(exped, 1)

            @block.vector
            def _(dve):
                link = Chain(dve, chain)
                nc.vector.tensor_reduce(gm[:, :], top[:, :, :].rearrange("p k h -> p h k"), AX.X, ALU.max).then_inc(peak, 1)
                dve.wait_ge(reduced, 1)
                link(nc.vector.scalar_tensor_tensor(ga[:, :], ga[:, :], 0.2, ga[:, :], ALU.mult, ALU.max))
                link(nc.vector.tensor_tensor(ex[:, :, :], ga[:, :].unsqueeze(1).to_broadcast([P, NT, 4]), rows[:, 0:NT, 4:8], ALU.subtract))
                nc.vector.tensor_scalar(ex[:, :, :], ex[:, :, :], math.log(1e-15), 88.0, ALU.add, ALU.min).then_inc(low, 1)
                dve.wait_ge(exped, 1)
                link(nc.vector.tensor_tensor(ex[:, :, :], ex[:, :, :], a3[:, 0:NT, 256:AW], ALU.add))
                link(nc.vector.tensor_scalar(ex[:, :, :], ex[:, :, :], 1e-37, None, ALU.max))
                link(nc.vector.reciprocal(ex[:, :, :], ex[:, :, :]))
                for s in range(SUPS):
                    t = slice(s * SUP, (s + 1) * SUP)
                    part = a3[:, t, 0:256].rearrange("p t (h d) -> p t h d", h=4)
                    link(nc.vector.tensor_tensor(part, part, ex[:, t, :].unsqueeze(3).to_broadcast([P, SUP, 4, 64]), ALU.mult))
                    dve.wait_ge(wh_in[s % 2], 16 * (s // 2 + 1))
                    nc.vector.tensor_tensor(a3[:, t, 0:256], a3[:, t, 0:256], wh[:, s % 2, :, :], ALU.add).then_inc(wh_used, 1)


def stage_ffn(nc, g, comb, w1, w2, wo, bn1, bn2):
    EPS = 0.001
    with stage(nc) as own:
        def sb(name, shape, dt=F32):
            return own.enter_context(nc.sbuf_tensor(name, shape, dt))

        def sem(name):
            return own.enter_context(semaphore(nc, name))
        NC_ = EXPERTS * 2
        ws = sb("ws_f", [P, 2, 3, 2, D])
        par_in = sb("par_in", [P, 2, 5, NC_])
        scale = sb("scale_f", [P, 2, NC_])
        shift = sb("shift_f", [P, 2, NC_])
        own_s = sb("own_scale", [P, 2, 2, 2, 2])
        h1 = sb("h1t", [P, 2, SW])
        h2 = sb("h2t", [P, 2, SW])
        ps_h = own.enter_context(nc.psum_tensor("ps_hf", [P, 4, 512], F32))
        ps_y = own.enter_context(nc.psum_tensor("ps_yf", [P, 4, 512], F32))
        w_in = [sem("wf_even_in"), sem("wf_odd_in")]
        p_in, root, ready, chain = sem("bn_in"), sem("bnf_root"), sem("bnf_ready"), sem("bnf_chain")
        h_made, h_ready, y_made, y_used, o_own = sem("hf_made"), sem("hf_ready"), sem("yf_made"), sem("yf_used"), sem("own_ready")
        with nc.Block() as block:
            @block.sync
            def _(sp):
                with nc.allow_non_contiguous_dma(reason="channel columns"):
                    for layer, arrays in enumerate((bn1, bn2)):
                        for k, a in enumerate(arrays):
                            sp.dma_start(par_in[:, layer, k, :], a.rearrange("e (f p) -> p (e f)", p=P)).then_inc(p_in, 16)
                views = [w.rearrange("e (c p) n -> (e c) p n", p=P) for w in (w1, w2, wo)]

                def load(pair, par):
                    for k in range(3):
                        for c in range(2):
                            sp.dma_start(ws[:, par, k, c, :], views[k][ds((pair * 2 + par) * 2 + c, 1), :, :].rearrange("o p n -> (o p) n"))\
                              .then_inc(w_in[par], 16)
                load(0, 0)
                load(0, 1)
                with sp.Fori(1, EXPERTS // 2) as pair:
                    for par in range(2):
                        sp.wait_ge(y_made, (pair * 2 + par - 1) * NT)
                        load(pair, par)

            @block.tensor
            def _(pe):
                def layer(q, l, par, rhs):
                    for f in range(2):
                        for hf in range(2):
                            j = f * 2 + hf
                            pe.wait_ge(h_ready, q * 8 + (l * 4 + j + 1))
                            for c in range(2):
                                last = nc.tensor.matmul(ps_h[:, j, 0:HW], ws[:, par, l, c, f * P:(f + 1) * P], rhs(c, hf),
                                                        start=(c == 0), stop=(c == 1))
                            last.then_inc(h_made, 1)

                def first_layer(q, par, s):
                    layer(q, 0, par, lambda c, hf: g.xt[:, c, ds(s * SW + hf * HW, HW)])

                def step(pair, par, s, ahead):
                    q = (pair * 2 + par) * SUPS + s
                    pe.wait_ge(h_ready, q * 8 + 8)
                    layer(q, 1, par, lambda c, hf: h1[:, c, hf * HW:(hf + 1) * HW])
                    ahead(q + 1)
                    pe.wait_ge(h_ready, q * 8 + 12)
                    for k in range(SUP):
                        pe.wait_ge(y_used, q * SUP + (k + 1))
                        for c in range(2):
                            last = nc.tensor.matmul(ps_y[:, k % 4, 0:D], h2[:, c, k * P:(k + 1) * P], ws[:, par, 2, c, :],
                                                    start=(c == 0), stop=(c == 1))
                        last.then_inc(y_made, 1)

                def expert(pair, par, final=False):
                    with pe.Fori(0, SUPS - 1) as s:
                        step(pair, par, s, lambda q: first_layer(q, par, s + 1))

                    def next_expert(q):
                        if not final:
                            pe.wait_ge(w_in[1 - par], pair * 96 + (96 if par == 0 else 192))
                            first_layer(q, 1 - par, 0)
                    step(pair, par, SUPS - 1, next_expert)
                    pe.nop(nofuse=True)
                pe.wait_ge(w_in[0], 96)
                first_layer(0, 0, 0)
                pe.nop(nofuse=True)
                with pe.Fori(0, EXPERTS // 2 - 1) as pair:
                    expert(pair, 0)
                    expert(pair, 1)
                expert(EXPERTS // 2 - 1, 0)
                expert(EXPERTS // 2 - 1, 1, final=True)

            @block.scalar
            def _(act):
                act.wait_ge(chain, 1)
                nc.scalar.activation(scale[:, :, :], scale[:, :, :], ACT.Sqrt).then_inc(root, 1)
                act.sem_inc(h_ready, 4)
                act.wait_ge(ready, 2)

                def step(pair, par, s, first):
                    q = (pair * 2 + par) * SUPS + s
                    for l, h in enumerate((h1, h2)):
                        if l == 1 and not first:
                            act.wait_ge(y_made, q * SUP)
                        for f in range(2):
                            for hf in range(2):
                                j = f * 2 + hf
                                act.wait_ge(h_made, q * 8 + (l * 4 + j + 1))
                                nc.scalar.activation(h[:, f, hf * HW:(hf + 1) * HW], ps_h[:, j, 0:HW], ACT.Relu,
                                                     bias=own_s[:, par, 1, l, f:f + 1], scale=own_s[:, par, 0, l, f:f + 1])\
                                  .then_inc(h_ready, 1)

                def own_columns(pair, par):
                    e = pair * 2 + par
                    nc.scalar.copy(own_s[:, par, 0, :, :], scale[:, :, ds(e * 2, 2)]).then_inc(o_own, 1)
                    nc.scalar.copy(own_s[:, par, 1, :, :], shift[:, :, ds(e * 2, 2)]).then_inc(o_own, 1)
                    act.wait_ge(o_own, e * 2 + 2)
                    act.nop(nofuse=True)
                own_columns(0, 0)
                step(0, 0, 0, True)
                with act.Fori(1, SUPS) as s:
                    step(0, 0, s, False)
                own_columns(0, 1)
                with act.Fori(0, SUPS) as s:
                    step(0, 1, s, False)
                with act.Fori(1, EXPERTS // 2) as pair:
                    for par in range(2):
                        own_columns(pair, par)
                        with act.Fori(0, SUPS) as s:
                            step(pair, par, s, False)

            @block.vector
            def _(dve):
                dve.wait_ge(p_in, 160)
                link = Chain(dve, chain)
                link(nc.vector.tensor_scalar(scale[:, :, :], par_in[:, :, 4, :], EPS, None, ALU.add))
                dve.wait_ge(root, 1)
                link(nc.vector.reciprocal(scale[:, :, :], scale[:, :, :]))
                link(nc.vector.tensor_tensor(scale[:, :, :], scale[:, :, :], par_in[:, :, 1, :], ALU.mult))
                dve.sem_inc(ready, 1)
                link(nc.vector.tensor_tensor(shift[:, :, :], par_in[:, :, 0, :], par_in[:, :, 3, :], ALU.subtract))
                link(nc.vector.tensor_tensor(shift[:, :, :], shift[:, :, :], scale[:, :, :], ALU.mult))
                nc.vector.tensor_tensor(shift[:, :, :], shift[:, :, :], par_in[:, :, 2, :], ALU.add).then_inc(ready, 1)
                dve.sem_inc(y_used, 3)

                def step(pair, par, s):
                    q = (pair * 2 + par) * SUPS + s
                    for k in range(SUP):
                        dve.wait_ge(y_made, q * SUP + (k + 1))
                        dve.wait_ge(y_used, q * SUP + (k + 2))
                        t = s * SUP + k
                        xr = g.x[:, ds(t, 1), :].rearrange("p t d -> p (t d)")
                        nc.vector.scalar_tensor_tensor(xr, ps_y[:, k % 4, 0:D], comb[:, ds(t * 8 + pair * 2 + par, 1)], xr,
                                                       ALU.mult, ALU.add).then_inc(y_used, 1)
                with dve.Fori(0, EXPERTS // 2) as pair:
                    for par in range(2):
                        with dve.Fori(0, SUPS) as s:
                            step(pair, par, s)


def build_all(nc, A, out):
    edge_list = nc.dram_tensor("edge_list", [TILES * P, 2], I32).ap()
    table0 = nc.dram_tensor("table0", [NPAD, 68], F32).ap()
    slots_in = nc.dram_tensor("slots_in", [SLOT_TILES * P, D], F32).ap()
    slots_out = nc.dram_tensor("slots_out", [SLOT_TILES * P, D], F32).ap()
    table1 = nc.dram_tensor("table1", [NPAD, AW], F32).ap()
    with ExitStack() as ctx:
        g = Space()
        stage_constants(nc, g, ctx)
        g.rows = ctx.enter_context(nc.sbuf_tensor("rows", [P, NTP * 8], F32))
        g.top = ctx.enter_context(nc.sbuf_tensor("top", [P, KT, 4], F32))
        g.x = ctx.enter_context(nc.sbuf_tensor("x_res", [P, NTP, D], F32))
        g.mean = ctx.enter_context(nc.sbuf_tensor("ln_mean", [P, NTP], F32))
        g.rstd = ctx.enter_context(nc.sbuf_tensor("ln_rstd", [P, NTP], F32))
        g.var = ctx.enter_context(nc.sbuf_tensor("ln_var", [P, NTP], F32))
        with stage(nc) as own:
            stage_places(nc, g, A["x"], A["src"], A["dst"], ctx, own, edge_list, slots_in, SCATTERS["places"])
            g.xt = own.enter_context(nc.sbuf_tensor("xt0", [P, 2, NPAD], F32))
            stage_ln_stats(nc, g, "_0", scatters=SCATTERS["stats"])
            stage_l0_gnn_table(nc, g, A["L0_gnn_W"], A["L0_gnn_W_t"], A["L0_gnn_b"], A["L0_gnn_a_src_t"], A["L0_gnn_a_dst_t"], table0)
            stage_l0_mix(nc, g, A["L0_mix_w_qkv_t"], A["L0_mix_bn_gamma"], A["L0_mix_bn_beta"], A["L0_mix_w_dw_mid"], A["L0_mix_w_pw_t"],
                         A["L0_mix_w_res_t"], A["L0_mix_b_res"])
            stage_list(nc, g, SCATTERS["ball"][1])
        with ExitStack() as own:
            acc = own.enter_context(nc.sbuf_tensor("acc0", [P, NTP * AW], F32))
            aggregate_passes(nc, g, "_0", table0, 68, True, acc, g.top)
            stage_add_messages(nc, g, acc, "_0")
        with ExitStack() as own:
            g.w1s = own.enter_context(nc.sbuf_tensor("w1s", [P, EXPERTS * 2, WIDE_E], F32))
            g.w2s = own.enter_context(nc.sbuf_tensor("w2s", [P, EXPERTS * 4, D], F32))
            g.b1s = own.enter_context(nc.sbuf_tensor("b1s", [P, EXPERTS, WIDE_E], F32))
            g.share = own.enter_context(nc.sbuf_tensor("share", [P, 2, NTP], F32))
            g.slot = own.enter_context(nc.sbuf_tensor("slot", [P, 2, NTP], U32))
            g.tile_expert = own.enter_context(nc.sbuf_tensor("tile_expert", [1, SLOT_TILES], I32))
            comb = own.enter_context(nc.sbuf_tensor("comb0", [P, NTP * 8], F32))
            stage_ln_stats(nc, g, "_1")

            def fill(own, wl, bias):
                load_wide(nc, own, "_1", [(wl[:, :, :], A["L0_ffn_Wg"].rearrange("(c p) n -> p c n", p=P))],
                          [A["L0_ffn_bg"], A["L0_ffn_bias"]], bias)
            stage_turn(nc, g, "_1", fill, 8, out=comb, keep_xt=False)
            stage_route(nc, g, comb)
            stage_send(nc, g, A["L0_ffn_W1"], A["L0_ffn_b1"], A["L0_ffn_W2"], slots_in)
            stage_experts(nc, g, slots_in, slots_out)
            stage_collect(nc, g, comb, A["L0_ffn_b2"], slots_out)
        with ExitStack() as own:
            g.xt = own.enter_context(nc.sbuf_tensor("xt2", [P, 2, NPAD], F32))
            hg = own.enter_context(nc.sbuf_tensor("hg", [P, NTP * 64], F32))
            rstd2 = own.enter_context(nc.sbuf_tensor("rstd2", [P, NTP], F32))
            stage_ln_stats(nc, g, "_2")
            stage_second_norm(nc, g, rstd2)
            stage_turn(nc, g, "_2", fill_l1(nc, A["L1_gnn_W"], A["L1_gnn_W_t"], A["L1_gnn_attn_fc"], A["L1_mix_ln_g"], A["L1_mix_ln_b"],
                                            A["L1_mix_Wg1"], A["L1_mix_bg1"]), 328, table=table1, gate=(hg, rstd2))
            stage_l1_mix(nc, g, hg, A["L1_mix_Wqkv"], A["L1_mix_Wq_t"], A["L1_mix_Wproj"], A["L1_mix_bproj"], A["L1_mix_Wg2"], A["L1_mix_bg2"])
        with ExitStack() as own:
            acc = own.enter_context(nc.sbuf_tensor("acc1", [P, NTP * AW], F32))

            def new_row(i):
                return acc[:, ds(i * AW, D)]
            aggregate_passes(nc, g, "_1", table1, AW, False, acc, g.top)
            stage_l1_messages(nc, g, acc, g.top, table1)
            stage_ln_stats(nc, g, "_3", source=new_row)
            stage_turn(nc, g, "_3", fill_folded(nc, A["L1_gnn_ln_gamma"], A["L1_gnn_ln_beta"], A["L1_gnn_ffn_w"], A["L1_gnn_ffn_b"]), D,
                       source=new_row, keep_xt=False)
        with ExitStack() as own:
            g.xt = own.enter_context(nc.sbuf_tensor("xt3", [P, 2, NPAD], F32))
            comb = own.enter_context(nc.sbuf_tensor("comb1", [P, NTP * 8], F32))
            stage_ln_stats(nc, g, "_4")

            def fill(own, wl, bias):
                load_wide(nc, own, "_4", [(wl[:, :, :], A["L1_ffn_Wr"].rearrange("(c p) n -> p c n", p=P))], [A["L1_ffn_br"]], bias)
            stage_turn(nc, g, "_4", fill, 8, out=comb)
            stage_softmax8(nc, g, comb)
            stage_expert_bias(nc, g, "_4", comb, A["L1_ffn_bo"])
            stage_ffn(nc, g, comb, A["L1_ffn_W1"], A["L1_ffn_W2"], A["L1_ffn_Wo"],
                      [A["L1_ffn_" + k] for k in ("b1", "g1", "be1", "m1", "v1")],
                      [A["L1_ffn_" + k] for k in ("b2", "g2", "be2", "m2", "v2")])
        saved = ctx.enter_context(semaphore(nc, "saved"))
        with nc.Block() as block:
            @block.sync
            def _(sp):
                sp.dma_start(out[0:(NT - 1) * P, :].rearrange("(t p) d -> p t d", p=P), g.x[:, 0:NT - 1, :]).then_inc(saved, 16)
                sp.dma_start(out[(NT - 1) * P:N, :], g.x[0:LAST, NT - 1, :]).then_inc(saved, 16)
                sp.wait_ge(saved, 32)


def kernel(**inputs):
    import numpy as _np
    import concourse.bacc as _bacc
    from concourse import mybir as _mybir
    from concourse.bass_utils import run_bass_kernel_spmd as _run

    laid = {name: a for name, a in inputs.items()
            if name not in ("L0_mix_w_qkv", "L0_mix_w_dw", "L0_mix_w_pw", "L0_mix_w_res", "L0_gnn_a_src", "L0_gnn_a_dst")}
    laid["L0_gnn_W_t"] = _np.asarray(inputs["L0_gnn_W"]).T
    laid["L0_gnn_a_src_t"] = _np.asarray(inputs["L0_gnn_a_src"]).T
    laid["L0_gnn_a_dst_t"] = _np.asarray(inputs["L0_gnn_a_dst"]).T
    laid["L0_mix_w_qkv_t"] = _np.asarray(inputs["L0_mix_w_qkv"])[:, :, 2].T
    laid["L0_mix_w_dw_mid"] = _np.asarray(inputs["L0_mix_w_dw"])[:, 0, 2]
    laid["L0_mix_w_pw_t"] = _np.asarray(inputs["L0_mix_w_pw"])[:, :, 0].T
    laid["L0_mix_w_res_t"] = _np.asarray(inputs["L0_mix_w_res"])[:, :, 0].T
    laid["L1_gnn_W_t"] = _np.asarray(inputs["L1_gnn_W"]).T
    laid["L1_mix_Wq_t"] = _np.asarray(inputs["L1_mix_Wqkv"])[:, :256].T
    nc = _bacc.Bacc("TRN2", target_bir_lowering=False, num_devices=1)
    arrays, dram = {}, {}
    for name, a in laid.items():
        a = _np.ascontiguousarray(a)
        arrays[f"in_{name}_dram"] = a
        dram[name] = nc.dram_tensor(f"in_{name}_dram", a.shape, _mybir.dt.from_np(a.dtype), kind="ExternalInput").ap()
    out = nc.dram_tensor("out_0_dram", (6250, 256), _mybir.dt.from_np(_np.dtype("float32")), kind="ExternalOutput").ap()
    build_all(nc, dram, out)
    r = _run(nc, [arrays], core_ids=[0])
    return r.results[0]["out_0_dram"]
```
